# Optimizing a Trainium2 kernel written in Bass

```python
import numpy as np
import jax
import jax.numpy as jnp

def _softmax(x, axis=-1):
    return jax.nn.softmax(x, axis=axis)

def _gelu(x):
    return jax.nn.gelu(x, approximate=True)

def _silu(x):
    return jax.nn.silu(x)

def _sigmoid(x):
    return jax.nn.sigmoid(x)

def _layernorm(x, axis=-1, eps=1e-05):
    m = jnp.mean(x, axis=axis, keepdims=True)
    v = jnp.var(x, axis=axis, keepdims=True)
    return (x - m) / jnp.sqrt(v + eps)

def _scatter_add(tgt, idx, src, axis=0):
    return tgt.at[idx].add(src)

def _segment_sum(src, seg, n):
    return jax.ops.segment_sum(src, seg, n)
kernel_name = 'mk_seq_preln_d2_jaxref_r4_697204'

def setup_inputs(seed: int=0):
    np.random.seed(seed)
    _w = jnp.asarray

    def _L0_attn_setup():
        import jax, jax.numpy as jnp
        import numpy as np
        import math
        B, T, C = (2, 512, 512)
        N_HEAD = 16
        N_KV = 4
        GROUP = N_HEAD // N_KV
        HS = C // N_HEAD
        WINDOW = 256
        SINK = 4

        def _sliding_window_sink_mask(t):
            i = jnp.arange(t)[:, None]
            j = jnp.arange(t)[None, :]
            causal = j <= i
            band = j >= i - (WINDOW - 1)
            mask = causal & band
            mask = mask | (j < SINK)
            mask = mask & ((i >= SINK) | causal)
            return mask
        key = jax.random.key(seed)
        ks = jax.random.split(key, 5)
        s = 1.0 / math.sqrt(C)
        return {'x': jax.random.normal(ks[0], (B, T, C), dtype=jnp.float32), 'Wq': jax.random.normal(ks[1], (C, C), dtype=jnp.float32) * s, 'Wk': jax.random.normal(ks[2], (N_KV * HS, C), dtype=jnp.float32) * s, 'Wv': jax.random.normal(ks[3], (N_KV * HS, C), dtype=jnp.float32) * s, 'Wo': jax.random.normal(ks[4], (C, C), dtype=jnp.float32) * s}
    _L0_attn_in = _L0_attn_setup()

    def _L0_ffn_setup():
        import jax, jax.numpy as jnp
        import numpy as np
        EPS = 1e-06
        Q_B = 128.0

        def layer_norm(x):
            mean = jnp.mean(x, axis=-1, keepdims=True)
            var = jnp.var(x, axis=-1, keepdims=True)
            return (x - mean) / jnp.sqrt(var + EPS)

        def absmax_quant(x):
            gamma = jnp.max(jnp.abs(x), axis=-1, keepdims=True)
            x_hat = jnp.clip(x * Q_B / gamma, -Q_B + EPS, Q_B - EPS)
            return x_hat * gamma / Q_B

        def ternarize_weights(w):
            gamma = jnp.mean(jnp.abs(w))
            return jnp.sign(jnp.round(w / (gamma + EPS))) * gamma

        def bitlinear(x, w):
            xn = layer_norm(x)
            x_hat = xn + jax.lax.stop_gradient(absmax_quant(xn) - xn)
            w_hat = w + jax.lax.stop_gradient(ternarize_weights(w) - w)
            return jnp.einsum('bsd,od->bso', x_hat, w_hat)
        key = jax.random.key(seed)
        k1, k2, k3 = jax.random.split(key, 3)
        B, S, D = (4, 512, 512)
        x = jax.random.normal(k1, (B, S, D), dtype=jnp.float32)
        w_fc = jax.random.normal(k2, (4 * D, D), dtype=jnp.float32) / np.sqrt(D)
        w_proj = jax.random.normal(k3, (D, 4 * D), dtype=jnp.float32) / np.sqrt(4 * D)
        return {'x': x, 'w_fc': w_fc, 'w_proj': w_proj}
    _L0_ffn_in = _L0_ffn_setup()

    def _L1_attn_setup():
        import jax, jax.numpy as jnp
        import numpy as np
        H = 16
        D_NOPE = 128
        D_ROPE = 64
        D_QK = 192
        D_V = 128
        THETA = 10000.0
        EPS = 1e-06

        def rmsnorm(x, w):
            x32 = x.astype(jnp.float32)
            x32 = x32 * jax.lax.rsqrt(jnp.mean(x32 * x32, axis=-1, keepdims=True) + EPS)
            return (x32 * w).astype(x.dtype)

        def rope_cos_sin(seq_len, dim, dtype):
            inv_freq = 1.0 / THETA ** (jnp.arange(0, dim, 2, dtype=jnp.float32) / dim)
            t = jnp.arange(seq_len, dtype=jnp.float32)
            freqs = jnp.outer(t, inv_freq)
            return (jnp.cos(freqs).astype(dtype), jnp.sin(freqs).astype(dtype))

        def apply_rope(x, cos, sin):
            d2 = x.shape[-1] // 2
            x1, x2 = (x[..., :d2], x[..., d2:])
            c = cos[None, :, None, :]
            s = sin[None, :, None, :]
            return jnp.concatenate([x1 * c - x2 * s, x2 * c + x1 * s], axis=-1)
        key = jax.random.key(seed)
        ks = jax.random.split(key, 8)
        B, T, D = (2, 512, 512)
        q_lora, kv_lora = (384, 128)

        def w(k, fan_in, fan_out):
            return jax.random.normal(k, (fan_in, fan_out), dtype=jnp.float32) * (1.0 / np.sqrt(fan_in))
        return {'hidden_states': jax.random.normal(ks[0], (B, T, D), dtype=jnp.float32), 'Wq_a': w(ks[1], D, q_lora), 'q_norm_w': jnp.ones((q_lora,), dtype=jnp.float32), 'Wq_b': w(ks[2], q_lora, H * D_QK), 'Wk_rope': w(ks[3], D, D_ROPE), 'Wkv_a': w(ks[4], D, kv_lora), 'kv_norm_w': jnp.ones((kv_lora,), dtype=jnp.float32), 'Wkv_b': w(ks[5], kv_lora, H * (D_NOPE + D_V)), 'Wo': w(ks[6], H * D_V, D)}
    _L1_attn_in = _L1_attn_setup()

    def _L1_ffn_setup():
        import jax, jax.numpy as jnp
        import numpy as np
        NUM_ROUTED = 7
        TOP_K = 3
        D = 512
        H = 512
        B, S = (4, 512)

        def _expert_ffn(x, w1, wg, w2):
            return jax.nn.silu(x @ w1) * (x @ wg) @ w2
        key = jax.random.key(seed)
        ks = jax.random.split(key, 8)
        s = 0.02
        return {'x': jax.random.normal(ks[0], (B, S, D), jnp.float32), 'W1': jax.random.normal(ks[1], (NUM_ROUTED, D, H), jnp.float32) * s, 'Wg': jax.random.normal(ks[2], (NUM_ROUTED, D, H), jnp.float32) * s, 'W2': jax.random.normal(ks[3], (NUM_ROUTED, H, D), jnp.float32) * s, 'Ws1': jax.random.normal(ks[4], (D, H), jnp.float32) * s, 'Wsg': jax.random.normal(ks[5], (D, H), jnp.float32) * s, 'Ws2': jax.random.normal(ks[6], (H, D), jnp.float32) * s, 'gate_w': jax.random.normal(ks[7], (D, NUM_ROUTED), jnp.float32) * s, 'gate_b': jnp.zeros((NUM_ROUTED,), jnp.float32), 'biases': jnp.zeros((NUM_ROUTED,), jnp.float32)}
    _L1_ffn_in = _L1_ffn_setup()
    _d = {'L0_attn_x': _L0_attn_in['x'], 'L0_attn_Wq': _L0_attn_in['Wq'], 'L0_attn_Wk': _L0_attn_in['Wk'], 'L0_attn_Wv': _L0_attn_in['Wv'], 'L0_attn_Wo': _L0_attn_in['Wo'], 'L0_ffn_w_fc': _L0_ffn_in['w_fc'], 'L0_ffn_w_proj': _L0_ffn_in['w_proj'], 'L1_attn_Wq_a': _L1_attn_in['Wq_a'], 'L1_attn_q_norm_w': _L1_attn_in['q_norm_w'], 'L1_attn_Wq_b': _L1_attn_in['Wq_b'], 'L1_attn_Wk_rope': _L1_attn_in['Wk_rope'], 'L1_attn_Wkv_a': _L1_attn_in['Wkv_a'], 'L1_attn_kv_norm_w': _L1_attn_in['kv_norm_w'], 'L1_attn_Wkv_b': _L1_attn_in['Wkv_b'], 'L1_attn_Wo': _L1_attn_in['Wo'], 'L1_ffn_W1': _L1_ffn_in['W1'], 'L1_ffn_Wg': _L1_ffn_in['Wg'], 'L1_ffn_W2': _L1_ffn_in['W2'], 'L1_ffn_Ws1': _L1_ffn_in['Ws1'], 'L1_ffn_Wsg': _L1_ffn_in['Wsg'], 'L1_ffn_Ws2': _L1_ffn_in['Ws2'], 'L1_ffn_gate_w': _L1_ffn_in['gate_w'], 'L1_ffn_gate_b': _L1_ffn_in['gate_b'], 'L1_ffn_biases': _L1_ffn_in['biases']}
    _x0 = _d['L0_attn_x']
    _d['L0_attn_x'] = jax.random.normal(jax.random.fold_in(jax.random.key(seed), 1), (4, 512, 512), dtype=_x0.dtype)
    del _x0
    return _d

def reference(L0_attn_x, L0_attn_Wq, L0_attn_Wk, L0_attn_Wv, L0_attn_Wo, L0_ffn_w_fc, L0_ffn_w_proj, L1_attn_Wq_a, L1_attn_q_norm_w, L1_attn_Wq_b, L1_attn_Wk_rope, L1_attn_Wkv_a, L1_attn_kv_norm_w, L1_attn_Wkv_b, L1_attn_Wo, L1_ffn_W1, L1_ffn_Wg, L1_ffn_W2, L1_ffn_Ws1, L1_ffn_Wsg, L1_ffn_Ws2, L1_ffn_gate_w, L1_ffn_gate_b, L1_ffn_biases):

    def _L0_attn_ref(x, Wq, Wk, Wv, Wo):
        import jax, jax.numpy as jnp
        import numpy as np
        import math
        B, T, C = (2, 512, 512)
        N_HEAD = 16
        N_KV = 4
        GROUP = N_HEAD // N_KV
        HS = C // N_HEAD
        WINDOW = 256
        SINK = 4

        def _sliding_window_sink_mask(t):
            i = jnp.arange(t)[:, None]
            j = jnp.arange(t)[None, :]
            causal = j <= i
            band = j >= i - (WINDOW - 1)
            mask = causal & band
            mask = mask | (j < SINK)
            mask = mask & ((i >= SINK) | causal)
            return mask
        b, t, c = x.shape
        q = (x @ Wq.T).reshape(b, t, N_HEAD, HS).transpose(0, 2, 1, 3)
        q = q.reshape(b, N_KV, GROUP, t, HS)
        k = (x @ Wk.T).reshape(b, t, N_KV, HS).transpose(0, 2, 1, 3)
        v = (x @ Wv.T).reshape(b, t, N_KV, HS).transpose(0, 2, 1, 3)
        scale = 1.0 / math.sqrt(HS)
        att = jnp.einsum('bkgqd,bkjd->bkgqj', q, k) * scale
        mask = _sliding_window_sink_mask(t)
        att = jnp.where(mask[None, None, None, :, :], att, -jnp.inf)
        att = jax.nn.softmax(att, axis=-1)
        y = jnp.einsum('bkgqj,bkjd->bkgqd', att, v)
        y = y.reshape(b, N_HEAD, t, HS).transpose(0, 2, 1, 3).reshape(b, t, c)
        return y @ Wo.T

    def _L0_ffn_ref(x, w_fc, w_proj):
        import jax, jax.numpy as jnp
        import numpy as np
        EPS = 1e-06
        Q_B = 128.0

        def layer_norm(x):
            mean = jnp.mean(x, axis=-1, keepdims=True)
            var = jnp.var(x, axis=-1, keepdims=True)
            return (x - mean) / jnp.sqrt(var + EPS)

        def absmax_quant(x):
            gamma = jnp.max(jnp.abs(x), axis=-1, keepdims=True)
            x_hat = jnp.clip(x * Q_B / gamma, -Q_B + EPS, Q_B - EPS)
            return x_hat * gamma / Q_B

        def ternarize_weights(w):
            gamma = jnp.mean(jnp.abs(w))
            return jnp.sign(jnp.round(w / (gamma + EPS))) * gamma

        def bitlinear(x, w):
            xn = layer_norm(x)
            x_hat = xn + jax.lax.stop_gradient(absmax_quant(xn) - xn)
            w_hat = w + jax.lax.stop_gradient(ternarize_weights(w) - w)
            return jnp.einsum('bsd,od->bso', x_hat, w_hat)
        h = bitlinear(x, w_fc)
        h = jax.nn.gelu(h, approximate=False)
        return bitlinear(h, w_proj)

    def _L1_attn_ref(hidden_states, Wq_a, q_norm_w, Wq_b, Wk_rope, Wkv_a, kv_norm_w, Wkv_b, Wo):
        import jax, jax.numpy as jnp
        import numpy as np
        H = 16
        D_NOPE = 128
        D_ROPE = 64
        D_QK = 192
        D_V = 128
        THETA = 10000.0
        EPS = 1e-06

        def rmsnorm(x, w):
            x32 = x.astype(jnp.float32)
            x32 = x32 * jax.lax.rsqrt(jnp.mean(x32 * x32, axis=-1, keepdims=True) + EPS)
            return (x32 * w).astype(x.dtype)

        def rope_cos_sin(seq_len, dim, dtype):
            inv_freq = 1.0 / THETA ** (jnp.arange(0, dim, 2, dtype=jnp.float32) / dim)
            t = jnp.arange(seq_len, dtype=jnp.float32)
            freqs = jnp.outer(t, inv_freq)
            return (jnp.cos(freqs).astype(dtype), jnp.sin(freqs).astype(dtype))

        def apply_rope(x, cos, sin):
            d2 = x.shape[-1] // 2
            x1, x2 = (x[..., :d2], x[..., d2:])
            c = cos[None, :, None, :]
            s = sin[None, :, None, :]
            return jnp.concatenate([x1 * c - x2 * s, x2 * c + x1 * s], axis=-1)
        B, T, D = hidden_states.shape
        q = rmsnorm(hidden_states @ Wq_a, q_norm_w) @ Wq_b
        q = q.reshape(B, T, H, D_QK)
        q_pass, q_rot = (q[..., :D_NOPE], q[..., D_NOPE:])
        kv = rmsnorm(hidden_states @ Wkv_a, kv_norm_w) @ Wkv_b
        kv = kv.reshape(B, T, H, D_NOPE + D_V)
        k_pass, v = (kv[..., :D_NOPE], kv[..., D_NOPE:])
        k_rot = (hidden_states @ Wk_rope)[:, :, None, :]
        cos, sin = rope_cos_sin(T, D_ROPE, hidden_states.dtype)
        q_rot = apply_rope(q_rot, cos, sin)
        k_rot = apply_rope(k_rot, cos, sin)
        k_rot = jnp.broadcast_to(k_rot, (B, T, H, D_ROPE))
        qf = jnp.concatenate([q_pass, q_rot], axis=-1)
        kf = jnp.concatenate([k_pass, k_rot], axis=-1)
        scale = 1.0 / np.sqrt(D_QK)
        scores = jnp.einsum('bqhd,bkhd->bhqk', qf, kf) * scale
        mask = jnp.tril(jnp.ones((T, T), dtype=bool))
        scores = jnp.where(mask[None, None], scores, jnp.finfo(scores.dtype).min)
        p = jax.nn.softmax(scores, axis=-1)
        o = jnp.einsum('bhqk,bkhd->bqhd', p, v)
        o = o.reshape(B, T, H * D_V) @ Wo
        return o

    def _L1_ffn_ref(x, W1, Wg, W2, Ws1, Wsg, Ws2, gate_w, gate_b, biases):
        import jax, jax.numpy as jnp
        import numpy as np
        NUM_ROUTED = 7
        TOP_K = 3
        D = 512
        H = 512
        B, S = (4, 512)

        def _expert_ffn(x, w1, wg, w2):
            return jax.nn.silu(x @ w1) * (x @ wg) @ w2
        output = _expert_ffn(x, Ws1, Wsg, Ws2)
        gate_logits = x @ gate_w + gate_b
        gate_probas = jax.nn.softmax(gate_logits, axis=-1)
        biased_probas = gate_probas + biases
        _, topk_idxs = jax.lax.top_k(biased_probas, TOP_K)
        topk_probas = jnp.take_along_axis(gate_probas, topk_idxs, axis=-1)
        topk_probas = topk_probas / jnp.sum(topk_probas, axis=-1, keepdims=True)
        for e in range(NUM_ROUTED):
            w_e = jnp.sum(topk_probas * (topk_idxs == e), axis=-1)
            output = output + _expert_ffn(x, W1[e], Wg[e], W2[e]) * w_e[..., None]
        return output
    x = L0_attn_x
    x = x + _L0_attn_ref(_layernorm(x, axis=-1), L0_attn_Wq, L0_attn_Wk, L0_attn_Wv, L0_attn_Wo)
    x = x + _L0_ffn_ref(_layernorm(x, axis=-1), L0_ffn_w_fc, L0_ffn_w_proj)
    x = x + _L1_attn_ref(_layernorm(x, axis=-1), L1_attn_Wq_a, L1_attn_q_norm_w, L1_attn_Wq_b, L1_attn_Wk_rope, L1_attn_Wkv_a, L1_attn_kv_norm_w, L1_attn_Wkv_b, L1_attn_Wo)
    x = x + _L1_ffn_ref(_layernorm(x, axis=-1), L1_ffn_W1, L1_ffn_Wg, L1_ffn_W2, L1_ffn_Ws1, L1_ffn_Wsg, L1_ffn_Ws2, L1_ffn_gate_w, L1_ffn_gate_b, L1_ffn_biases)
    return x

_drawn_inputs = setup_inputs


def setup_inputs(seed=0):
    import zlib

    import numpy as np

    out = dict(_drawn_inputs(seed))
    spreads = {'L1_attn_q_norm_w': (1.0, 0.561),
     'L1_attn_kv_norm_w': (1.0, 0.2),
     'L1_ffn_gate_b': (0.0, 0.8),
     'L1_ffn_biases': (0.0, 0.472)}
    factors = {'L1_ffn_gate_w': 3.431}
    for name, (base, spread) in spreads.items():
        noise = np.random.default_rng([zlib.crc32(name.encode()), seed]).standard_normal(out[name].shape)
        drawn = base * np.exp(spread * noise) if base else spread * noise
        out[name] = jnp.asarray(drawn.astype(out[name].dtype))
    for name, factor in factors.items():
        out[name] = (out[name] * factor).astype(out[name].dtype)
    return out
```

```python
from contextlib import ExitStack, contextmanager

import concourse.bass as bass
import numpy as np
from concourse import mybir

F32 = mybir.dt.float32
F32R = mybir.dt.float32r
ALU = mybir.AluOpType
ACT = mybir.ActivationFunctionType
AX = mybir.AxisListType

P = 128
D = 512
KD = D // P
BATCH, SEQ = 4, 512
TILES = BATCH * SEQ // P
TPB = SEQ // P
MASKED = -1.0e30

LN_EPS = 1e-5


class Tally:

    def __init__(self, sem, base=0):
        self.sem, self.base, self.n = sem, base, 0

    def inc(self, instruction, by=1):
        instruction.then_inc(self.sem, by)
        self.n += by

    def wait(self, engine, n=None):
        engine.wait_ge(self.sem, self.base + (self.n if n is None else n))


def wait_apart(engine, sem, value):
    engine.wait_ge(sem, value)
    engine.nop(nofuse=True)


@contextmanager
def semaphores(nc):
    handles = []

    def make(name):
        handles.append(nc.alloc_semaphore(name=name))
        return handles[-1]

    yield make
    with nc.Block() as block:

        @block.sync
        def _(sp):
            for handle in handles:
                sp.sem_clear(handle)
    for handle in handles:
        nc.release_semaphore(handle)



HEADS, GROUPS, HS = 16, 4, 32
PER_GROUP = HEADS // GROUPS
SCORE_OFFSET = [0, 128, 384, 768]
SCORE_COLS = 1280
SCORE_PLACE = [(0, 0), (1, 0), (0, 128), (2, 0)]
PT_PLACE = [(3, 0), (4, 0), (5, 0), (4, 384)]
PT_OFFSET = [0, 512, 1024, 896]


def window_attention(nc, x_res, ident, wq, wk, wv, wo, mask_dram, clear=None):
    with ExitStack() as ctx:
        def sb(name, shape, dt=F32):
            return ctx.enter_context(nc.sbuf_tensor(name, shape, dt))

        sem = ctx.enter_context(semaphores(nc))

        psum = ctx.enter_context(nc.psum_tensor("a_psum", [P, 8, 512], F32))
        w_hi = sb("a_w_hi", [P, KD, 1280], F32R)
        w_lo = sb("a_w_lo", [P, KD, 1280], F32R)
        WQ, WK, WV, WO = 0, 512, 640, 768
        mask = sb("a_mask", [P, SCORE_COLS])
        stats = sb("a_stats", [P, TPB, 6])
        meanvar = sb("a_meanvar", [P, TPB, 2])
        sdev = sb("a_sdev", [P, TPB])
        rstd = sb("a_rstd", [P, TPB])
        xt_hi = sb("a_xt_hi", [P, KD, SEQ], F32R)
        xt_lo = sb("a_xt_lo", [P, KD, SEQ], F32R)
        qk_hi = sb("a_qk_hi", [P, 5, SEQ], F32R)
        qk_lo = sb("a_qk_lo", [P, 5, SEQ], F32R)
        q_stack = sb("a_q_stack", [3 * HS, GROUPS, PER_GROUP, SEQ], F32R)
        k_stack = sb("a_k_stack", [3 * HS, GROUPS, SEQ], F32R)
        v_pad = sb("a_v_pad", [P, TPB, GROUPS, 3 * HS + HS + 3 * HS])
        masked = sb("a_masked", [P, 2, SCORE_COLS])
        probs = sb("a_probs", [P, 2, SCORE_COLS])
        probs_t = sb("a_probs_t", [P, 2, SCORE_COLS])
        w_raw = masked
        xn = probs_t[:, :, :].rearrange("p a n -> p (a n)")[:, 0:TPB * D].rearrange("p (t n) -> p t n", t=TPB)
        low = sb("a_low", [P, 2, TPB])
        rowsum = sb("a_rowsum", [P, 2, TPB])
        rinv = sb("a_rinv", [P, 2, TPB])
        y_hi, y_lo = xt_hi, xt_lo

        loaded = [sem(f"a_loaded{k}") for k in range(KD)]
        mask_loaded = sem("a_mask_loaded")
        weights_hi = sem("a_weights_hi")
        weights_lo = sem("a_weights_lo")
        v_zeroed = sem("a_v_zeroed")
        dve_step = sem("a_dve_step")
        var_ready = sem("a_var_ready")
        sdev_ready = sem("a_sdev_ready")
        xn_ready = sem("a_xn_ready")
        xn_turned = sem("a_xn_turned")
        xt_hi_ready = sem("a_xt_hi_ready")
        xt_lo_ready = sem("a_xt_lo_ready")
        projected = sem("a_projected")
        qk_hi_ready = sem("a_qk_hi_ready")
        qk_lo_ready = sem("a_qk_lo_ready")
        v_ready = sem("a_v_ready")
        stacked = [sem(f"a_stacked{g}") for g in range(GROUPS)]
        scores_ready = sem("a_scores_ready")
        masked_ready = sem("a_masked_ready")
        exp_ready = sem("a_exp_ready")
        probs_ready = sem("a_probs_ready")
        turned = sem("a_turned")
        pt_act = sem("a_pt_act")
        pt_dve = sem("a_pt_dve")
        mixed = sem("a_mixed")
        y_hi_ready = sem("a_y_hi_ready")
        y_lo_ready = sem("a_y_lo_ready")
        out_ready = sem("a_out_ready")

        STACK_DMAS = 6
        GROUP_ORDER = range(GROUPS)
        block = ctx.enter_context(nc.Block())

        @block.sync
        def _(sp):
            for k in range(KD):
                if k >= 2:
                    sp.wait_ge(weights_lo, k - 1)
                rows = slice(P * k, P * k + P)
                for w, lo, hi in ((wq, WQ, WK), (wk, WK, WV), (wv, WV, WO), (wo, WO, WO + D)):
                    sp.dma_start(w_raw[:, k % 2, lo:hi], w[rows, :]).then_inc(loaded[k], 16)
            sp.dma_start(mask[:], mask_dram).then_inc(mask_loaded, 16)
            with sp.Fori(0, BATCH) as b:
                sp.wait_ge(qk_hi_ready, b * 5 + 5)
                sp.wait_ge(qk_lo_ready, b * 5 + 5)
                for g in GROUP_ORDER:
                    rows = slice(HS * g, HS * g + HS)
                    for c, part in enumerate((qk_hi, qk_lo, qk_hi)):
                        sp.dma_start(k_stack[HS * c:HS * c + HS, g, :].bitcast(F32), part[rows, 4, :].bitcast(F32)).then_inc(stacked[g], 16)
                    for c, part in enumerate((qk_hi, qk_hi, qk_lo)):
                        sp.dma_start(q_stack[HS * c:HS * c + HS, g, :, :].bitcast(F32), part[rows, 0:4, :].bitcast(F32)).then_inc(stacked[g], 16)
                if clear:
                    clear(sp, b)
            if clear:
                clear(sp, BATCH)

        @block.gpsimd
        def _(pool):
            pool.memset(v_pad[:], 0.0).then_inc(v_zeroed, 1)

        @block.scalar
        def _(act):
            for k in range(KD):
                act.wait_ge(loaded[k], 16 * 4)
                act.activation(w_hi[:, k, :], w_raw[:, k % 2, :], ACT.Copy).then_inc(weights_hi, 1)
            act.wait_ge(v_zeroed, 1)
            with act.Fori(0, BATCH) as b:
                act.wait_ge(var_ready, b + 1)
                act.activation(sdev[:], meanvar[:, :, 1], ACT.Sqrt).then_inc(sdev_ready, 1)
                for t in range(TPB):
                    act.wait_ge(xn_turned, b * TPB + t + 1)
                    act.activation(xt_hi[:, :, P * t:P * t + P], psum[:, t, :].rearrange("p (k n) -> p k n", k=KD),
                                   ACT.Copy).then_inc(xt_hi_ready, 1)
                for n, (slot, bank) in enumerate(((4, 4), (0, 5), (1, 6), (2, 7), (3, 0))):
                    act.wait_ge(projected, b * 6 + n + 1)
                    act.activation(qk_hi[:, slot, :], psum[:, bank, :], ACT.Copy).then_inc(qk_hi_ready, 1)
                act.wait_ge(projected, b * 6 + 6)
                for t in range(TPB):
                    act.activation(v_pad[:, t, :, 3 * HS:4 * HS],
                                   psum[:, 1, P * t:P * t + P].rearrange("p (g d) -> p g d", g=GROUPS),
                                   ACT.Copy).then_inc(v_ready, 1)

                def keep_pt(h):
                    act.wait_ge(turned, b * HEADS + h + 1)
                    if h >= 2:
                        act.wait_ge(mixed, b * HEADS + h - 1)
                    act.activation(probs_t[:, h % 2, 0:512], psum[:, 3, :], ACT.Copy).then_inc(pt_act, 1)
                    act.activation(probs_t[:, h % 2, 1024:1280], psum[:, 5, 0:256], ACT.Copy).then_inc(pt_act, 1)

                def keep_y(g):
                    act.wait_ge(mixed, b * HEADS + PER_GROUP * (g + 1))
                    act.activation(y_hi[:, g, :], psum[:, 6 + g % 2, :], ACT.Copy).then_inc(y_hi_ready, 1)

                for s in range(HEADS + 4):
                    if 0 <= s - 2 < HEADS:
                        keep_pt(s - 2)
                    if s < HEADS:
                        if s >= 2:
                            act.wait_ge(turned, b * HEADS + s - 1)
                        for i in range(TPB):
                            act.wait_ge(masked_ready, (b * HEADS + s) * TPB + i + 1)
                            o, n = SCORE_OFFSET[i], P * (i + 1)
                            act.activation(probs[:, s % 2, o:o + n], masked[:, s % 2, o:o + n], ACT.Exp,
                                           bias=low[:, s % 2, i:i + 1], scale=-1.0,
                                           accum_out=rowsum[:, s % 2, i:i + 1]).then_inc(exp_ready, 1)
                    if s >= PER_GROUP + 3 and (s - 3) % PER_GROUP == 0:
                        keep_y((s - 3) // PER_GROUP - 1)

        @block.vector
        def _(dve):
            for k in range(KD):
                dve.wait_ge(weights_hi, k + 1)
                dve.tensor_tensor(w_lo[:, k, :], w_raw[:, k % 2, :], w_hi[:, k, :].bitcast(F32), ALU.subtract)\
                   .then_inc(weights_lo, 1)
            dve.wait_ge(mask_loaded, 16)
            STEPS = 3 * TPB + 1 + HEADS
            with dve.Fori(0, BATCH) as b:
                step = Tally(dve_step, b * STEPS)
                for t in range(TPB):
                    step.inc(dve.bn_stats(stats[:, t, :], x_res[:, bass.ds(b * TPB + t, 1), :]
                                          .rearrange("p a n -> p (a n)")))
                wait_apart(dve, step.sem, step.base + step.n)
                for t in range(TPB):
                    step.inc(dve.bn_aggr(meanvar[:, t, :], stats[:, t, :]))
                step.wait(dve)
                dve.tensor_scalar(meanvar[:, :, 1], meanvar[:, :, 1], LN_EPS, None, ALU.add).then_inc(var_ready, 1)
                dve.wait_ge(sdev_ready, b + 1)
                step.inc(dve.reciprocal(rstd[:], sdev[:]))
                step.wait(dve)
                for t in range(TPB):
                    dve.tensor_scalar(xn[:, t, :], x_res[:, bass.ds(b * TPB + t, 1), :].rearrange("p a n -> p (a n)"),
                                      meanvar[:, t, 0:1], rstd[:, t:t + 1], ALU.subtract, ALU.mult)\
                       .then_inc(xn_ready, 1)
                for t in range(TPB):
                    dve.wait_ge(xt_hi_ready, b * TPB + t + 1)
                    cols = slice(P * t, P * t + P)
                    dve.tensor_tensor(xt_lo[:, :, cols], psum[:, t, :].rearrange("p (k n) -> p k n", k=KD),
                                      xt_hi[:, :, cols].bitcast(F32), ALU.subtract).then_inc(xt_lo_ready, 1)
                for n, (slot, bank) in enumerate(((4, 4), (0, 5), (1, 6), (2, 7), (3, 0))):
                    dve.wait_ge(qk_hi_ready, b * 5 + n + 1)
                    dve.tensor_tensor(qk_lo[:, slot, :], psum[:, bank, :], qk_hi[:, slot, :].bitcast(F32),
                                      ALU.subtract).then_inc(qk_lo_ready, 1)

                def mask_scores(h):
                    if h >= 2:
                        dve.wait_ge(exp_ready, (b * HEADS + h - 1) * TPB)
                    for i in range(TPB):
                        wait_apart(dve, scores_ready, (b * HEADS + h) * TPB + (3, 2, 3, 4)[i])
                        bank, c = SCORE_PLACE[i]
                        o, n = SCORE_OFFSET[i], P * (i + 1)
                        dve.tensor_tensor_reduce(masked[:, h % 2, o:o + n], psum[:, bank, c:c + n], mask[:, o:o + n],
                                                 -(HS ** -0.5), -MASKED, ALU.add, ALU.min,
                                                 low[:, h % 2, i:i + 1]).then_inc(masked_ready, 1)

                def normalise(h):
                    dve.wait_ge(exp_ready, (b * HEADS + h + 1) * TPB)
                    step.inc(dve.reciprocal(rinv[:, h % 2, :], rowsum[:, h % 2, :]))
                    step.wait(dve)
                    for i in range(TPB):
                        o, n = SCORE_OFFSET[i], P * (i + 1)
                        dve.tensor_scalar(probs[:, h % 2, o:o + n], probs[:, h % 2, o:o + n],
                                          rinv[:, h % 2, i:i + 1], None, ALU.mult).then_inc(probs_ready, 1)

                def keep_pt(h):
                    dve.wait_ge(turned, b * HEADS + h + 1)
                    if h >= 2:
                        dve.wait_ge(mixed, b * HEADS + h - 1)
                    dve.tensor_copy(probs_t[:, h % 2, 512:1024], psum[:, 4, :]).then_inc(pt_dve, 1)

                def keep_y(g):
                    dve.wait_ge(y_hi_ready, b * GROUPS + g + 1)
                    dve.tensor_tensor(y_lo[:, g, :], psum[:, 6 + g % 2, :], y_hi[:, g, :].bitcast(F32),
                                      ALU.subtract).then_inc(y_lo_ready, 1)

                for s in range(HEADS + 4):
                    if s < HEADS:
                        mask_scores(s)
                    if 0 <= s - 1 < HEADS:
                        normalise(s - 1)
                    if 0 <= s - 2 < HEADS:
                        keep_pt(s - 2)
                    if s >= PER_GROUP + 3 and (s - 3) % PER_GROUP == 0:
                        keep_y((s - 3) // PER_GROUP - 1)
                for t in range(TPB):
                    dve.wait_ge(out_ready, b * TPB + t + 1)
                    tile = x_res[:, bass.ds(b * TPB + t, 1), :].rearrange("p a n -> p (a n)")
                    step.inc(dve.tensor_tensor(tile, psum[:, t, :], tile, ALU.add))
                step.wait(dve)
                assert step.n == STEPS

        @block.tensor
        def _(pe):
            pe.wait_ge(weights_lo, KD)

            def product(out, lhs_hi, lhs_lo, rhs_hi, rhs_lo, chunks):
                n = 3 * len(chunks)
                for j in range(n):
                    k, (a, c) = chunks[j // 3], ((lhs_hi, rhs_hi), (lhs_hi, rhs_lo), (lhs_lo, rhs_hi))[j % 3]
                    ins = pe.matmul(out, a(k), c(k), start=j == 0, stop=j == n - 1)
                return ins

            def w(part, lo, n):
                return lambda k: part[:, k, lo:lo + n]

            def xt(part, lo=0, n=SEQ):
                return lambda k: part[:, k, lo:lo + n]

            with pe.Fori(0, BATCH) as b:
                for t in range(TPB):
                    pe.wait_ge(xn_ready, b * TPB + t + 1)
                    for k in range(KD):
                        ins = pe.transpose(psum[:, t, P * k:P * k + P], xn[:, t, P * k:P * k + P], ident[:])
                    ins.then_inc(xn_turned, 1)
                pe.wait_ge(xt_lo_ready, b * TPB + TPB)
                product(psum[:, 4, :], w(w_hi, WK, P), w(w_lo, WK, P), xt(xt_hi), xt(xt_lo), range(KD))\
                    .then_inc(projected, 1)
                for s, bank in enumerate((5, 6, 7, 0)):
                    product(psum[:, bank, :], w(w_hi, WQ + P * s, P), w(w_lo, WQ + P * s, P), xt(xt_hi), xt(xt_lo),
                            range(KD)).then_inc(projected, 1)
                for t in range(TPB):
                    ins = product(psum[:, 1, P * t:P * t + P], xt(xt_hi, P * t, P), xt(xt_lo, P * t, P),
                                  w(w_hi, WV, P), w(w_lo, WV, P), range(KD))
                ins.then_inc(projected, 1)

                def scores(h):
                    g, j = divmod(h, PER_GROUP)
                    if j == 0:
                        pe.wait_ge(stacked[g], (b + 1) * STACK_DMAS * 16)
                    if h == 0:
                        pe.wait_ge(v_ready, (b + 1) * TPB)
                    else:
                        pe.wait_ge(masked_ready, (b * HEADS + h) * TPB)
                    for i in range(TPB):
                        bank, c = SCORE_PLACE[i]
                        pe.matmul(psum[:, bank, c:c + P * (i + 1)], q_stack[:, g, j, P * i:P * i + P],
                                  k_stack[:, g, 0:P * (i + 1)], start=True, stop=True).then_inc(scores_ready, 1)

                def turn(h):
                    pe.wait_ge(probs_ready, (b * HEADS + h + 1) * TPB)
                    if h >= 1:
                        pe.wait_ge(pt_act, (b * HEADS + h) * 2)
                        pe.wait_ge(pt_dve, b * HEADS + h)
                    for j in range(TPB):
                        bank, c = PT_PLACE[j]
                        for i in range(j, TPB):
                            o = SCORE_OFFSET[i] + P * j
                            ins = pe.transpose(psum[:, bank, c + P * (i - j):c + P * (i - j + 1)],
                                               probs[:, h % 2, o:o + P], ident[:])
                    ins.then_inc(turned, 1)

                def mix(h):
                    g, j = divmod(h, PER_GROUP)
                    pe.wait_ge(pt_act, (b * HEADS + h + 1) * 2)
                    pe.wait_ge(pt_dve, b * HEADS + h + 1)
                    if j == 0 and g >= 2:
                        pe.wait_ge(y_lo_ready, b * GROUPS + g - 1)
                    first = 3 * HS - HS * j
                    for kt in range(TPB):
                        o = PT_OFFSET[kt]
                        ins = pe.matmul(psum[:, 6 + g % 2, P * kt:SEQ], v_pad[:, kt, g, first:first + P],
                                        probs_t[:, h % 2, o:o + SEQ - P * kt], start=j == 0 and kt == 0,
                                        stop=j == PER_GROUP - 1 and kt == TPB - 1, skip_group_check=True)
                    ins.then_inc(mixed, 1)

                for s in range(HEADS + 3):
                    if s < HEADS:
                        scores(s)
                    if 0 <= s - 2 < HEADS:
                        turn(s - 2)
                    if 0 <= s - 3 < HEADS:
                        mix(s - 3)
                for t in range(TPB):
                    pe.wait_ge(y_lo_ready, (b + 1) * GROUPS)
                    product(psum[:, t, :], lambda k: y_hi[:, k, P * t:P * t + P], lambda k: y_lo[:, k, P * t:P * t + P],
                            w(w_hi, WO, D), w(w_lo, WO, D), range(GROUPS)).then_inc(out_ready, 1)



FF = 4 * D
KF = FF // P
PIECES = 4
Q_MAX = 128.0
BIT_EPS = 1e-6


def row(x_res, t):
    return x_res[:, bass.ds(t, 1), :].rearrange("p a n -> p (a n)")


def tiles_in_steps(engine, step):
    step(0, 0, True, False)
    step(1, 1, False, False)
    with engine.Fori(0, (TILES - 4) // 2) as j:
        for u in range(2):
            step(j * 2 + (2 + u), u, False, False)
    step(TILES - 2, 0, False, False)
    step(TILES - 1, 1, False, False)
    step(TILES, TILES % 2, False, True)


def ternary_mlp(nc, x_res, ident, w_fc, w_proj):
    with ExitStack() as ctx:
        def sb(name, shape, dt=F32):
            return ctx.enter_context(nc.sbuf_tensor(name, shape, dt))

        sem = ctx.enter_context(semaphores(nc))

        psum = ctx.enter_context(nc.psum_tensor("b_psum", [P, 8, 512], F32))
        FC, PROJ = 0, 1
        TURN_X_BANK, OUT_BANK = 6, 7

        raw = sb("b_raw", [P, PIECES, FF])
        negative = sb("b_negative", [P, FF])
        tern = [sb("b_tern_fc", [P, PIECES, FF], F32R), sb("b_tern_proj", [P, PIECES, FF], F32R)]
        piece_sum = sb("b_piece_sum", [P, 2, PIECES])
        row_sum = sb("b_row_sum", [P, 2])
        ones = sb("b_ones", [P, P])
        gamma = sb("b_gamma", [P, 2])
        above = sb("b_above", [P, 2])
        below = sb("b_below", [P, 2])
        minus_half = sb("b_minus_half", [P, 1])
        x_stats = sb("b_x_stats", [P, 2, 6])
        x_mv = sb("b_x_mv", [P, 2, 2, 2])
        x_ve = sb("b_x_ve", [P, 2, 2])
        x_rstd = sb("b_x_rstd", [P, 2, 2])
        x_max = sb("b_x_max", [P, 2])
        x_inv = sb("b_x_inv", [P, 2])
        x_scale = sb("b_x_scale", [P, 2, 2])
        xn = sb("b_xn", [P, 2, D])
        xq_hi = sb("b_xq_hi", [P, 2, KD, P], F32R)
        xq_lo = sb("b_xq_lo", [P, 2, KD, P], F32R)
        h = sb("b_h", [P, 2, FF])
        h_stats = sb("b_h_stats", [P, 2, 4, 6])
        h_mv = sb("b_h_mv", [P, 2, 2])
        h_ve = sb("b_h_ve", [P, 2])
        h_rstd = sb("b_h_rstd", [P, 2])
        h_shift = sb("b_h_shift", [P, 2])
        h_max = sb("b_h_max", [P, 2])
        h_inv = sb("b_h_inv", [P, 2])
        h_scale = sb("b_h_scale", [P, 2, 2])
        ht_hi = sb("b_ht_hi", [P, KF, P], F32R)
        ht_lo = sb("b_ht_lo", [P, KF, P], F32R)

        loaded = [sem(f"b_loaded{k}") for k in range(PIECES)]
        summed = sem("b_summed")
        const_ready = sem("b_const_ready")
        row_summed = sem("b_row_summed")
        total_ready = sem("b_total_ready")
        gamma_ready = sem("b_gamma_ready")
        neg_ready = sem("b_neg_ready")
        tern_ready = [sem("b_tern_fc_ready"), sem("b_tern_proj_ready")]
        x_stat = sem("b_x_stat")
        x_var = sem("b_x_var")
        x_ve_ready = sem("b_x_ve_ready")
        x_rstd_ready = sem("b_x_rstd_ready")
        x_norm = sem("b_x_norm")
        x_peak = sem("b_x_peak")
        x_inv_ready = sem("b_x_inv_ready")
        x_scale_ready = sem("b_x_scale_ready")
        x_clip = sem("b_x_clip")
        xq_ready = sem("b_xq_ready")
        x_turned = sem("b_x_turned")
        xq_hi_ready = sem("b_xq_hi_ready")
        xq_lo_ready = sem("b_xq_lo_ready")
        fc_ready = sem("b_fc_ready")
        gelu_ready = sem("b_gelu_ready")
        h_stat = sem("b_h_stat")
        h_var = sem("b_h_var")
        h_ve_ready = sem("b_h_ve_ready")
        h_rstd_ready = sem("b_h_rstd_ready")
        h_shift_ready = sem("b_h_shift_ready")
        h_norm = sem("b_h_norm")
        h_peak = sem("b_h_peak")
        h_inv_ready = sem("b_h_inv_ready")
        h_scale_ready = sem("b_h_scale_ready")
        h_clip = sem("b_h_clip")
        hq_ready = sem("b_hq_ready")
        h_turned = sem("b_h_turned")
        ht_hi_ready = sem("b_ht_hi_ready")
        ht_lo_ready = sem("b_ht_lo_ready")
        proj_ready = sem("b_proj_ready")
        added = sem("b_added")

        block = ctx.enter_context(nc.Block())

        @block.sync
        def _(sp):
            fc = w_fc.rearrange("(k p) n -> k p n", p=P)
            proj = w_proj.rearrange("(a k p) n -> a p k n", p=P, k=KF // PIECES)
            for k in range(PIECES):
                sp.dma_start(raw[:, k, :], fc[k]).then_inc(loaded[k], 16)
            for k in range(PIECES):
                sp.wait_ge(tern_ready[FC], k + 1)
                sp.dma_start(raw[:, k, :].rearrange("p (k n) -> p k n", k=KF // PIECES), proj[k])\
                  .then_inc(loaded[k], 16)

        @block.gpsimd
        def _(pool):
            pool.memset(ones[:], 1.0).then_inc(const_ready, 1)
            pool.memset(minus_half[:], -0.5).then_inc(const_ready, 1)
            pool.wait_ge(const_ready, 2)

            def x_deviation(t, par, which):
                n = 2 * t + which + 1
                wait_apart(pool, x_var, n)
                pool.tensor_scalar(x_ve[:, par, which:which + 1], x_mv[:, par, which, 1:2],
                                   (LN_EPS, BIT_EPS)[which], None, ALU.add).then_inc(x_ve_ready, 1)
                pool.wait_ge(x_ve_ready, n)
                pool.tensor_tensor(x_rstd[:, par, which:which + 1], x_ve[:, par, which:which + 1], minus_half[:],
                                   ALU.pow).then_inc(x_rstd_ready, 1)

            def x_quantise(t, par):
                wait_apart(pool, x_inv_ready, t + 1)
                pool.tensor_scalar(x_scale[:, par, 0:1], x_inv[:, par:par + 1], Q_MAX, None, ALU.mult)\
                    .then_inc(x_scale_ready, 1)
                pool.tensor_scalar(x_scale[:, par, 1:2], x_max[:, par:par + 1], 1.0 / Q_MAX, None, ALU.mult)\
                    .then_inc(x_scale_ready, 1)
                wait_apart(pool, x_scale_ready, 2 * t + 2)
                pool.tensor_scalar(xn[:, par, :], xn[:, par, :], x_scale[:, par, 0:1], Q_MAX, ALU.mult, ALU.min)\
                    .then_inc(x_clip, 1)
                wait_apart(pool, x_clip, t + 1)
                pool.tensor_scalar(xn[:, par, :], xn[:, par, :], -Q_MAX, x_scale[:, par, 1:2], ALU.max, ALU.mult)\
                    .then_inc(xq_ready, 1)

            def h_deviation(t, par):
                wait_apart(pool, h_var, t + 1)
                pool.tensor_scalar(h_ve[:, par:par + 1], h_mv[:, par, 1:2], BIT_EPS, None, ALU.add)\
                    .then_inc(h_ve_ready, 1)
                pool.wait_ge(h_ve_ready, t + 1)
                pool.tensor_tensor(h_rstd[:, par:par + 1], h_ve[:, par:par + 1], minus_half[:], ALU.pow)\
                    .then_inc(h_rstd_ready, 1)
                wait_apart(pool, h_rstd_ready, t + 1)
                pool.tensor_scalar(h_shift[:, par:par + 1], h_mv[:, par, 0:1], -1.0, h_rstd[:, par:par + 1],
                                   ALU.mult, ALU.mult).then_inc(h_shift_ready, 1)

            x_deviation(0, 0, 0)
            x_deviation(0, 0, 1)
            x_quantise(0, 0)

            def step(t, par, first, last):
                nxt = None if last or (isinstance(t, int) and t == TILES - 1) else t + 1
                if not first:
                    h_deviation(t - 1, 1 - par)
                if nxt is not None:
                    x_deviation(nxt, 1 - par, 0)
                    x_deviation(nxt, 1 - par, 1)
                    x_quantise(nxt, 1 - par)

            tiles_in_steps(pool, step)

        @block.scalar
        def _(act):
            def absolute_sums(w):
                for k in range(PIECES):
                    act.wait_ge(loaded[k], 16 * (w + 1))
                    if w or k:
                        act.wait_ge(summed, PIECES * w + k)
                    act.activation(negative[:], raw[:, k, :], ACT.Abs, accum_out=piece_sum[:, w, k:k + 1])\
                       .then_inc(summed, 1)

            def keep_x(t, par):
                act.wait_ge(x_turned, t + 1)
                act.activation(xq_hi[:, par, :, :], psum[:, TURN_X_BANK, :].rearrange("p (k n) -> p k n", k=KD),
                               ACT.Copy).then_inc(xq_hi_ready, 1)

            def gelu(t, par, slices):
                for s in slices:
                    act.wait_ge(fc_ready, 4 * t + s + 1)
                    act.activation(h[:, par, 512 * s:512 * s + 512], psum[:, s, :], ACT.Gelu,
                                   scale=gamma[:, FC:FC + 1]).then_inc(gelu_ready, 1)

            def normalise_h(t, par):
                act.wait_ge(h_shift_ready, t + 1)
                act.activation(h[:, par, :], h[:, par, :], ACT.Identity, bias=h_shift[:, par:par + 1],
                               scale=h_rstd[:, par:par + 1]).then_inc(h_norm, 1)

            def keep_h(t):
                for s in range(4):
                    act.wait_ge(h_turned, 4 * t + s + 1)
                    act.activation(ht_hi[:, 4 * s:4 * s + 4, :],
                                   psum[:, 4 + s % 2, :].rearrange("p (k n) -> p k n", k=4), ACT.Copy)\
                       .then_inc(ht_hi_ready, 1)

            absolute_sums(FC)
            act.wait_ge(tern_ready[FC], PIECES)
            absolute_sums(PROJ)
            keep_x(0, 0)

            def step(t, par, first, last):
                nxt = None if last or (isinstance(t, int) and t == TILES - 1) else t + 1
                if not last:
                    gelu(t, par, (0, 1))
                if not first:
                    normalise_h(t - 1, 1 - par)
                if not last:
                    gelu(t, par, (2, 3))
                if nxt is not None:
                    keep_x(nxt, 1 - par)
                if not first:
                    keep_h(t - 1)

            act.wait_ge(gamma_ready, 3)
            tiles_in_steps(act, step)

        @block.vector
        def _(dve):
            def thresholds(w):
                dve.wait_ge(summed, PIECES * (w + 1))
                dve.tensor_reduce(row_sum[:, w:w + 1], piece_sum[:, w, :], AX.X, ALU.add).then_inc(row_summed, 1)
                dve.wait_ge(total_ready, w + 1)
                mean = 1.0 / (D * FF)
                total = psum[:, TURN_X_BANK, 0:1]
                dve.tensor_scalar(gamma[:, w:w + 1], total, mean, None, ALU.mult).then_inc(gamma_ready, 1)
                dve.tensor_scalar(above[:, w:w + 1], total, 0.5 * mean, 0.5 * BIT_EPS, ALU.mult, ALU.add)\
                   .then_inc(gamma_ready, 1)
                dve.tensor_scalar(below[:, w:w + 1], total, -0.5 * mean, -0.5 * BIT_EPS, ALU.mult, ALU.add)\
                   .then_inc(gamma_ready, 1)
                dve.wait_ge(gamma_ready, 3 * (w + 1))

            def ternary(w):
                for k in range(PIECES):
                    if k or w:
                        dve.wait_ge(tern_ready[0], k if w == 0 else PIECES)
                    if w and k:
                        dve.wait_ge(tern_ready[1], k)
                    dve.tensor_scalar(negative[:], raw[:, k, :], below[:, w:w + 1], None, ALU.is_lt)\
                       .then_inc(neg_ready, 1)
                    dve.wait_ge(neg_ready, PIECES * w + k + 1)
                    dve.scalar_tensor_tensor(out=tern[w][:, k, :], in0=raw[:, k, :], scalar=above[:, w:w + 1],
                                             in1=negative[:], op0=ALU.is_gt, op1=ALU.subtract)\
                       .then_inc(tern_ready[w], 1)

            def x_variance(t, par, which, source):
                n = 2 * t + which + 1
                dve.bn_stats(x_stats[:, which, :], source).then_inc(x_stat, 1)
                wait_apart(dve, x_stat, n)
                dve.bn_aggr(x_mv[:, par, which, :], x_stats[:, which, :]).then_inc(x_var, 1)

            def x_normalise(t, par, which, source):
                dve.wait_ge(x_rstd_ready, 2 * t + which + 1)
                dve.tensor_scalar(xn[:, par, :], source, x_mv[:, par, which, 0:1], x_rstd[:, par, which:which + 1],
                                  ALU.subtract, ALU.mult).then_inc(x_norm, 1)
                dve.wait_ge(x_norm, 2 * t + which + 1)

            def x_peaks(t, par):
                dve.tensor_reduce(x_max[:, par:par + 1], xn[:, par, :], AX.X, ALU.max, apply_absolute_value=True)\
                   .then_inc(x_peak, 1)
                dve.wait_ge(x_peak, t + 1)
                dve.reciprocal(x_inv[:, par:par + 1], x_max[:, par:par + 1]).then_inc(x_inv_ready, 1)

            def keep_x_low(t, par):
                dve.wait_ge(xq_hi_ready, t + 1)
                dve.tensor_tensor(xq_lo[:, par, :, :], psum[:, TURN_X_BANK, :].rearrange("p (k n) -> p k n", k=KD),
                                  xq_hi[:, par, :, :].bitcast(F32), ALU.subtract).then_inc(xq_lo_ready, 1)

            def h_variance(t, par):
                for s in range(4):
                    dve.wait_ge(gelu_ready, 4 * t + s + 1)
                    dve.bn_stats(h_stats[:, par, s, :], h[:, par, 512 * s:512 * s + 512]).then_inc(h_stat, 1)
                wait_apart(dve, h_stat, 4 * t + 4)
                dve.bn_aggr(h_mv[:, par, :], h_stats[:, par, :, :].rearrange("p s n -> p (s n)")).then_inc(h_var, 1)

            def h_quantise(t, par):
                dve.wait_ge(h_norm, t + 1)
                dve.tensor_reduce(h_max[:, par:par + 1], h[:, par, :], AX.X, ALU.max, apply_absolute_value=True)\
                   .then_inc(h_peak, 1)
                dve.wait_ge(h_peak, t + 1)
                dve.reciprocal(h_inv[:, par:par + 1], h_max[:, par:par + 1]).then_inc(h_inv_ready, 1)
                dve.wait_ge(h_inv_ready, t + 1)
                dve.tensor_scalar(h_scale[:, par, 0:1], h_inv[:, par:par + 1], Q_MAX, None, ALU.mult)\
                   .then_inc(h_scale_ready, 1)
                dve.tensor_scalar(h_scale[:, par, 1:2], h_max[:, par:par + 1], 1.0 / Q_MAX, None, ALU.mult)\
                   .then_inc(h_scale_ready, 1)
                dve.wait_ge(h_scale_ready, 2 * t + 2)
                dve.tensor_scalar(h[:, par, :], h[:, par, :], h_scale[:, par, 0:1], Q_MAX, ALU.mult, ALU.min)\
                   .then_inc(h_clip, 1)
                dve.wait_ge(h_clip, t + 1)
                dve.tensor_scalar(h[:, par, :], h[:, par, :], -Q_MAX, h_scale[:, par, 1:2], ALU.max, ALU.mult)\
                   .then_inc(hq_ready, 1)

            def keep_h_low(t):
                for s in range(4):
                    dve.wait_ge(ht_hi_ready, 4 * t + s + 1)
                    dve.tensor_tensor(ht_lo[:, 4 * s:4 * s + 4, :],
                                      psum[:, 4 + s % 2, :].rearrange("p (k n) -> p k n", k=4),
                                      ht_hi[:, 4 * s:4 * s + 4, :].bitcast(F32), ALU.subtract)\
                       .then_inc(ht_lo_ready, 1)

            def add(t):
                dve.wait_ge(proj_ready, t + 1)
                dve.scalar_tensor_tensor(out=row(x_res, t), in0=psum[:, OUT_BANK, :], scalar=gamma[:, PROJ:PROJ + 1],
                                         in1=row(x_res, t), op0=ALU.mult, op1=ALU.add).then_inc(added, 1)

            x_variance(0, 0, 0, row(x_res, 0))
            x_normalise(0, 0, 0, row(x_res, 0))
            x_variance(0, 0, 1, xn[:, 0, :])
            x_normalise(0, 0, 1, xn[:, 0, :])
            x_peaks(0, 0)
            thresholds(FC)
            ternary(FC)
            keep_x_low(0, 0)
            thresholds(PROJ)
            ternary(PROJ)

            def step(t, par, first, last):
                nxt = None if last or (isinstance(t, int) and t == TILES - 1) else t + 1
                other = 1 - par
                if not first:
                    h_variance(t - 1, other)
                if nxt is not None:
                    x_variance(nxt, other, 0, row(x_res, nxt))
                    x_normalise(nxt, other, 0, row(x_res, nxt))
                    x_variance(nxt, other, 1, xn[:, other, :])
                    x_normalise(nxt, other, 1, xn[:, other, :])
                    x_peaks(nxt, other)
                if not first:
                    h_quantise(t - 1, other)
                if nxt is not None:
                    keep_x_low(nxt, other)
                if not first:
                    keep_h_low(t - 1)
                    add(t - 1)

            tiles_in_steps(dve, step)
            dve.wait_ge(added, TILES)

        @block.tensor
        def _(pe):
            def total(w):
                pe.wait_ge(const_ready, 2)
                pe.wait_ge(row_summed, w + 1)
                pe.matmul(psum[:, TURN_X_BANK, 0:1], ones[:], row_sum[:, w:w + 1], start=True, stop=True)\
                  .then_inc(total_ready, 1)

            def turn_x(t, par):
                pe.wait_ge(xq_ready, t + 1)
                for k in range(KD):
                    ins = pe.transpose(psum[:, TURN_X_BANK, P * k:P * k + P], xn[:, par, P * k:P * k + P], ident[:])
                ins.then_inc(x_turned, 1)

            def fc(t, par, first):
                pe.wait_ge(xq_lo_ready, t + 1)
                for s in range(4):
                    if not first:
                        pe.wait_ge(gelu_ready, 4 * t + s - 3)
                    for k in range(KD):
                        for part in (xq_hi, xq_lo):
                            ins = pe.matmul(psum[:, s, :], part[:, par, k, :], tern[FC][:, k, 512 * s:512 * s + 512],
                                            start=k == 0 and part is xq_hi, stop=k == KD - 1 and part is xq_lo)
                    ins.then_inc(fc_ready, 1)

            def turn_h(t, par):
                pe.wait_ge(hq_ready, t + 1)
                for s in range(4):
                    if s >= 2:
                        pe.wait_ge(ht_lo_ready, 4 * t + s - 1)
                    for k in range(4):
                        c = P * (4 * s + k)
                        ins = pe.transpose(psum[:, 4 + s % 2, P * k:P * k + P], h[:, par, c:c + P], ident[:])
                    ins.then_inc(h_turned, 1)

            def proj(t, first):
                if not first:
                    pe.wait_ge(added, t)
                w = tern[PROJ][:, :, :].rearrange("p a (k n) -> p (a k) n", n=D)
                for k in range(KF):
                    if k % 4 == 0:
                        pe.wait_ge(ht_lo_ready, 4 * t + k // 4 + 1)
                    for part in (ht_hi, ht_lo):
                        ins = pe.matmul(psum[:, OUT_BANK, :], part[:, k, :], w[:, k, :],
                                        start=k == 0 and part is ht_hi, stop=k == KF - 1 and part is ht_lo)
                ins.then_inc(proj_ready, 1)

            total(FC)
            pe.wait_ge(gamma_ready, 3)
            turn_x(0, 0)
            pe.wait_ge(xq_lo_ready, 1)
            total(PROJ)
            pe.wait_ge(gamma_ready, 6)
            pe.wait_ge(tern_ready[FC], PIECES)

            def step(t, par, first, last):
                nxt = None if last or (isinstance(t, int) and t == TILES - 1) else t + 1
                if not last:
                    fc(t, par, first)
                if nxt is not None:
                    turn_x(nxt, 1 - par)
                if first:
                    pe.wait_ge(tern_ready[PROJ], PIECES)
                else:
                    turn_h(t - 1, 1 - par)
                    proj(t - 1, isinstance(t, int) and t == 1)

            tiles_in_steps(pe, step)



L_HEADS = 16
Q_LORA, KV_LORA, NOPE, ROPE, D_V = 384, 128, 128, 64, 128
KQ = Q_LORA // P
TOKENS = BATCH * SEQ
RMS_EPS = 1e-6
SLABS = KQ + 2
H_WQ, H_WK, H_WR, H_WV, H_WO, H_COLS = 0, 384, 512, 896, 1024, 1536


class Step:

    SPAN = 8

    def __init__(self, j, off):
        self.j, self.off = j, off

    def back(self, lag):
        return Step(self.j, self.off - lag)

    def count(self, each=1, more=0):
        n = self.off * each + more
        return n if isinstance(self.j, int) else self.j * (self.SPAN * each) + n

    @property
    def b(self):
        return self.off % BATCH

    @property
    def head(self):
        return Step2(self.j, self.off // BATCH)


class Step2:

    def __init__(self, j, off):
        self.j, self.off = j, off

    def count(self, each=1, more=0):
        n = self.off * each + more
        return n if isinstance(self.j, int) else self.j * (2 * each) + n


def tiles_in_quads(engine, step):
    step(0, 0, True, False)
    step(1, 1, False, False)
    with engine.Fori(0, 3) as j:
        for u in range(4):
            step(j * 4 + (2 + u), (2 + u) % 4, False, False)
    for t in range(14, TILES + 1):
        step(t, t % 4, False, t == TILES)


def latent_projections(nc, x_res, ident, lat_hi, lat_lo, v_hi, v_lo, wqa, wkr, norm_w, key_cos, key_sin):
    with ExitStack() as ctx:
        def sb(name, shape, dt=F32):
            return ctx.enter_context(nc.sbuf_tensor(name, shape, dt))

        sem = ctx.enter_context(semaphores(nc))

        psum = ctx.enter_context(nc.psum_tensor("c_psum", [P, 8, 512], F32))
        X_BANK, Q_BANK, KV_BANK, TURN_BANK = 0, 1, 3, 5
        NQ, NKV = Q_LORA, KV_LORA + ROPE
        w_raw = sb("c_w_raw", [P, KD, NQ + NKV])
        w_hi = sb("c_w_hi", [P, KD, NQ + NKV], F32R)
        w_lo = sb("c_w_lo", [P, KD, NQ + NKV], F32R)
        gain = sb("c_gain", [P, Q_LORA + KV_LORA])
        cosine = sb("c_cosine", [P, TPB, ROPE])
        sine = sb("c_sine", [P, TPB, ROPE])
        minus_half = sb("c_minus_half", [P, 2])
        stats = sb("c_stats", [P, 2, 6])
        mv = sb("c_mv", [P, 2, 2])
        ve = sb("c_ve", [P, 2])
        rstd = sb("c_rstd", [P, 2])
        xn = sb("c_xn", [P, 2, D])
        xt_hi = sb("c_xt_hi", [P, 2, KD, P], F32R)
        xt_lo = sb("c_xt_lo", [P, 2, KD, P], F32R)
        squares = sb("c_squares", [P, 2, Q_LORA])
        mean_sq = sb("c_mean_sq", [P, 2, 2])
        mean_sq_eps = sb("c_mean_sq_eps", [P, 2, 2])
        rms_inv = sb("c_rms_inv", [P, 2, 2])
        latent = sb("c_latent", [P, 2, SLABS * P])
        rot = sb("c_rot", [P, 2, 2, ROPE])

        loaded = sem("c_loaded")
        w_hi_ready = sem("c_w_hi_ready")
        w_lo_ready = sem("c_w_lo_ready")
        const_ready = sem("c_const_ready")
        stat_ready = sem("c_stat_ready")
        var_ready = sem("c_var_ready")
        ve_ready = sem("c_ve_ready")
        rstd_ready = sem("c_rstd_ready")
        xn_ready = sem("c_xn_ready")
        xn_turned = sem("c_xn_turned")
        xt_hi_ready = sem("c_xt_hi_ready")
        xt_lo_ready = sem("c_xt_lo_ready")
        projected = sem("c_projected")
        squared = sem("c_squared")
        ms_ready = sem("c_ms_ready")
        rms_ready = sem("c_rms_ready")
        rot_ready = sem("c_rot_ready")
        latent_ready = sem("c_latent_ready")
        latent_turned = sem("c_latent_turned")
        lat_hi_ready = sem("c_lat_hi_ready")
        lat_lo_ready = sem("c_lat_lo_ready")
        v_hi_ready = sem("c_v_hi_ready")
        v_lo_ready = sem("c_v_lo_ready")
        LATENT_OPS = 4

        block = ctx.enter_context(nc.Block())

        def turned_view():
            return psum[:, :, :].rearrange("p a n -> p (a n)")[:, 512 * TURN_BANK:512 * TURN_BANK + SLABS * P]\
                .rearrange("p (k n) -> p k n", k=SLABS)

        def cols(t):
            return bass.ds(t * P, P)

        def tile(part, t):
            return part[:, bass.ds(t, 1), :].rearrange("p a n -> p (a n)")

        def has_next(t, last):
            return not last and not (isinstance(t, int) and t == TILES - 1)

        @block.sync
        def _(sp):
            sp.dma_start(w_raw[:, :, 0:NQ], wqa.rearrange("(k p) n -> p k n", p=P)).then_inc(loaded, 16)
            sp.dma_start(w_raw[:, :, NQ:NQ + NKV], wkr.rearrange("(k p) n -> p k n", p=P)).then_inc(loaded, 16)
            sp.dma_start(gain[:], norm_w).then_inc(loaded, 16)
            sp.dma_start(cosine[:], key_cos).then_inc(loaded, 16)
            sp.dma_start(sine[:], key_sin).then_inc(loaded, 16)

        @block.gpsimd
        def _(pool):
            pool.memset(minus_half[:], -0.5).then_inc(const_ready, 1)
            pool.wait_ge(const_ready, 1)

            def deviation(t, par):
                wait_apart(pool, var_ready, t + 1)
                pool.tensor_scalar(ve[:, par:par + 1], mv[:, par, 1:2], LN_EPS, None, ALU.add).then_inc(ve_ready, 1)
                pool.wait_ge(ve_ready, t + 1)
                pool.tensor_tensor(rstd[:, par:par + 1], ve[:, par:par + 1], minus_half[:, 0:1], ALU.pow)\
                    .then_inc(rstd_ready, 1)

            def rms(t, par):
                wait_apart(pool, squared, 2 * t + 2)
                pool.tensor_scalar(mean_sq_eps[:, par, :], mean_sq[:, par, :], RMS_EPS, None, ALU.add)\
                    .then_inc(ms_ready, 1)
                pool.wait_ge(ms_ready, t + 1)
                pool.tensor_tensor(rms_inv[:, par, :], mean_sq_eps[:, par, :], minus_half[:], ALU.pow)\
                    .then_inc(rms_ready, 1)

            deviation(0, 0)

            def step(t, quad, first, last):
                par = quad % 2
                if has_next(t, last):
                    deviation(t + 1, 1 - par)
                if not last:
                    rms(t, par)

            tiles_in_quads(pool, step)

        @block.scalar
        def _(act):
            act.wait_ge(loaded, 16 * 5)
            for k in range(KD):
                act.activation(w_hi[:, k, :], w_raw[:, k, :], ACT.Copy).then_inc(w_hi_ready, 1)

            def keep_x(t, par):
                act.wait_ge(xn_turned, t + 1)
                act.activation(xt_hi[:, par, :, :], psum[:, X_BANK, :].rearrange("p (k n) -> p k n", k=KD), ACT.Copy)\
                   .then_inc(xt_hi_ready, 1)

            def mean_squares(t, par, first):
                act.wait_ge(projected, t + 1)
                for which, (bank, n) in enumerate(((Q_BANK, Q_LORA), (KV_BANK, KV_LORA))):
                    if not first:
                        act.wait_ge(squared, 2 * t + which - 1)
                    act.activation(squares[:, which, 0:n], psum[:, bank + par, 0:n], ACT.Square, scale=float(n) ** -0.5,
                                   accum_out=mean_sq[:, par, which:which + 1]).then_inc(squared, 1)

            def keep_latent(t, par):
                act.wait_ge(latent_ready, LATENT_OPS * (t + 1))
                act.activation(tile(v_hi, t), latent[:, par, Q_LORA:Q_LORA + KV_LORA], ACT.Copy).then_inc(v_hi_ready, 1)
                act.wait_ge(latent_turned, t + 1)
                act.activation(lat_hi[:, :, cols(t)], turned_view(), ACT.Copy).then_inc(lat_hi_ready, 1)

            keep_x(0, 0)

            def step(t, quad, first, last):
                par = quad % 2
                if has_next(t, last):
                    keep_x(t + 1, 1 - par)
                if not last:
                    mean_squares(t, par, first)
                if not first:
                    keep_latent(t - 1, 1 - par)

            tiles_in_quads(act, step)
            act.wait_ge(lat_hi_ready, TILES)

        @block.vector
        def _(dve):
            def normalise(t, par):
                dve.bn_stats(stats[:, par, :], row(x_res, t)).then_inc(stat_ready, 1)
                wait_apart(dve, stat_ready, t + 1)
                dve.bn_aggr(mv[:, par, :], stats[:, par, :]).then_inc(var_ready, 1)
                dve.wait_ge(rstd_ready, t + 1)
                dve.tensor_scalar(xn[:, par, :], row(x_res, t), mv[:, par, 0:1], rstd[:, par:par + 1],
                                  ALU.subtract, ALU.mult).then_inc(xn_ready, 1)

            def keep_x_low(t, par):
                dve.wait_ge(xt_hi_ready, t + 1)
                dve.tensor_tensor(xt_lo[:, par, :, :], psum[:, X_BANK, :].rearrange("p (k n) -> p k n", k=KD),
                                  xt_hi[:, par, :, :].bitcast(F32), ALU.subtract).then_inc(xt_lo_ready, 1)

            def make_latent(t, par, quad):
                half = ROPE // 2
                keys = psum[:, KV_BANK + par, KV_LORA:KV_LORA + ROPE]
                dve.wait_ge(projected, t + 1)
                dve.wait_ge(squared, 2 * t + 2)
                if not isinstance(t, int) or t >= 2:
                    dve.wait_ge(v_lo_ready, t - 1)
                dve.tensor_tensor(rot[:, par, 0, :], keys, cosine[:, quad, :], ALU.mult).then_inc(rot_ready, 1)
                dve.tensor_tensor(rot[:, par, 1, 0:half], keys[:, half:ROPE], sine[:, quad, 0:half], ALU.mult)\
                   .then_inc(rot_ready, 1)
                dve.tensor_tensor(rot[:, par, 1, half:ROPE], keys[:, 0:half], sine[:, quad, half:ROPE], ALU.mult)\
                   .then_inc(rot_ready, 1)
                dve.wait_ge(rms_ready, t + 1)
                dve.scalar_tensor_tensor(out=latent[:, par, 0:Q_LORA], in0=psum[:, Q_BANK + par, 0:Q_LORA],
                                         scalar=rms_inv[:, par, 0:1], in1=gain[:, 0:Q_LORA], op0=ALU.mult,
                                         op1=ALU.mult).then_inc(latent_ready, 1)
                dve.scalar_tensor_tensor(out=latent[:, par, Q_LORA:Q_LORA + KV_LORA],
                                         in0=psum[:, KV_BANK + par, 0:KV_LORA], scalar=rms_inv[:, par, 1:2],
                                         in1=gain[:, Q_LORA:Q_LORA + KV_LORA], op0=ALU.mult, op1=ALU.mult)\
                   .then_inc(latent_ready, 1)
                dve.wait_ge(rot_ready, 3 * t + 3)
                for c in range(2):
                    o = Q_LORA + KV_LORA + ROPE * c
                    dve.tensor_tensor(latent[:, par, o:o + ROPE], rot[:, par, 0, :], rot[:, par, 1, :], ALU.add)\
                       .then_inc(latent_ready, 1)

            def keep_latent_low(t, par):
                dve.wait_ge(v_hi_ready, t + 1)
                dve.tensor_tensor(tile(v_lo, t), latent[:, par, Q_LORA:Q_LORA + KV_LORA],
                                  tile(v_hi, t).bitcast(F32), ALU.subtract).then_inc(v_lo_ready, 1)
                dve.wait_ge(lat_hi_ready, t + 1)
                dve.tensor_tensor(lat_lo[:, :, cols(t)], turned_view(), lat_hi[:, :, cols(t)].bitcast(F32),
                                  ALU.subtract).then_inc(lat_lo_ready, 1)

            for k in range(KD):
                dve.wait_ge(w_hi_ready, k + 1)
                dve.tensor_tensor(w_lo[:, k, :], w_raw[:, k, :], w_hi[:, k, :].bitcast(F32), ALU.subtract)\
                   .then_inc(w_lo_ready, 1)
            normalise(0, 0)
            keep_x_low(0, 0)

            def step(t, quad, first, last):
                par = quad % 2
                if has_next(t, last):
                    normalise(t + 1, 1 - par)
                    keep_x_low(t + 1, 1 - par)
                if not last:
                    make_latent(t, par, quad)
                if not first:
                    keep_latent_low(t - 1, 1 - par)

            tiles_in_quads(dve, step)
            dve.wait_ge(lat_lo_ready, TILES)

        @block.tensor
        def _(pe):
            def turn_x(t, par):
                pe.wait_ge(xn_ready, t + 1)
                for k in range(KD):
                    ins = pe.transpose(psum[:, X_BANK, P * k:P * k + P], xn[:, par, P * k:P * k + P], ident[:])
                ins.then_inc(xn_turned, 1)

            def project(t, par):
                pe.wait_ge(xt_lo_ready, t + 1)
                for bank, lo, n in ((Q_BANK, 0, NQ), (KV_BANK, NQ, NKV)):
                    for k in range(KD):
                        for i, (x, w) in enumerate(((xt_hi, w_hi), (xt_hi, w_lo), (xt_lo, w_hi))):
                            ins = pe.matmul(psum[:, bank + par, 0:n], x[:, par, k, :], w[:, k, lo:lo + n],
                                            start=k == 0 and i == 0, stop=k == KD - 1 and i == 2)
                ins.then_inc(projected, 1)

            def turn_latent(t, par):
                pe.wait_ge(latent_ready, LATENT_OPS * (t + 1))
                out = psum[:, :, :].rearrange("p a n -> p (a n)")
                for k in range(SLABS):
                    o = 512 * TURN_BANK + P * k
                    ins = pe.transpose(out[:, o:o + P], latent[:, par, P * k:P * k + P], ident[:])
                ins.then_inc(latent_turned, 1)

            pe.wait_ge(w_lo_ready, KD)
            turn_x(0, 0)

            def step(t, quad, first, last):
                par = quad % 2
                if not last:
                    project(t, par)
                if has_next(t, last):
                    turn_x(t + 1, 1 - par)
                if not first:
                    if not (isinstance(t, int) and t == 1):
                        pe.wait_ge(lat_lo_ready, t - 1)
                    turn_latent(t - 1, 1 - par)

            tiles_in_quads(pe, step)


L_OUT_BANKS = (6, 7, 0, 1)
L_Q_BANK, L_Z_BANK, L_O_BANK = 2, 6, 7
L_WP_BANK, L_WVO_BANK = 3, 4
LAST_LAG = 3


def latent_attention(nc, x_res, ident, lat_hi, lat_lo, v_hi, v_lo, head_w, causal, rotation):
    with ExitStack() as ctx:
        def sb(name, shape, dt=F32):
            return ctx.enter_context(nc.sbuf_tensor(name, shape, dt))

        sem = ctx.enter_context(semaphores(nc))

        psum = ctx.enter_context(nc.psum_tensor("d_psum", [P, 8, 512], F32))
        w_raw = sb("d_w_raw", [P, H_COLS])
        pre_hi = sb("d_pre_hi", [P, 640], F32R)
        pre_lo = sb("d_pre_lo", [P, 640], F32R)
        wr_hi = sb("d_wr_hi", [P, 2, KQ * P], F32R)
        wr_lo = sb("d_wr_lo", [P, 2, KQ * P], F32R)
        wp_hi = sb("d_wp_hi", [P, 2, KQ * P], F32R)
        wp_lo = sb("d_wp_lo", [P, 2, KQ * P], F32R)
        wvo_hi = sb("d_wvo_hi", [P, 2, D], F32R)
        wvo_lo = sb("d_wvo_lo", [P, 2, D], F32R)
        mask = sb("d_mask", [P, SEQ])
        rotate = sb("d_rotate", [P, SEQ])
        q_hi = sb("d_q_hi", [P, 2, SEQ], F32R)
        q_lo = sb("d_q_lo", [P, 2, SEQ], F32R)
        zf = sb("d_zf", [P, SEQ])
        z_hi = sb("d_z_hi", [P, 2, SEQ], F32R)
        z_lo = sb("d_z_lo", [P, 2, SEQ], F32R)
        probs = sb("d_probs", [P, 2, SCORE_COLS])
        pt_hi = sb("d_pt_hi", [P, SCORE_COLS], F32R)
        pt_lo = sb("d_pt_lo", [P, SCORE_COLS], F32R)
        low = sb("d_low", [P, 2, TPB])
        rowsum = sb("d_rowsum", [P, 2, TPB])
        rinv = sb("d_rinv", [P, 2, TPB])
        o_hi = sb("d_o_hi", [P, SEQ], F32R)
        o_lo = sb("d_o_lo", [P, SEQ], F32R)

        tables_loaded = sem("d_tables_loaded")
        w_loaded = sem("d_w_loaded")
        keys_hi = sem("d_keys_hi")
        keys_lo = sem("d_keys_lo")
        rope_hi = sem("d_rope_hi")
        rope_lo = sem("d_rope_lo")
        values_hi = sem("d_values_hi")
        values_lo = sem("d_values_lo")
        wp_made = sem("d_wp_made")
        wp_hi_ready = sem("d_wp_hi_ready")
        wp_lo_ready = sem("d_wp_lo_ready")
        wvo_made = sem("d_wvo_made")
        wvo_hi_ready = sem("d_wvo_hi_ready")
        wvo_lo_ready = sem("d_wvo_lo_ready")
        q_made = sem("d_q_made")
        z_made = sem("d_z_made")
        q_hi_ready = sem("d_q_hi_ready")
        q_lo_ready = sem("d_q_lo_ready")
        zf_ready = sem("d_zf_ready")
        z_hi_ready = sem("d_z_hi_ready")
        z_lo_ready = sem("d_z_lo_ready")
        scores_ready = sem("d_scores_ready")
        masked_ready = sem("d_masked_ready")
        exp_ready = sem("d_exp_ready")
        rinv_ready = sem("d_rinv_ready")
        probs_ready = sem("d_probs_ready")
        turned = sem("d_turned")
        pt_hi_ready = sem("d_pt_hi_ready")
        pt_lo_ready = sem("d_pt_lo_ready")
        mixed = sem("d_mixed")
        o_hi_ready = sem("d_o_hi_ready")
        o_lo_ready = sem("d_o_lo_ready")
        out_ready = sem("d_out_ready")
        added = sem("d_added")

        STEPS = L_HEADS * BATCH
        PT_COPIES = ((3, 0, 512), (4, 512, 512), (5, 1024, 256))

        def run(engine, step):
            for off in range(Step.SPAN):
                step(Step(0, off))
            with engine.Fori(1, STEPS // Step.SPAN - 1) as j:
                for off in range(Step.SPAN):
                    step(Step(j, off))
            for off in range(STEPS - Step.SPAN, STEPS + LAST_LAG):
                step(Step(0, off))

        def begun(s):
            return not isinstance(s.j, int) or 0 <= s.off < STEPS

        def started(s, n=0):
            return not isinstance(s.j, int) or s.off >= n

        def prepares(s, b):
            return s.b == b and begun(s) and not (isinstance(s.j, int) and s.off >= STEPS - BATCH)

        block = ctx.enter_context(nc.Block())

        @block.sync
        def _(sp):
            sp.dma_start(mask[:], causal).then_inc(tables_loaded, 16)
            sp.dma_start(rotate[:], rotation).then_inc(tables_loaded, 16)
            sp.dma_start(w_raw[:], head_w[0]).then_inc(w_loaded, 16)
            with sp.Fori(1, L_HEADS) as h:
                sp.wait_ge(keys_lo, h)
                sp.wait_ge(rope_lo, h)
                sp.wait_ge(values_lo, h)
                sp.dma_start(w_raw[:], head_w[bass.ds(h, 1)].rearrange("a p n -> p (a n)")).then_inc(w_loaded, 16)
            sp.wait_ge(w_loaded, 16 * L_HEADS)

        @block.scalar
        def _(act):
            def split_keys(h, slot, first=False):
                act.wait_ge(w_loaded, h.count(16, 16))
                if not first:
                    act.wait_ge(wvo_made, h.count())
                act.activation(pre_hi[:, 0:512], w_raw[:, 0:512], ACT.Copy).then_inc(keys_hi, 1)
                act.activation(wr_hi[:, slot, :], w_raw[:, H_WR:H_WV], ACT.Copy).then_inc(rope_hi, 1)

            def keep_wp(h, slot):
                act.wait_ge(wp_made, h.count(1, 1))
                act.activation(wp_hi[:, slot, :], psum[:, L_WP_BANK, 0:KQ * P], ACT.Copy).then_inc(wp_hi_ready, 1)

            def split_values(h):
                act.wait_ge(wp_made, h.count(1, 1))
                act.activation(pre_hi[:, 0:640], w_raw[:, H_WV:H_COLS], ACT.Copy).then_inc(values_hi, 1)

            def keep_wvo(h, slot):
                act.wait_ge(wvo_made, h.count(1, 1))
                act.activation(wvo_hi[:, slot, :], psum[:, L_WVO_BANK, :], ACT.Copy).then_inc(wvo_hi_ready, 1)

            h0 = Step2(0, 0)
            split_keys(h0, 0, True)
            keep_wp(h0, 0)
            split_values(h0)
            keep_wvo(h0, 0)

            def step(s):
                o, e, n = s.back(3), s.back(2), s.back(1)
                nxt = s.head
                nxt = Step2(nxt.j, nxt.off + 1)
                slot = nxt.off % 2
                if prepares(s, 2):
                    keep_wp(nxt, slot)
                if prepares(s, 3):
                    keep_wvo(nxt, slot)
                if begun(o):
                    act.wait_ge(mixed, o.count(1, 1))
                    act.activation(o_hi[:], psum[:, L_O_BANK, :], ACT.Copy).then_inc(o_hi_ready, 1)
                if begun(n):
                    for i in range(TPB):
                        act.wait_ge(masked_ready, n.count(TPB, i + 1))
                        c, w = SCORE_OFFSET[i], P * (i + 1)
                        part = probs[:, n.off % 2, c:c + w]
                        act.activation(part, part, ACT.Exp, bias=low[:, n.off % 2, i:i + 1], scale=-1.0,
                                       accum_out=rowsum[:, n.off % 2, i:i + 1]).then_inc(exp_ready, 1)
                if begun(e):
                    act.wait_ge(turned, e.count(1, 1))
                    for bank, c, w in PT_COPIES:
                        act.activation(pt_hi[:, c:c + w], psum[:, bank, 0:w], ACT.Copy).then_inc(pt_hi_ready, 1)
                if begun(s):
                    act.wait_ge(q_made, s.count(1, 1))
                    act.activation(q_hi[:, s.off % 2, :], psum[:, L_Q_BANK, :], ACT.Copy).then_inc(q_hi_ready, 1)
                    act.wait_ge(zf_ready, s.count(1, 1))
                    act.activation(z_hi[:, s.off % 2, :], zf[:], ACT.Copy).then_inc(z_hi_ready, 1)
                if prepares(s, 0):
                    split_keys(nxt, slot)
                if prepares(s, 2):
                    split_values(nxt)

            run(act, step)

        @block.vector
        def _(dve):
            def split_keys(h, slot):
                dve.wait_ge(keys_hi, h.count(1, 1))
                dve.tensor_tensor(pre_lo[:, 0:512], w_raw[:, 0:512], pre_hi[:, 0:512].bitcast(F32), ALU.subtract)\
                   .then_inc(keys_lo, 1)
                dve.wait_ge(rope_hi, h.count(1, 1))
                dve.tensor_tensor(wr_lo[:, slot, :], w_raw[:, H_WR:H_WV], wr_hi[:, slot, :].bitcast(F32),
                                  ALU.subtract).then_inc(rope_lo, 1)

            def keep_wp(h, slot):
                dve.wait_ge(wp_hi_ready, h.count(1, 1))
                dve.tensor_tensor(wp_lo[:, slot, :], psum[:, L_WP_BANK, 0:KQ * P], wp_hi[:, slot, :].bitcast(F32),
                                  ALU.subtract).then_inc(wp_lo_ready, 1)

            def split_values(h):
                dve.wait_ge(values_hi, h.count(1, 1))
                dve.tensor_tensor(pre_lo[:, 0:640], w_raw[:, H_WV:H_COLS], pre_hi[:, 0:640].bitcast(F32),
                                  ALU.subtract).then_inc(values_lo, 1)

            def keep_wvo(h, slot):
                dve.wait_ge(wvo_hi_ready, h.count(1, 1))
                dve.tensor_tensor(wvo_lo[:, slot, :], psum[:, L_WVO_BANK, :], wvo_hi[:, slot, :].bitcast(F32),
                                  ALU.subtract).then_inc(wvo_lo_ready, 1)

            h0 = Step2(0, 0)
            dve.wait_ge(tables_loaded, 32)
            split_keys(h0, 0)
            keep_wp(h0, 0)
            split_values(h0)
            keep_wvo(h0, 0)

            def step(s):
                o, e, n = s.back(3), s.back(2), s.back(1)
                nxt = s.head
                nxt = Step2(nxt.j, nxt.off + 1)
                slot = nxt.off % 2
                if prepares(s, 2):
                    keep_wp(nxt, slot)
                if prepares(s, 3):
                    keep_wvo(nxt, slot)
                if begun(o):
                    dve.wait_ge(o_hi_ready, o.count(1, 1))
                    dve.tensor_tensor(o_lo[:], psum[:, L_O_BANK, :], o_hi[:].bitcast(F32),
                                      ALU.subtract).then_inc(o_lo_ready, 1)
                if begun(n):
                    if started(n, 2):
                        dve.wait_ge(turned, n.count(1, -1))
                    for i in range(TPB):
                        wait_apart(dve, scores_ready, n.count(TPB, (3, 2, 3, 4)[i]))
                        bank, at = SCORE_PLACE[i]
                        c, w = SCORE_OFFSET[i], P * (i + 1)
                        dve.tensor_tensor_reduce(probs[:, n.off % 2, c:c + w], psum[:, bank, at:at + w],
                                                 mask[:, SEQ - w:SEQ], -((NOPE + ROPE) ** -0.5), -MASKED,
                                                 ALU.add, ALU.min, low[:, n.off % 2, i:i + 1])\
                           .then_inc(masked_ready, 1)
                if begun(e):
                    for i, (bank, c, w) in enumerate(PT_COPIES):
                        dve.wait_ge(pt_hi_ready, e.count(3, i + 1))
                        dve.tensor_tensor(pt_lo[:, c:c + w], psum[:, bank, 0:w], pt_hi[:, c:c + w].bitcast(F32),
                                          ALU.subtract).then_inc(pt_lo_ready, 1)
                if begun(n):
                    dve.wait_ge(exp_ready, n.count(TPB, TPB))
                    dve.reciprocal(rinv[:, n.off % 2, :], rowsum[:, n.off % 2, :]).then_inc(rinv_ready, 1)
                    dve.wait_ge(rinv_ready, n.count(1, 1))
                    for i in range(TPB):
                        c, w = SCORE_OFFSET[i], P * (i + 1)
                        part = probs[:, n.off % 2, c:c + w]
                        dve.tensor_scalar(part, part, rinv[:, n.off % 2, i:i + 1], None, ALU.mult)\
                           .then_inc(probs_ready, 1)
                if begun(o):
                    for i, bank in enumerate(L_OUT_BANKS):
                        dve.wait_ge(out_ready, o.count(TPB, i + 1))
                        if started(o, BATCH):
                            dve.wait_ge(added, o.count(TPB, i + 1 - TPB * BATCH))
                        tile = x_res[:, o.b * TPB + i, :]
                        dve.tensor_tensor(tile, psum[:, bank, :], tile, ALU.add).then_inc(added, 1)
                if begun(s):
                    dve.wait_ge(z_made, s.count(1, 1))
                    if started(s, 1):
                        dve.wait_ge(z_hi_ready, s.count())
                        dve.wait_ge(z_lo_ready, s.count())
                    dve.tensor_tensor(zf[:], psum[:, L_Z_BANK, :], rotate[:], ALU.mult).then_inc(zf_ready, 1)
                    dve.wait_ge(q_hi_ready, s.count(1, 1))
                    dve.tensor_tensor(q_lo[:, s.off % 2, :], psum[:, L_Q_BANK, :], q_hi[:, s.off % 2, :].bitcast(F32),
                                      ALU.subtract).then_inc(q_lo_ready, 1)
                    dve.wait_ge(z_hi_ready, s.count(1, 1))
                    dve.tensor_tensor(z_lo[:, s.off % 2, :], zf[:], z_hi[:, s.off % 2, :].bitcast(F32),
                                      ALU.subtract).then_inc(z_lo_ready, 1)
                if prepares(s, 0):
                    split_keys(nxt, slot)
                if prepares(s, 2):
                    split_values(nxt)

            run(dve, step)
            dve.wait_ge(added, STEPS * TPB)

        @block.tensor
        def _(pe):
            def three(out, lhs_hi, lhs_lo, rhs_hi, rhs_lo, first, last):
                for i, (a, c) in enumerate(((lhs_hi, rhs_hi), (lhs_hi, rhs_lo), (lhs_lo, rhs_hi))):
                    ins = pe.matmul(out, a, c, start=first and i == 0, stop=last and i == 2)
                return ins

            def make_wp(h):
                pe.wait_ge(keys_lo, h.count(1, 1))
                for k in range(KQ):
                    ins = three(psum[:, L_WP_BANK, P * k:P * k + P], pre_hi[:, P * k:P * k + P],
                                pre_lo[:, P * k:P * k + P], pre_hi[:, H_WK:H_WK + P], pre_lo[:, H_WK:H_WK + P],
                                True, True)
                ins.then_inc(wp_made, 1)

            def make_wvo(h):
                pe.wait_ge(values_lo, h.count(1, 1))
                three(psum[:, L_WVO_BANK, :], pre_hi[:, 0:P], pre_lo[:, 0:P], pre_hi[:, P:P + D], pre_lo[:, P:P + D],
                      True, True).then_inc(wvo_made, 1)

            h0 = Step2(0, 0)
            make_wp(h0)
            make_wvo(h0)

            def scores(n):
                pe.wait_ge(q_lo_ready, n.count(1, 1))
                pe.wait_ge(z_lo_ready, n.count(1, 1))
                if started(n, 3):
                    pe.wait_ge(added, n.count(TPB, -2 * TPB))
                for i in range(TPB):
                    bank, at = SCORE_PLACE[i]
                    w = P * (i + 1)
                    rows = slice(P * i, P * i + P)
                    out = psum[:, bank, at:at + w]
                    ks = slice(n.b * SEQ, n.b * SEQ + w)
                    three(out, q_hi[:, n.off % 2, rows], q_lo[:, n.off % 2, rows], lat_hi[:, KQ, ks], lat_lo[:, KQ, ks],
                          True, False)
                    three(out, z_hi[:, n.off % 2, rows], z_lo[:, n.off % 2, rows], lat_hi[:, KQ + 1, ks],
                          lat_lo[:, KQ + 1, ks], False, True).then_inc(scores_ready, 1)

            def turn(e):
                pe.wait_ge(probs_ready, e.count(TPB, TPB))
                for kt in range(TPB):
                    bank, at = PT_PLACE[kt]
                    for i in range(kt, TPB):
                        c = SCORE_OFFSET[i] + P * kt
                        ins = pe.transpose(psum[:, bank, at + P * (i - kt):at + P * (i - kt + 1)],
                                           probs[:, e.off % 2, c:c + P], ident[:])
                ins.then_inc(turned, 1)

            def outputs(o):
                pe.wait_ge(o_lo_ready, o.count(1, 1))
                slot = o.head.off % 2
                for i, bank in enumerate(L_OUT_BANKS):
                    rows = slice(P * i, P * i + P)
                    three(psum[:, bank, :], o_hi[:, rows], o_lo[:, rows], wvo_hi[:, slot, :],
                          wvo_lo[:, slot, :], True, True).then_inc(out_ready, 1)

            def project(s):
                slot = s.head.off % 2
                toks = slice(s.b * SEQ, s.b * SEQ + SEQ)
                for bank, hi, lo, made in ((L_Q_BANK, wp_hi, wp_lo, q_made), (L_Z_BANK, wr_hi, wr_lo, z_made)):
                    if bank == L_Z_BANK and started(s, 3):
                        pe.wait_ge(added, s.count(TPB, 1 - 3 * TPB))
                    for k in range(KQ):
                        ins = three(psum[:, bank, :], hi[:, slot, P * k:P * k + P], lo[:, slot, P * k:P * k + P],
                                    lat_hi[:, k, toks], lat_lo[:, k, toks], k == 0, k == KQ - 1)
                    ins.then_inc(made, 1)

            def mix(e):
                pe.wait_ge(pt_lo_ready, e.count(3, 3))
                if started(e, 1):
                    pe.wait_ge(added, e.count(TPB, 2 - TPB))
                for kt in range(TPB):
                    c, w = PT_OFFSET[kt], SEQ - P * kt
                    out = psum[:, L_O_BANK, P * kt:SEQ]
                    t = e.b * TPB + kt
                    for i, (v, p) in enumerate(((v_hi, pt_hi), (v_hi, pt_lo), (v_lo, pt_hi))):
                        ins = pe.matmul(out, v[:, t, :], p[:, c:c + w], start=kt == 0 and i == 0,
                                        stop=kt == TPB - 1 and i == 2, skip_group_check=True)
                ins.then_inc(mixed, 1)

            def step(s):
                o, e, n = s.back(3), s.back(2), s.back(1)
                nxt = s.head
                nxt = Step2(nxt.j, nxt.off + 1)
                if begun(n):
                    scores(n)
                if begun(e):
                    if prepares(s, 2):
                        pe.wait_ge(wp_lo_ready, nxt.count(1, 1))
                    if prepares(s, 3):
                        pe.wait_ge(wvo_lo_ready, nxt.count(1, 1))
                    turn(e)
                if begun(n):
                    pe.wait_ge(masked_ready, n.count(TPB, TPB))
                if begun(o):
                    outputs(o)
                if begun(s):
                    if s.b == 0:
                        pe.wait_ge(wp_lo_ready, s.head.count(1, 1))
                        pe.wait_ge(rope_lo, s.head.count(1, 1))
                    project(s)
                if begun(e):
                    mix(e)
                if prepares(s, 1):
                    make_wp(nxt)
                if prepares(s, 2):
                    make_wvo(nxt)

            run(pe, step)



ROUTED, TOP_K = 7, 3
EXPERTS = ROUTED + 1
HALF = TILES // 2
ROUTED_SLOTS = TOP_K * TOKENS // P + ROUTED - 1
LAST_HALF = HALF + ROUTED_SLOTS
SLOTS = LAST_HALF + HALF
TURNS = ROUTED + 2
RANKS = ROUTED * ROUTED
TABLE = "table"
K_BEFORE, K_EARLIER, K_FILLS, K_SLOT = 0, P, P + RANKS, P + RANKS + TILES
K_COLS = K_SLOT + SLOTS


def mixture_of_experts(nc, x_res, ident, weights, gate_w, gate_b, select_b, constants, slot_in, slot_out):
    with ExitStack() as ctx:
        def sb(name, shape, dt=F32):
            return ctx.enter_context(nc.sbuf_tensor(name, shape, dt))

        sem = ctx.enter_context(semaphores(nc))

        psum = ctx.enter_context(nc.psum_tensor("e_psum", [P, 8, 512], F32))
        X_BANK, UP_BANK, GATE_BANK, H_BANK, OUT_BANK, COUNT_BANK, LOGIT_BANK, PLACE_BANK = range(8)
        LOGIT_T_BANKS = (4, 5)
        raw = sb("e_raw", [P, 3, KD, D])
        w_hi = sb("e_w_hi", [P, 2, 3, KD, D], F32R)
        w_lo = sb("e_w_lo", [P, 2, 3, KD, D], F32R)
        gt_hi, gt_lo = w_hi[:, 1, 0], w_lo[:, 1, 0]
        rows = sb("e_rows", [P, 2, TPB, D])
        xs = sb("e_xs", [P, D])
        xt_hi = sb("e_xt_hi", [P, KD, P], F32R)
        xt_lo = sb("e_xt_lo", [P, KD, P], F32R)
        gated = sb("e_gated", [P, D])
        product = sb("e_product", [P, D])
        logits_t = (gated[0:EXPERTS, :], product[0:EXPERTS, :])
        ht_hi = sb("e_ht_hi", [P, KD, P], F32R)
        ht_lo = sb("e_ht_lo", [P, KD, P], F32R)
        ys = sb("e_ys", [P, D])
        stats = sb("e_stats", [P, TPB, 6])
        mv = sb("e_mv", [P, TPB, 2])
        ve = sb("e_ve", [P, TPB])
        rstd = sb("e_rstd", [P, 2, TPB])
        shift = sb("e_shift", [P, 2, TPB])
        minus_half = sb("e_minus_half", [P, TPB])
        ones = sb("e_ones", [P, P])
        ones_r = sb("e_ones_r", [P, P], F32R)
        above_r = sb("e_above_r", [P, P], F32R)
        zero = sb("e_zero", [P, TILES])
        table = sb("e_table", [P, K_COLS])
        g_raw = sb("e_g_raw", [P, KD, EXPERTS])
        g_hi = sb("e_g_hi", [P, KD, EXPERTS], F32R)
        g_lo = sb("e_g_lo", [P, KD, EXPERTS], F32R)
        g_bias = sb("e_g_bias", [EXPERTS, 1])
        s_bias = sb("e_s_bias", [P, ROUTED])
        logits = sb("e_logits", [P, TILES, ROUTED])
        top = sb("e_top", [P, TILES])
        proba = sb("e_proba", [P, TILES, ROUTED])
        biased = sb("e_biased", [P, TILES, ROUTED])
        beats = sb("e_beats", [P, TILES, ROUTED, ROUTED])
        rank = sb("e_rank", [P, TILES, ROUTED])
        total = sb("e_total", [P, 2, TILES])
        chosen = sb("e_chosen", [P, TILES, EXPERTS], F32R)
        per_expert = sb("e_per_expert", [P, ROUTED])
        fills = sb("e_fills", [P, ROUTED, TILES])
        slots_of = sb("e_slots_of", [P, ROUTED])
        before_of = sb("e_before_of", [P, ROUTED, ROUTED])
        start = sb("e_start", [P, EXPERTS])
        place = sb("e_place", [P, TILES, ROUTED])
        nth = sb("e_nth", [P, TILES, ROUTED])
        pick = sb("e_pick", [P, TILES, ROUTED])
        picked = sb("e_picked", [P, TILES, ROUTED])
        share = sb("e_share", [P, TILES, TOP_K])
        target = sb("e_target", [P, TILES, TOP_K])
        target_row = sb("e_target_row", [P, TILES * TOP_K], mybir.dt.int32)
        result_row = sb("e_result_row", [P, TILES * TOP_K], mybir.dt.int32)
        share_now = sb("e_share_now", [P, 2 * TOP_K])
        started = sb("e_started", [1, SLOTS, EXPERTS])
        turn = sb("e_turn", [1, SLOTS])
        fresh = sb("e_fresh", [1, 2, SLOTS])
        turn_of = sb("e_turn_of", [1, SLOTS], mybir.dt.int32)
        next_of = sb("e_next_of", [1, SLOTS], mybir.dt.int32)

        small_loaded = sem("e_small_loaded")
        w_loaded = [sem(f"e_w_loaded{m}") for m in range(3)]
        const_ready = sem("e_const_ready")
        g_hi_ready = sem("e_g_hi_ready")
        g_lo_ready = sem("e_g_lo_ready")
        stat_ready = sem("e_stat_ready")
        var_ready = sem("e_var_ready")
        ve_ready = sem("e_ve_ready")
        rstd_ready = sem("e_rstd_ready")
        shift_ready = sem("e_shift_ready")
        xn_ready = sem("e_xn_ready")
        xn_turned = sem("e_xn_turned")
        xn_stored = sem("e_xn_stored")
        gt_hi_ready = sem("e_gt_hi_ready")
        gt_lo_ready = sem("e_gt_lo_ready")
        logits_made = sem("e_logits_made")
        centred_ready = sem("e_centred_ready")
        exp_ready = sem("e_exp_ready")
        logits_kept = sem("e_logits_kept")
        logits_turned = sem("e_logits_turned")
        gate_step = sem("e_gate_step")
        sums_ready = sem("e_sums_ready")
        chosen_ready = sem("e_chosen_ready")
        place_made = sem("e_place_made")
        counted = sem("e_counted")
        targets_ready = sem("e_targets_ready")
        turns_ready = sem("e_turns_ready")
        rows_loaded = sem("e_rows_loaded")
        row_ready = sem("e_row_ready")
        scattered = sem("e_scattered")
        xs_loaded = sem("e_xs_loaded")
        x_turned = sem("e_x_turned")
        xt_hi_ready = sem("e_xt_hi_ready")
        xt_lo_ready = sem("e_xt_lo_ready")
        w_hi_ready = sem("e_w_hi_ready")
        w_lo_ready = sem("e_w_lo_ready")
        up_made = sem("e_up_made")
        gated_ready = sem("e_gated_ready")
        product_ready = sem("e_product_ready")
        h_turned = sem("e_h_turned")
        ht_hi_ready = sem("e_ht_hi_ready")
        ht_lo_ready = sem("e_ht_lo_ready")
        out_made = sem("e_out_made")
        ys_ready = sem("e_ys_ready")
        ys_stored = sem("e_ys_stored")
        gathered = [sem("e_gathered0"), sem("e_gathered1")]
        share_ready = sem("e_share_ready")
        combined = sem("e_combined")
        added = sem("e_added")

        block = ctx.enter_context(nc.Block())

        def steps(engine, step):
            last = TURNS - 1
            step(0, 0, None, None)
            with engine.Fori(1, HALF) as s:
                step(s, 0, 0, "first half")
            step(HALF, 1, 0, "first half")
            step(HALF + 1, TABLE, 1, "routed")
            with engine.Fori(HALF + 2, LAST_HALF) as s:
                step(s, TABLE, TABLE, "routed")
            step(LAST_HALF, last, TABLE, "routed")
            with engine.Fori(LAST_HALF + 1, SLOTS - 1) as s:
                step(s, last, last, "second half")
            step(SLOTS - 1, last, last, "second half")
            step(SLOTS, None, last, "second half")

        def has_next(s):
            return not (isinstance(s, int) and s >= SLOTS - 1)

        def turn_at(engine, s, known):
            if known is not TABLE:
                return known
            return engine.value_load(turn_of[0:1, bass.ds(s, 1)], min_val=1, max_val=TURNS - 2)

        def when_fresh(engine, s, now, split):
            if now is TABLE:
                n = engine.value_load(next_of[0:1, bass.ds(s, 1)], min_val=0, max_val=TURNS - 1)
                with engine.If(n != 0):
                    split(n)
            elif isinstance(s, int) and s in (0, HALF):
                split(now + 1)

        def matrix(part, n, m):
            if isinstance(n, int):
                return part[:, n % 2, m]
            return part[:, bass.ds(n % 2, 1), m].rearrange("p a k n -> p (a k) n")

        def block_of(part, n, m, k):
            if isinstance(n, int):
                return part[:, n % 2, m, k]
            return part[:, bass.ds(n % 2, 1), m, k].rearrange("p a n -> p (a n)")

        def home(b):
            slot = TPB * b if b < BATCH // 2 else LAST_HALF - HALF + TPB * b
            return slot_in[P * slot:P * (slot + TPB)].rearrange("(t p) n -> p t n", p=P)

        def chunks(bank):
            return psum[:, bank, :].rearrange("p (k n) -> p k n", k=KD)

        @block.sync
        def _(sp):
            for dest, source in ((table, constants), (g_bias, gate_b), (s_bias, select_b)):
                sp.dma_start(dest[:], source).then_inc(small_loaded, 16)
            sp.dma_start(g_raw[:], gate_w.rearrange("(k p) n -> p k n", p=P)).then_inc(small_loaded, 16)
            for b in range(BATCH):
                sp.wait_ge(xn_ready, TPB * (b + 1))
                if b:
                    sp.wait_ge(xn_stored, 16 * b)
                sp.dma_start(home(b), rows[:, b % 2]).then_inc(xn_stored, 16)
            sp.wait_ge(xn_stored, 16 * BATCH)

            def load(s):
                if not (isinstance(s, int) and s == 0):
                    sp.wait_ge(x_turned, s)
                sp.dma_start(xs[:], slot_in[bass.ds(s * P, P), :]).then_inc(xs_loaded, 16)

            def store(s):
                sp.wait_ge(ys_ready, s - (HALF - 1))
                sp.dma_start(slot_out[bass.ds((s - HALF) * P, P), :], ys[:]).then_inc(ys_stored, 16)

            load(0)
            with sp.Fori(1, HALF) as s:
                load(s)
            sp.wait_ge(scattered, 16 * TILES * TOP_K)
            load(HALF)
            load(HALF + 1)
            with sp.Fori(HALF + 1, LAST_HALF + 1) as s:
                load(s + 1)
                store(s - 1)
            with sp.Fori(LAST_HALF + 2, SLOTS) as s:
                load(s)
            sp.wait_ge(ys_stored, 16 * ROUTED_SLOTS)

        @block.gpsimd
        def _(pool):
            for m in range(3):
                pool.dma_start(raw[:, m], weights[0, m].rearrange("(k p) n -> p k n", p=P)).then_inc(w_loaded[m], 16)
            pool.memset(minus_half[:], -0.5).then_inc(const_ready, 1)
            pool.memset(ones[:], 1.0).then_inc(const_ready, 1)
            pool.memset(zero[:], 0.0).then_inc(const_ready, 1)
            pool.wait_ge(const_ready, 3)
            for b in range(BATCH):
                if b:
                    pool.wait_ge(rstd_ready, b)
                pool.wait_ge(var_ready, TPB * (b + 1))
                pool.tensor_scalar(ve[:], mv[:, :, 1], LN_EPS, None, ALU.add).then_inc(ve_ready, 1)
                pool.wait_ge(ve_ready, b + 1)
                if b >= 2:
                    pool.wait_ge(xn_ready, TPB * (b - 1))
                pool.tensor_tensor(rstd[:, b % 2, :], ve[:], minus_half[:], ALU.pow).then_inc(rstd_ready, 1)

            def load_weights(n):
                for m in range(3):
                    pool.wait_ge(w_lo_ready, n * 3 + (m - 2))
                    source = weights[bass.ds(n, 1), m].rearrange("a (k p) n -> p (a k) n", p=P)
                    pool.dma_start(raw[:, m], source).then_inc(w_loaded[m], 16)

            load_weights(1)
            pool.wait_ge(xn_stored, 16 * BATCH)
            pool.wait_ge(targets_ready, 2)

            def load_rows(b):
                if b >= 2:
                    pool.wait_ge(scattered, 16 * TPB * TOP_K * (b - 1))
                pool.dma_start(rows[:, b % 2], home(b)).then_inc(rows_loaded, 16)

            def row_of(table_, t, c):
                at = t * TOP_K + c
                return bass.IndirectOffsetOnAxis(ap=table_[:, at:at + 1], axis=0)

            load_rows(0)
            for b in range(BATCH):
                pool.wait_ge(rows_loaded, 16 * (b + 1))
                if b + 1 < BATCH:
                    load_rows(b + 1)
                for i in range(TPB):
                    for c in range(TOP_K):
                        pool.indirect_dma_start(slot_in, row_of(target_row, TPB * b + i, c), rows[:, b % 2, i, :], None)\
                            .then_inc(scattered, 16)
            with pool.Fori(2, TURNS) as n:
                load_weights(n)

            pool.wait_ge(scattered, 16 * TILES * TOP_K)
            pool.wait_ge(ys_stored, 16 * ROUTED_SLOTS)
            for t in range(TILES):
                if t >= 2:
                    pool.wait_ge(combined, TOP_K * (t - 1))
                for c in range(TOP_K):
                    pool.indirect_dma_start(rows[:, t % 2, c, :], None, slot_out, row_of(result_row, t, c))\
                        .then_inc(gathered[t % 2], 16)

        @block.scalar
        def _(act):
            act.wait_ge(small_loaded, 64)
            act.activation(g_hi[:], g_raw[:], ACT.Copy).then_inc(g_hi_ready, 1)
            act.activation(above_r[:], table[:, K_BEFORE:K_BEFORE + P], ACT.Copy).then_inc(sums_ready, 1)
            act.wait_ge(const_ready, 3)
            act.activation(ones_r[:], ones[:], ACT.Copy).then_inc(sums_ready, 1)

            def keep_logits(b):
                act.wait_ge(logits_made, b + 1)
                if b >= 2:
                    act.wait_ge(logits_turned, b - 1)
                act.activation(logits_t[b % 2], psum[0:EXPERTS, LOGIT_T_BANKS[b % 2], :], ACT.Identity,
                               bias=g_bias[:]).then_inc(logits_kept, 1)

            for b in range(BATCH):
                act.wait_ge(shift_ready, b + 1)
                if b >= 2:
                    act.wait_ge(xn_stored, 16 * (b - 1))
                for i in range(TPB):
                    act.activation(rows[:, b % 2, i, :], x_res[:, TPB * b + i, :], ACT.Identity,
                                   bias=shift[:, b % 2, i:i + 1], scale=rstd[:, b % 2, i:i + 1]).then_inc(xn_ready, 1)
                if b:
                    keep_logits(b - 1)
                for i in range(TPB):
                    act.wait_ge(xn_turned, TPB * b + i + 1)
                    if b:
                        act.wait_ge(logits_made, b)
                    act.activation(gt_hi[:, :, P * i:P * i + P], chunks(i), ACT.Copy).then_inc(gt_hi_ready, 1)
                if b < 3:
                    act.wait_ge(w_loaded[b], 16)
                    act.activation(w_hi[:, 0, b], raw[:, b], ACT.Copy).then_inc(w_hi_ready, 1)
            keep_logits(BATCH - 1)
            act.wait_ge(centred_ready, 1)
            act.activation(proba[:], logits[:], ACT.Exp).then_inc(exp_ready, 1)

            def keep_x(s):
                act.wait_ge(x_turned, s + 1)
                act.activation(xt_hi[:], chunks(X_BANK), ACT.Copy).then_inc(xt_hi_ready, 1)

            def split(n):
                for m in range(3):
                    act.wait_ge(w_loaded[m], n * 16 + 16)
                    act.activation(matrix(w_hi, n, m), raw[:, m], ACT.Copy).then_inc(w_hi_ready, 1)

            def step(s, now, before, kind):
                if now is not None:
                    act.wait_ge(up_made, s * 2 + 1)
                    act.activation(gated[:], psum[:, UP_BANK, :], ACT.Silu).then_inc(gated_ready, 1)
                    if has_next(s):
                        keep_x(s + 1)
                if kind == "routed":
                    act.wait_ge(out_made, s)
                    if not (isinstance(s, int) and s == HALF + 1):
                        act.wait_ge(ys_stored, s * 16 - 16 * (HALF + 1))
                    act.activation(ys[:], psum[:, OUT_BANK, :], ACT.Copy).then_inc(ys_ready, 1)
                if now is not None:
                    act.wait_ge(h_turned, s + 1)
                    act.activation(ht_hi[:], chunks(H_BANK), ACT.Copy).then_inc(ht_hi_ready, 1)
                    when_fresh(act, s, now, split)

            keep_x(0)
            steps(act, step)

        @block.vector
        def _(dve):
            own = Tally(gate_step)

            def done(ins):
                own.inc(ins)
                own.wait(dve)

            def over_experts(column):
                return column.unsqueeze(2).broadcast_to([P, TILES, ROUTED])

            def on_every_tile(line):
                return line.unsqueeze(1).broadcast_to([P, TILES, ROUTED])

            dve.wait_ge(g_hi_ready, 1)
            dve.tensor_tensor(g_lo[:], g_raw[:], g_hi[:].bitcast(F32), ALU.subtract).then_inc(g_lo_ready, 1)

            def statistics(b):
                for i in range(TPB):
                    dve.bn_stats(stats[:, i, :], x_res[:, TPB * b + i, :]).then_inc(stat_ready, 1)
                for i in range(TPB):
                    dve.wait_ge(stat_ready, TPB * b + i + 1)
                    dve.bn_aggr(mv[:, i, :], stats[:, i, :]).then_inc(var_ready, 1)

            statistics(0)
            for b in range(BATCH):
                dve.wait_ge(rstd_ready, b + 1)
                if b >= 2:
                    dve.wait_ge(xn_ready, TPB * (b - 1))
                dve.scalar_tensor_tensor(out=shift[:, b % 2, :], in0=mv[:, :, 0], scalar=-1.0, in1=rstd[:, b % 2, :],
                                         op0=ALU.mult, op1=ALU.mult).then_inc(shift_ready, 1)
                if b + 1 < BATCH:
                    dve.wait_ge(shift_ready, b + 1)
                    statistics(b + 1)
                for i in range(TPB):
                    dve.wait_ge(gt_hi_ready, TPB * b + i + 1)
                    cols = slice(P * i, P * i + P)
                    dve.tensor_tensor(gt_lo[:, :, cols], chunks(i), gt_hi[:, :, cols].bitcast(F32), ALU.subtract)\
                       .then_inc(gt_lo_ready, 1)

            dve.wait_ge(logits_turned, BATCH)
            made = psum[:, LOGIT_BANK, 0:TILES * EXPERTS].rearrange("p (t e) -> p t e", e=EXPERTS)[:, :, 0:ROUTED]
            done(dve.tensor_reduce(top[:], made, AX.X, ALU.max))
            dve.tensor_tensor(logits[:], made, over_experts(top[:]), ALU.subtract).then_inc(centred_ready, 1)
            dve.wait_ge(exp_ready, 1)
            done(dve.tensor_reduce(total[:, 0, :], proba[:], AX.X, ALU.add))
            done(dve.reciprocal(total[:, 1, :], total[:, 0, :]))
            done(dve.tensor_tensor(proba[:], proba[:], over_experts(total[:, 1, :]), ALU.mult))
            done(dve.tensor_tensor(biased[:], proba[:], on_every_tile(s_bias[:]), ALU.add))
            for j in range(ROUTED):
                for lo, hi, op in ((0, j, ALU.is_gt), (j, ROUTED, ALU.is_ge)):
                    if hi > lo:
                        other = biased[:, :, j:j + 1].broadcast_to([P, TILES, hi - lo])
                        own.inc(dve.tensor_tensor(beats[:, :, lo:hi, j], other, biased[:, :, lo:hi], op))
            own.wait(dve)
            done(dve.tensor_reduce(rank[:], beats[:], AX.X, ALU.add))
            dve.wait_ge(const_ready, 3)
            dve.tensor_copy(chosen[:, :, ROUTED], zero[:]).then_inc(chosen_ready, 1)
            dve.tensor_scalar(chosen[:, :, 0:ROUTED], rank[:], TOP_K + 0.5, None, ALU.is_lt).then_inc(chosen_ready, 1)
            dve.wait_ge(chosen_ready, 2)
            picks = chosen[:, :, 0:ROUTED].bitcast(F32)
            dve.tensor_reduce(per_expert[:], picks.rearrange("p t e -> p e t"), AX.X, ALU.add)\
               .then_inc(chosen_ready, 1)
            done(dve.tensor_tensor(proba[:], proba[:], picks, ALU.mult))
            done(dve.tensor_reduce(total[:, 0, :], proba[:], AX.X, ALU.add))
            done(dve.reciprocal(total[:, 1, :], total[:, 0, :]))
            done(dve.tensor_tensor(proba[:], proba[:], over_experts(total[:, 1, :]), ALU.mult))
            own.inc(dve.memset(nth[:, :, 0:1], 0.0))
            for e in range(1, ROUTED):
                own.wait(dve)
                own.inc(dve.tensor_tensor(nth[:, :, e:e + 1], nth[:, :, e - 1:e], picks[:, :, e - 1:e], ALU.add))
            for m in range(3):
                dve.wait_ge(w_hi_ready, m + 1)
                dve.tensor_tensor(w_lo[:, 0, m], raw[:, m], w_hi[:, 0, m].bitcast(F32), ALU.subtract)\
                   .then_inc(w_lo_ready, 1)

            dve.wait_ge(counted, 1)
            full = table[:, K_FILLS:K_FILLS + TILES].unsqueeze(1).broadcast_to([P, ROUTED, TILES])
            count = psum[:, COUNT_BANK, 0:ROUTED].unsqueeze(2).broadcast_to([P, ROUTED, TILES])
            done(dve.tensor_tensor(fills[:], count, full, ALU.is_gt))
            done(dve.tensor_reduce(slots_of[:], fills[:], AX.X, ALU.add))
            done(dve.tensor_scalar(slots_of[:], slots_of[:], 1.0, None, ALU.max))
            earlier = table[:, K_EARLIER:K_EARLIER + RANKS].rearrange("p (e f) -> p e f", f=ROUTED)
            done(dve.tensor_tensor(before_of[:], slots_of[:].unsqueeze(1).broadcast_to([P, ROUTED, ROUTED]), earlier,
                                   ALU.mult))
            done(dve.tensor_reduce(start[:, 0:ROUTED], before_of[:], AX.X, ALU.add))
            done(dve.tensor_scalar(start[:, 0:ROUTED], start[:, 0:ROUTED], float(HALF), None, ALU.add))
            done(dve.memset(start[:, ROUTED:EXPERTS], float(LAST_HALF)))
            ahead = psum[:, PLACE_BANK, 0:TILES * EXPERTS].rearrange("p (t e) -> p t e", e=EXPERTS)[:, :, 0:ROUTED]
            dve.wait_ge(place_made, 1)
            done(dve.scalar_tensor_tensor(out=place[:], in0=on_every_tile(start[:, 0:ROUTED]), scalar=float(P),
                                          in1=ahead, op0=ALU.mult, op1=ALU.add))
            for c in range(TOP_K):
                done(dve.scalar_tensor_tensor(out=pick[:], in0=nth[:], scalar=float(c), in1=picks,
                                              op0=ALU.is_equal, op1=ALU.mult))
                for source, dest in ((place, target), (proba, share)):
                    done(dve.tensor_tensor(picked[:], pick[:], source[:], ALU.mult))
                    done(dve.tensor_reduce(dest[:, :, c], picked[:], AX.X, ALU.add))
            dve.tensor_copy(target_row[:], target[:].rearrange("p t c -> p (t c)")).then_inc(targets_ready, 1)
            done(dve.tensor_scalar(target[:], target[:], float(-HALF * P), None, ALU.add))
            dve.tensor_copy(result_row[:], target[:].rearrange("p t c -> p (t c)")).then_inc(targets_ready, 1)
            slot = table[0:1, K_SLOT:K_SLOT + SLOTS].unsqueeze(2).broadcast_to([1, SLOTS, EXPERTS])
            done(dve.tensor_tensor(started[:], slot, start[0:1, :].unsqueeze(1).broadcast_to([1, SLOTS, EXPERTS]),
                                   ALU.is_ge))
            done(dve.tensor_reduce(turn[:], started[:], AX.X, ALU.add))
            done(dve.tensor_tensor(fresh[:, 0, 1:SLOTS], turn[:, 1:SLOTS], turn[:, 0:SLOTS - 1], ALU.subtract))
            done(dve.memset(fresh[:, 0, 0:1], 0.0))
            done(dve.scalar_tensor_tensor(out=fresh[:, 1, :], in0=turn[:], scalar=1.0, in1=fresh[:, 0, :],
                                          op0=ALU.add, op1=ALU.mult))
            dve.tensor_copy(turn_of[:], turn[:]).then_inc(turns_ready, 1)
            dve.tensor_copy(next_of[:], fresh[:, 1, :]).then_inc(turns_ready, 1)

            def keep_x_low(s):
                dve.wait_ge(xt_hi_ready, s + 1)
                dve.tensor_tensor(xt_lo[:], chunks(X_BANK), xt_hi[:].bitcast(F32), ALU.subtract)\
                   .then_inc(xt_lo_ready, 1)

            def split(n):
                for m in range(3):
                    dve.wait_ge(w_hi_ready, n * 3 + (m + 1))
                    dve.tensor_tensor(matrix(w_lo, n, m), raw[:, m], matrix(w_hi, n, m).bitcast(F32), ALU.subtract)\
                       .then_inc(w_lo_ready, 1)

            def combine(s):
                i = s - (LAST_HALF + 1)
                dve.tensor_copy(share_now[:], share[:, bass.ds(i * 2, 2), :].rearrange("p t c -> p (t c)"))\
                   .then_inc(share_ready, 1)
                dve.wait_ge(share_ready, i + 1)
                for j in range(2):
                    dve.wait_ge(gathered[j], (i + 1) * (16 * TOP_K))
                    tile = x_res[:, bass.ds(i * 2 + j, 1), :].rearrange("p a n -> p (a n)")
                    for c in range(TOP_K):
                        dve.scalar_tensor_tensor(out=tile, in0=rows[:, j, c, :],
                                                 scalar=share_now[:, TOP_K * j + c:TOP_K * j + c + 1], in1=tile,
                                                 op0=ALU.mult, op1=ALU.add).then_inc(combined, 1)
                        dve.wait_ge(combined, i * (2 * TOP_K) + (TOP_K * j + c + 1))

            def step(s, now, before, kind):
                if now is not None:
                    dve.wait_ge(gated_ready, s + 1)
                    dve.wait_ge(up_made, s * 2 + 2)
                    dve.tensor_tensor(product[:], gated[:], psum[:, GATE_BANK, :], ALU.mult).then_inc(product_ready, 1)
                    if has_next(s):
                        keep_x_low(s + 1)
                if kind in ("first half", "second half"):
                    dve.wait_ge(out_made, s)
                    t = s - 1 if kind == "first half" else s - (LAST_HALF + 1 - HALF)
                    dve.tensor_tensor(row(x_res, t), psum[:, OUT_BANK, :], row(x_res, t), ALU.add).then_inc(added, 1)
                if now is not None:
                    dve.wait_ge(ht_hi_ready, s + 1)
                    dve.tensor_tensor(ht_lo[:], chunks(H_BANK), ht_hi[:].bitcast(F32), ALU.subtract)\
                       .then_inc(ht_lo_ready, 1)
                    when_fresh(dve, s, now, split)
                if kind == "second half":
                    dve.wait_ge(added, s - (LAST_HALF - HALF))
                    combine(s)

            keep_x_low(0)
            steps(dve, step)

        @block.tensor
        def _(pe):
            def three(out, lhs, rhs, first, last):
                for i, (a, c) in enumerate(((lhs[0], rhs[0]), (lhs[0], rhs[1]), (lhs[1], rhs[0]))):
                    ins = pe.matmul(out, a, c, start=first and i == 0, stop=last and i == 2)
                return ins

            def turn_logits(b):
                pe.wait_ge(logits_kept, b + 1)
                for i in range(TPB):
                    at = EXPERTS * (TPB * b + i)
                    ins = pe.transpose(psum[:, LOGIT_BANK, at:at + EXPERTS], logits_t[b % 2][:, P * i:P * i + P],
                                       ident[0:EXPERTS, 0:EXPERTS])
                ins.then_inc(logits_turned, 1)

            pe.wait_ge(g_lo_ready, 1)
            for b in range(BATCH):
                for i in range(TPB):
                    pe.wait_ge(xn_ready, TPB * b + i + 1)
                    if b:
                        pe.wait_ge(gt_lo_ready, TPB * (b - 1) + i + 1)
                    for k in range(KD):
                        ins = pe.transpose(psum[:, i, P * k:P * k + P], rows[:, b % 2, i, P * k:P * k + P], ident[:])
                    ins.then_inc(xn_turned, 1)
                if b:
                    turn_logits(b - 1)
                pe.wait_ge(gt_lo_ready, TPB * (b + 1))
                for k in range(KD):
                    ins = three(psum[0:EXPERTS, LOGIT_T_BANKS[b % 2], :], (g_hi[:, k], g_lo[:, k]),
                                (gt_hi[:, k], gt_lo[:, k]), k == 0, k == KD - 1)
                ins.then_inc(logits_made, 1)
            turn_logits(BATCH - 1)

            pe.wait_ge(sums_ready, 2)
            pe.wait_ge(chosen_ready, 2)
            flags = chosen[:].rearrange("p t e -> p (t e)")
            n = TILES * EXPERTS
            pe.matmul(psum[:, PLACE_BANK, 0:n], above_r[:], flags, start=True, stop=False, skip_group_check=True)
            for t in range(1, TILES):
                ins = pe.matmul(psum[:, PLACE_BANK, EXPERTS * t:n], ones_r[:], flags[:, 0:n - EXPERTS * t],
                                start=False, stop=t == TILES - 1, skip_group_check=True)
            ins.then_inc(place_made, 1)
            pe.wait_ge(chosen_ready, 3)
            pe.matmul(psum[:, COUNT_BANK, 0:ROUTED], ones[:], per_expert[:], start=True, stop=True)\
              .then_inc(counted, 1)

            def turn_x(s):
                pe.wait_ge(xs_loaded, s * 16 + 16)
                for k in range(KD):
                    ins = pe.transpose(psum[:, X_BANK, P * k:P * k + P], xs[:, P * k:P * k + P], ident[:])
                ins.then_inc(x_turned, 1)

            def step(s, now, before, kind):
                if now is not None:
                    n = turn_at(pe, s, now)
                    pe.wait_ge(xt_lo_ready, s + 1)
                    pe.wait_ge(w_lo_ready, n * 3 + 2)
                    for m, bank in ((0, UP_BANK), (1, GATE_BANK)):
                        for k in range(KD):
                            ins = three(psum[:, bank, :], (xt_hi[:, k], xt_lo[:, k]),
                                        (block_of(w_hi, n, m, k), block_of(w_lo, n, m, k)), k == 0, k == KD - 1)
                        ins.then_inc(up_made, 1)
                    if has_next(s):
                        turn_x(s + 1)
                if before is not None:
                    n = turn_at(pe, s - 1, before)
                    pe.wait_ge(ht_lo_ready, s)
                    pe.wait_ge(w_lo_ready, n * 3 + 3)
                    for k in range(KD):
                        ins = three(psum[:, OUT_BANK, :], (ht_hi[:, k], ht_lo[:, k]),
                                    (block_of(w_hi, n, 2, k), block_of(w_lo, n, 2, k)), k == 0, k == KD - 1)
                    ins.then_inc(out_made, 1)
                if now is not None:
                    pe.wait_ge(product_ready, s + 1)
                    for k in range(KD):
                        ins = pe.transpose(psum[:, H_BANK, P * k:P * k + P], product[:, P * k:P * k + P], ident[:])
                    ins.then_inc(h_turned, 1)

            pe.wait_ge(gt_lo_ready, TILES)
            turn_x(0)
            pe.wait_ge(turns_ready, 2)
            steps(pe, step)



def program(nc, x, a_wq, a_wk, a_wv, a_wo, a_mask, b_fc, b_proj, c_wqa, c_wkr, c_gain, c_cos, c_sin, c_heads,
            c_causal, c_rotation, d_weights, d_gate_w, d_gate_b, d_select_b, d_constants, identity, out):
    with ExitStack() as ctx:
        x_res = ctx.enter_context(nc.sbuf_tensor("x_res", [P, TILES, D], F32))
        ident = ctx.enter_context(nc.sbuf_tensor("ident", [P, P], F32))
        x_loaded = ctx.enter_context(nc.semaphore("x_loaded"))
        stored = ctx.enter_context(nc.semaphore("stored"))
        zeroed = ctx.enter_context(nc.semaphore("zeroed"))
        slots_cleared = ctx.enter_context(nc.semaphore("slots_cleared"))
        slot_in = nc.dram_tensor("slot_in", [SLOTS * P, D], F32).ap()
        slot_out = nc.dram_tensor("slot_out", [ROUTED_SLOTS * P, D], F32).ap()
        early = ctx.enter_context(ExitStack())
        zeros = early.enter_context(nc.sbuf_tensor("zeros", [P, D], F32))
        with nc.Block() as block:

            @block.gpsimd
            def _(pool):
                pool.memset(zeros[:], 0.0).then_inc(zeroed, 1)

            @block.sync
            def _(sp):
                for b in range(BATCH):
                    sp.dma_start(x_res[:, TPB * b:TPB * b + TPB, :], x[b].rearrange("(t p) n -> p t n", p=P))\
                      .then_inc(x_loaded, 16)
                sp.dma_start(ident[:], identity).then_inc(x_loaded, 16)
                sp.wait_ge(zeroed, 1)
                sp.wait_ge(x_loaded, 16 * (BATCH + 1))

        each = ROUTED_SLOTS // BATCH

        def clear_slots(sp, b):
            n = each if not isinstance(b, int) else ROUTED_SLOTS - BATCH * each
            rows = slot_in[bass.ds(b * (each * P) + HALF * P, n * P), :].rearrange("(t p) n -> p t n", p=P)
            sp.dma_start(rows, zeros[:].unsqueeze(1).broadcast_to([P, n, D])).then_inc(slots_cleared, 16)

        window_attention(nc, x_res, ident, a_wq, a_wk, a_wv, a_wo, a_mask, clear_slots)
        ternary_mlp(nc, x_res, ident, b_fc, b_proj)
        with nc.Block() as block:

            @block.sync
            def _(sp):
                sp.wait_ge(slots_cleared, 16 * (BATCH + 1))

        early.close()
        with ExitStack() as latents:
            lat_hi = latents.enter_context(nc.sbuf_tensor("lat_hi", [P, SLABS, TOKENS], F32R))
            lat_lo = latents.enter_context(nc.sbuf_tensor("lat_lo", [P, SLABS, TOKENS], F32R))
            v_hi = latents.enter_context(nc.sbuf_tensor("v_hi", [P, TILES, P], F32R))
            v_lo = latents.enter_context(nc.sbuf_tensor("v_lo", [P, TILES, P], F32R))
            latent_projections(nc, x_res, ident, lat_hi, lat_lo, v_hi, v_lo, c_wqa, c_wkr, c_gain, c_cos, c_sin)
            latent_attention(nc, x_res, ident, lat_hi, lat_lo, v_hi, v_lo, c_heads, c_causal, c_rotation)
        mixture_of_experts(nc, x_res, ident, d_weights, d_gate_w, d_gate_b, d_select_b, d_constants, slot_in, slot_out)
        with nc.Block() as block:

            @block.sync
            def _(sp):
                for b in range(BATCH):
                    sp.dma_start(out[b].rearrange("(t p) n -> p t n", p=P), x_res[:, TPB * b:TPB * b + TPB, :])\
                      .then_inc(stored, 16)
                sp.wait_ge(stored, 16 * BATCH)



def window_mask():
    i, j = np.arange(SEQ)[:, None], np.arange(SEQ)[None, :]
    seen = ((j <= i) & (j >= i - 255)) | (j < 4)
    seen &= (i >= 4) | (j <= i)
    m = np.where(seen, 0.0, MASKED).astype(np.float32)
    return np.concatenate([m[P * t:P * t + P, :P * (t + 1)] for t in range(TPB)], axis=1)


def rotary():
    freq = (np.float32(1.0) / np.float32(10000.0) ** (np.arange(0, ROPE, 2, dtype=np.float32) / np.float32(ROPE)))
    angle = np.outer(np.arange(SEQ, dtype=np.float32), freq.astype(np.float32)).astype(np.float32)
    c, s = np.cos(angle), np.sin(angle)
    return np.concatenate([c, c], axis=1), np.concatenate([-s, s], axis=1)


def slot_constants():
    c = np.zeros((P, K_COLS), np.float32)
    c[:, K_BEFORE:K_BEFORE + P] = np.arange(P)[:, None] < np.arange(P)[None, :]
    e = np.arange(ROUTED)
    c[:, K_EARLIER:K_EARLIER + RANKS] = (e[None, :] < e[:, None]).reshape(-1)
    c[:, K_FILLS:K_FILLS + TILES] = P * np.arange(TILES)
    c[:, K_SLOT:K_SLOT + SLOTS] = np.arange(SLOTS)
    return c


def head_weights(wq_b, wkv_b, wo):
    wq = wq_b.reshape(Q_LORA, L_HEADS, NOPE + ROPE)
    wkv = wkv_b.reshape(KV_LORA, L_HEADS, NOPE + D_V)
    half = NOPE + ROPE // 2
    wr = np.concatenate([wq[:, :, NOPE:], wq[:, :, half:], wq[:, :, NOPE:half]], axis=2)
    wr = wr.reshape(KQ, P, L_HEADS, P).transpose(2, 1, 0, 3).reshape(L_HEADS, P, KQ * P)
    return np.concatenate([wq[:, :, :NOPE].transpose(1, 2, 0), wkv[:, :, :NOPE].transpose(1, 2, 0), wr,
                           wkv[:, :, NOPE:].transpose(1, 2, 0), wo.reshape(L_HEADS, D_V, D)], axis=2)


def kernel(**inputs):
    import numpy as _np
    import concourse.bacc as _bacc
    from concourse.bass_utils import run_bass_kernel_spmd as _run

    a = {name: _np.asarray(value) for name, value in inputs.items()}
    cos, sin = rotary()
    wq = a["L0_attn_Wq"].T.reshape(D, GROUPS, PER_GROUP, HS).transpose(0, 2, 1, 3).reshape(D, D)
    tri = _np.where(_np.arange(P)[None, :] <= _np.arange(P)[:, None], 0.0, MASKED)
    experts = _np.stack([_np.concatenate([a["L1_ffn_" + s][None], a["L1_ffn_" + r], a["L1_ffn_" + s][None]])
                         for r, s in (("W1", "Ws1"), ("Wg", "Wsg"), ("W2", "Ws2"))], axis=1)
    arrays = {
        "x": a["L0_attn_x"],
        "a_wq": wq, "a_wk": a["L0_attn_Wk"].T, "a_wv": a["L0_attn_Wv"].T, "a_wo": a["L0_attn_Wo"].T,
        "a_mask": window_mask(),
        "b_fc": a["L0_ffn_w_fc"].T, "b_proj": a["L0_ffn_w_proj"].T,
        "c_wqa": a["L1_attn_Wq_a"],
        "c_wkr": _np.concatenate([a["L1_attn_Wkv_a"], a["L1_attn_Wk_rope"]], axis=1),
        "c_gain": _np.broadcast_to(_np.concatenate([a["L1_attn_q_norm_w"], a["L1_attn_kv_norm_w"]]),
                                   (P, Q_LORA + KV_LORA)),
        "c_cos": cos.reshape(TPB, P, ROPE).transpose(1, 0, 2), "c_sin": sin.reshape(TPB, P, ROPE).transpose(1, 0, 2),
        "c_heads": head_weights(a["L1_attn_Wq_b"], a["L1_attn_Wkv_b"], a["L1_attn_Wo"]),
        "c_causal": _np.concatenate([_np.zeros((P, SEQ - P)), tri], axis=1).astype(_np.float32),
        "c_rotation": _np.concatenate([cos.T, sin.T], axis=0),
        "d_weights": experts,
        "d_gate_w": _np.concatenate([a["L1_ffn_gate_w"], _np.zeros((D, 1), _np.float32)], axis=1),
        "d_gate_b": _np.concatenate([a["L1_ffn_gate_b"], _np.zeros(1, _np.float32)])[:, None],
        "d_select_b": _np.broadcast_to(a["L1_ffn_biases"], (P, ROUTED)),
        "d_constants": slot_constants(),
        "identity": _np.eye(P, dtype=_np.float32),
    }
    arrays = {name + "_dram": _np.ascontiguousarray(value) for name, value in arrays.items()}
    nc = _bacc.Bacc("TRN2", target_bir_lowering=False, num_devices=1)
    args = [nc.dram_tensor(name, value.shape, mybir.dt.from_np(value.dtype), kind="ExternalInput").ap()
            for name, value in arrays.items()]
    args.append(nc.dram_tensor("out_dram", [BATCH, SEQ, D], F32, kind="ExternalOutput").ap())
    program(nc, *args)
    return _run(nc, [arrays], core_ids=[0]).results[0]["out_dram"]
```

```python
from contextlib import ExitStack, contextmanager

import concourse.bass as bass
import numpy as np
from concourse import mybir

F32 = mybir.dt.float32
F32R = mybir.dt.float32r
ALU = mybir.AluOpType
ACT = mybir.ActivationFunctionType
AX = mybir.AxisListType

P = 128
D = 512
KD = D // P
BATCH, SEQ = 4, 512
TILES = BATCH * SEQ // P
TPB = SEQ // P
MASKED = -1.0e30

LN_EPS = 1e-5


class Tally:

    def __init__(self, sem, base=0):
        self.sem, self.base, self.n = sem, base, 0

    def inc(self, instruction, by=1):
        instruction.then_inc(self.sem, by)
        self.n += by

    def wait(self, engine, n=None):
        engine.wait_ge(self.sem, self.base + (self.n if n is None else n))


def row(x_res, t):
    return x_res[:, bass.ds(t, 1), :].rearrange("p a n -> p (a n)")


def wait_apart(engine, sem, value):
    engine.wait_ge(sem, value)
    engine.nop(nofuse=True)


@contextmanager
def semaphores(nc):
    handles = []

    def make(name):
        handles.append(nc.alloc_semaphore(name=name))
        return handles[-1]

    yield make
    with nc.Block() as block:

        @block.sync
        def _(sp):
            for handle in handles:
                sp.sem_clear(handle)
    for handle in handles:
        nc.release_semaphore(handle)



HEADS, GROUPS, HS = 16, 4, 32
PER_GROUP = HEADS // GROUPS
SCORE_OFFSET = [0, 128, 384, 768]
SCORE_COLS = 1280
SCORE_PLACE = [(0, 0), (1, 0), (0, 128), (2, 0)]
PT_PLACE = [(3, 0), (4, 0), (5, 0), (4, 384)]
PT_OFFSET = [0, 512, 1024, 896]


def window_attention(nc, x_res, ident, x, identity, wq, wk, wv, wo, mask_dram, next_weights, piece_sum, clear):
    with ExitStack() as ctx:
        def sb(name, shape, dt=F32):
            return ctx.enter_context(nc.sbuf_tensor(name, shape, dt))

        sem = ctx.enter_context(semaphores(nc))

        psum = ctx.enter_context(nc.psum_tensor("a_psum", [P, 8, 512], F32))
        w_hi = sb("a_w_hi", [P, KD, 1280], F32R)
        w_lo = sb("a_w_lo", [P, KD, 1280], F32R)
        WQ, WK, WV, WO = 0, 512, 640, 768
        mask = sb("a_mask", [P, SCORE_COLS])
        stats = sb("a_stats", [P, TPB, 6])
        meanvar = sb("a_meanvar", [P, TPB, 2])
        ve = sb("a_ve", [P, TPB])
        minus_half = sb("a_minus_half", [P, TPB])
        rstd = sb("a_rstd", [P, TPB])
        xt_hi = sb("a_xt_hi", [P, KD, SEQ], F32R)
        xt_lo = sb("a_xt_lo", [P, KD, SEQ], F32R)
        qk_hi = sb("a_qk_hi", [P, 5, SEQ], F32R)
        qk_lo = sb("a_qk_lo", [P, 5, SEQ], F32R)
        q_stack = sb("a_q_stack", [3 * HS, GROUPS, PER_GROUP, SEQ], F32R)
        k_stack = sb("a_k_stack", [3 * HS, GROUPS, SEQ], F32R)
        v_pad = sb("a_v_pad", [P, TPB, GROUPS, 3 * HS + HS + 3 * HS])
        masked = sb("a_masked", [P, 2, SCORE_COLS])
        probs = sb("a_probs", [P, 2, SCORE_COLS])
        probs_t = sb("a_probs_t", [P, 2, SCORE_COLS])
        w_raw = masked
        xn = sb("a_xn", [P, TPB, D])
        flat_xn = xn[:, :, :].rearrange("p t n -> p (t n)")
        low = sb("a_low", [P, 2, TPB])
        rowsum = sb("a_rowsum", [P, 2, TPB])
        rinv = sb("a_rinv", [P, 2, TPB])
        y_hi, y_lo = xt_hi, xt_lo

        x_first_loaded = sem("a_x_first_loaded")
        x_rest_loaded = sem("a_x_rest_loaded")
        piece_loaded = sem("a_piece_loaded")
        piece_summed = sem("a_piece_summed")
        loaded = [sem(f"a_loaded{k}") for k in range(KD)]
        mask_loaded = sem("a_mask_loaded")
        weights_hi = sem("a_weights_hi")
        weights_lo = sem("a_weights_lo")
        v_zeroed = sem("a_v_zeroed")
        const_ready = sem("a_const_ready")
        stat_ready = sem("a_stat_ready")
        var_ready = sem("a_var_ready")
        ve_ready = sem("a_ve_ready")
        rstd_ready = sem("a_rstd_ready")
        xn_ready = sem("a_xn_ready")
        xn_turned = sem("a_xn_turned")
        xt_hi_ready = sem("a_xt_hi_ready")
        xt_lo_ready = sem("a_xt_lo_ready")
        projected = sem("a_projected")
        qk_hi_ready = sem("a_qk_hi_ready")
        qk_lo_ready = sem("a_qk_lo_ready")
        v_ready = sem("a_v_ready")
        k_stacked = sem("a_k_stacked")
        q_stacked = [sem(f"a_q_stacked{g}") for g in range(GROUPS)]
        scores_ready = sem("a_scores_ready")
        masked_ready = sem("a_masked_ready")
        exp_ready = sem("a_exp_ready")
        rinv_ready = sem("a_rinv_ready")
        probs_ready = sem("a_probs_ready")
        turned = sem("a_turned")
        pt_act = sem("a_pt_act")
        pt_dve = sem("a_pt_dve")
        mixed = sem("a_mixed")
        y_hi_ready = sem("a_y_hi_ready")
        y_lo_ready = sem("a_y_lo_ready")
        out_ready = sem("a_out_ready")
        added = sem("a_added")

        QK_BANKS = (4, 5, 0, 1, 2)
        V_BANKS = (7, 7, 6, 6)
        PRODUCTS = 5 + TPB

        def batches(engine, batch):
            with engine.Fori(0, BATCH - 1) as b:
                batch(b, True)
            batch(BATCH - 1, False)

        block = ctx.enter_context(nc.Block())

        @block.sync
        def _(sp):
            sp.dma_start(x_res[:, 0:TPB, :], x[0].rearrange("(t p) n -> p t n", p=P)).then_inc(x_first_loaded, 16)
            sp.dma_start(ident[:], identity).then_inc(x_first_loaded, 16)
            for k in range(KD):
                if k >= 2:
                    sp.wait_ge(weights_lo, k - 1)
                rows = slice(P * k, P * k + P)
                for w, lo, hi in ((wq, WQ, WK), (wk, WK, WV), (wv, WV, WO), (wo, WO, WO + D)):
                    sp.dma_start(w_raw[:, k % 2, lo:hi], w[rows, :]).then_inc(loaded[k], 16)
            sp.dma_start(mask[:], mask_dram).then_inc(mask_loaded, 16)
            sp.dma_start(x_res[:, TPB:TILES, :], x[1:BATCH].rearrange("b (t p) n -> p (b t) n", p=P))\
              .then_inc(x_rest_loaded, 16)
            with sp.Fori(0, BATCH) as b:
                sp.wait_ge(qk_hi_ready, b * 5 + 1)
                sp.wait_ge(qk_lo_ready, b * 5 + 1)
                for g in range(GROUPS):
                    rows = slice(HS * g, HS * g + HS)
                    for c, part in enumerate((qk_hi, qk_lo, qk_hi)):
                        sp.dma_start(k_stack[HS * c:HS * c + HS, g, :].bitcast(F32), part[rows, 4, :].bitcast(F32))\
                          .then_inc(k_stacked, 16)
                sp.wait_ge(qk_hi_ready, b * 5 + 5)
                sp.wait_ge(qk_lo_ready, b * 5 + 5)
                for g in range(GROUPS):
                    rows = slice(HS * g, HS * g + HS)
                    for c, part in enumerate((qk_hi, qk_hi, qk_lo)):
                        sp.dma_start(q_stack[HS * c:HS * c + HS, g, :, :].bitcast(F32),
                                     part[rows, 0:4, :].bitcast(F32)).then_inc(q_stacked[g], 16)
                for j in range(2):
                    if j:
                        sp.wait_ge(piece_summed, b * 2 + 1)
                    sp.dma_start(flat_xn, next_weights[bass.ds(b * 2 + j, 1)].rearrange("a p n -> p (a n)"))\
                      .then_inc(piece_loaded, 16)
                clear(sp, b)
            clear(sp, BATCH)

        @block.gpsimd
        def _(pool):
            pool.memset(minus_half[:], -0.5).then_inc(const_ready, 1)
            pool.memset(v_pad[:], 0.0).then_inc(v_zeroed, 1)
            pool.wait_ge(const_ready, 1)
            with pool.Fori(0, BATCH) as b:
                wait_apart(pool, var_ready, b * TPB + TPB)
                pool.tensor_scalar(ve[:], meanvar[:, :, 1], LN_EPS, None, ALU.add).then_inc(ve_ready, 1)
                pool.wait_ge(ve_ready, b + 1)
                pool.tensor_tensor(rstd[:], ve[:], minus_half[:], ALU.pow).then_inc(rstd_ready, 1)

        @block.scalar
        def _(act):
            for k in range(KD):
                act.wait_ge(loaded[k], 16 * 4)
                act.activation(w_hi[:, k, :], w_raw[:, k % 2, :], ACT.Copy).then_inc(weights_hi, 1)
            act.wait_ge(v_zeroed, 1)

            def keep_x(b, first=False):
                for t in range(TPB):
                    act.wait_ge(xn_turned, b * TPB + (t + 1))
                    if not first:
                        act.wait_ge(out_ready, (b - 1) * TPB + (t + 1))
                    act.activation(xt_hi[:, :, P * t:P * t + P], psum[:, t, :].rearrange("p (k n) -> p k n", k=KD),
                                   ACT.Copy).then_inc(xt_hi_ready, 1)

            def batch(b, more):
                for n, (slot, bank) in enumerate(zip((4, 0, 1, 2, 3), QK_BANKS)):
                    act.wait_ge(projected, b * PRODUCTS + (n + 1))
                    act.activation(qk_hi[:, slot, :], psum[:, bank, :], ACT.Copy).then_inc(qk_hi_ready, 1)

                def keep_v(tiles):
                    act.wait_ge(projected, b * PRODUCTS + (5 + tiles[-1] + 1))
                    for t in tiles:
                        act.activation(v_pad[:, t, :, 3 * HS:4 * HS],
                                       psum[:, V_BANKS[t], P * t:P * t + P].rearrange("p (g d) -> p g d", g=GROUPS),
                                       ACT.Copy).then_inc(v_ready, 1)

                keep_v((0, 1))

                def keep_pt(h):
                    act.wait_ge(turned, b * HEADS + h + 1)
                    if h >= 2:
                        act.wait_ge(mixed, b * HEADS + h - 1)
                    act.activation(probs_t[:, h % 2, 0:512], psum[:, 3, :], ACT.Copy).then_inc(pt_act, 1)
                    act.activation(probs_t[:, h % 2, 1024:1280], psum[:, 5, 0:256], ACT.Copy).then_inc(pt_act, 1)

                def keep_y(g):
                    act.wait_ge(mixed, b * HEADS + PER_GROUP * (g + 1))
                    act.activation(y_hi[:, g, :], psum[:, 6 + g % 2, :], ACT.Copy).then_inc(y_hi_ready, 1)

                for s in range(HEADS + 4):
                    if 0 <= s - 2 < HEADS:
                        keep_pt(s - 2)
                    if s < HEADS:
                        if s >= 2:
                            act.wait_ge(turned, b * HEADS + s - 1)
                        for i in range(TPB):
                            act.wait_ge(masked_ready, (b * HEADS + s) * TPB + i + 1)
                            o, n = SCORE_OFFSET[i], P * (i + 1)
                            act.activation(probs[:, s % 2, o:o + n], masked[:, s % 2, o:o + n], ACT.Exp,
                                           bias=low[:, s % 2, i:i + 1], scale=-1.0,
                                           accum_out=rowsum[:, s % 2, i:i + 1]).then_inc(exp_ready, 1)
                    if s == 1:
                        keep_v((2, 3))
                    if s in (6, 12):
                        n = (6, 12).index(s)
                        act.wait_ge(piece_loaded, b * 32 + 16 * (n + 1))
                        act.activation(flat_xn, flat_xn, ACT.Abs, accum_out=piece_sum[:, bass.ds(b * 2 + n, 1)])\
                           .then_inc(piece_summed, 1)
                    if s >= PER_GROUP + 3 and (s - 3) % PER_GROUP == 0:
                        keep_y((s - 3) // PER_GROUP - 1)
                if more:
                    keep_x(b + 1)

            keep_x(0, True)
            batches(act, batch)

        @block.vector
        def _(dve):

            def statistics(b):
                for t in range(TPB):
                    dve.bn_stats(stats[:, t, :], row(x_res, b * TPB + t)).then_inc(stat_ready, 1)
                wait_apart(dve, stat_ready, b * TPB + TPB)
                for t in range(TPB):
                    dve.bn_aggr(meanvar[:, t, :], stats[:, t, :]).then_inc(var_ready, 1)

            def normalise_x(b):
                dve.wait_ge(rstd_ready, b + 1)
                if not (isinstance(b, int) and b == 0):
                    dve.wait_ge(piece_summed, b * 2)
                for t in range(TPB):
                    dve.tensor_scalar(xn[:, t, :], row(x_res, b * TPB + t), meanvar[:, t, 0:1], rstd[:, t:t + 1],
                                      ALU.subtract, ALU.mult).then_inc(xn_ready, 1)

            def keep_x_low(b, t):
                dve.wait_ge(xt_hi_ready, b * TPB + (t + 1))
                cols = slice(P * t, P * t + P)
                dve.tensor_tensor(xt_lo[:, :, cols], psum[:, t, :].rearrange("p (k n) -> p k n", k=KD),
                                  xt_hi[:, :, cols].bitcast(F32), ALU.subtract).then_inc(xt_lo_ready, 1)

            def batch(b, more):
                for n, (slot, bank) in enumerate(zip((4, 0, 1, 2, 3), QK_BANKS)):
                    dve.wait_ge(qk_hi_ready, b * 5 + (n + 1))
                    dve.tensor_tensor(qk_lo[:, slot, :], psum[:, bank, :], qk_hi[:, slot, :].bitcast(F32),
                                      ALU.subtract).then_inc(qk_lo_ready, 1)

                def mask_scores(h):
                    if h >= 2:
                        dve.wait_ge(exp_ready, (b * HEADS + h - 1) * TPB)
                    for i in range(TPB):
                        wait_apart(dve, scores_ready, (b * HEADS + h) * TPB + (3, 2, 3, 4)[i])
                        bank, c = SCORE_PLACE[i]
                        o, n = SCORE_OFFSET[i], P * (i + 1)
                        dve.tensor_tensor_reduce(masked[:, h % 2, o:o + n], psum[:, bank, c:c + n], mask[:, o:o + n],
                                                 -(HS ** -0.5), -MASKED, ALU.add, ALU.min,
                                                 low[:, h % 2, i:i + 1]).then_inc(masked_ready, 1)

                def normalise(h):
                    dve.wait_ge(exp_ready, (b * HEADS + h + 1) * TPB)
                    dve.reciprocal(rinv[:, h % 2, :], rowsum[:, h % 2, :]).then_inc(rinv_ready, 1)
                    dve.wait_ge(rinv_ready, b * HEADS + (h + 1))
                    for i in range(TPB):
                        o, n = SCORE_OFFSET[i], P * (i + 1)
                        dve.tensor_scalar(probs[:, h % 2, o:o + n], probs[:, h % 2, o:o + n],
                                          rinv[:, h % 2, i:i + 1], None, ALU.mult).then_inc(probs_ready, 1)

                def keep_pt(h):
                    dve.wait_ge(turned, b * HEADS + h + 1)
                    if h >= 2:
                        dve.wait_ge(mixed, b * HEADS + h - 1)
                    dve.tensor_copy(probs_t[:, h % 2, 512:1024], psum[:, 4, :]).then_inc(pt_dve, 1)

                def keep_y(g):
                    dve.wait_ge(y_hi_ready, b * GROUPS + g + 1)
                    dve.tensor_tensor(y_lo[:, g, :], psum[:, 6 + g % 2, :], y_hi[:, g, :].bitcast(F32),
                                      ALU.subtract).then_inc(y_lo_ready, 1)

                for s in range(HEADS + 4):
                    if s < HEADS:
                        mask_scores(s)
                    if 0 <= s - 1 < HEADS:
                        normalise(s - 1)
                    if 0 <= s - 2 < HEADS:
                        keep_pt(s - 2)
                    if s >= PER_GROUP + 3 and (s - 3) % PER_GROUP == 0:
                        keep_y((s - 3) // PER_GROUP - 1)
                    if more and s == HEADS:
                        statistics(b + 1)
                    if more and s == HEADS + 1:
                        normalise_x(b + 1)
                for t in range(TPB):
                    dve.wait_ge(out_ready, b * TPB + (t + 1))
                    tile = row(x_res, b * TPB + t)
                    dve.tensor_tensor(tile, psum[:, 4 + t, :], tile, ALU.add).then_inc(added, 1)
                    if more:
                        keep_x_low(b + 1, t)

            dve.wait_ge(x_first_loaded, 32)
            statistics(0)
            normalise_x(0)
            for k in range(KD):
                dve.wait_ge(weights_hi, k + 1)
                dve.tensor_tensor(w_lo[:, k, :], w_raw[:, k % 2, :], w_hi[:, k, :].bitcast(F32), ALU.subtract)\
                   .then_inc(weights_lo, 1)
            for t in range(TPB):
                keep_x_low(0, t)
            dve.wait_ge(mask_loaded, 16)
            dve.wait_ge(x_rest_loaded, 16)
            batches(dve, batch)
            dve.wait_ge(added, TILES)

        @block.tensor
        def _(pe):

            def product(out, lhs_hi, lhs_lo, rhs_hi, rhs_lo, chunks):
                n = 3 * len(chunks)
                for j in range(n):
                    k, (a, c) = chunks[j // 3], ((lhs_hi, rhs_hi), (lhs_hi, rhs_lo), (lhs_lo, rhs_hi))[j % 3]
                    ins = pe.matmul(out, a(k), c(k), start=j == 0, stop=j == n - 1)
                return ins

            def w(part, lo, n):
                return lambda k: part[:, k, lo:lo + n]

            def xt(part, lo=0, n=SEQ):
                return lambda k: part[:, k, lo:lo + n]

            def turn_x(b):
                for t in range(TPB):
                    pe.wait_ge(xn_ready, b * TPB + (t + 1))
                    for k in range(KD):
                        ins = pe.transpose(psum[:, t, P * k:P * k + P], xn[:, t, P * k:P * k + P], ident[:])
                    ins.then_inc(xn_turned, 1)

            def batch(b, more):
                pe.wait_ge(xt_lo_ready, b * TPB + TPB)
                product(psum[:, QK_BANKS[0], :], w(w_hi, WK, P), w(w_lo, WK, P), xt(xt_hi), xt(xt_lo), range(KD))\
                    .then_inc(projected, 1)
                for s, bank in enumerate(QK_BANKS[1:]):
                    product(psum[:, bank, :], w(w_hi, WQ + P * s, P), w(w_lo, WQ + P * s, P), xt(xt_hi), xt(xt_lo),
                            range(KD)).then_inc(projected, 1)

                def values(t):
                    product(psum[:, V_BANKS[t], P * t:P * t + P], xt(xt_hi, P * t, P), xt(xt_lo, P * t, P),
                            w(w_hi, WV, P), w(w_lo, WV, P), range(KD)).then_inc(projected, 1)

                values(0)
                values(1)

                def scores(h):
                    g, j = divmod(h, PER_GROUP)
                    if h == 0:
                        pe.wait_ge(k_stacked, b * (GROUPS * 48) + GROUPS * 48)
                    else:
                        pe.wait_ge(masked_ready, (b * HEADS + h) * TPB)
                    if j == 0:
                        pe.wait_ge(q_stacked[g], b * 48 + 48)
                    for i in range(TPB):
                        bank, c = SCORE_PLACE[i]
                        pe.matmul(psum[:, bank, c:c + P * (i + 1)], q_stack[:, g, j, P * i:P * i + P],
                                  k_stack[:, g, 0:P * (i + 1)], start=True, stop=True).then_inc(scores_ready, 1)

                def turn(h):
                    pe.wait_ge(probs_ready, (b * HEADS + h + 1) * TPB)
                    if h >= 1:
                        pe.wait_ge(pt_act, (b * HEADS + h) * 2)
                        pe.wait_ge(pt_dve, b * HEADS + h)
                    for j in range(TPB):
                        bank, c = PT_PLACE[j]
                        for i in range(j, TPB):
                            o = SCORE_OFFSET[i] + P * j
                            ins = pe.transpose(psum[:, bank, c + P * (i - j):c + P * (i - j + 1)],
                                               probs[:, h % 2, o:o + P], ident[:])
                    ins.then_inc(turned, 1)

                def mix(h):
                    g, j = divmod(h, PER_GROUP)
                    pe.wait_ge(pt_act, (b * HEADS + h + 1) * 2)
                    pe.wait_ge(pt_dve, b * HEADS + h + 1)
                    if h == 0:
                        pe.wait_ge(v_ready, b * TPB + TPB)
                    if j == 0 and g >= 2:
                        pe.wait_ge(y_lo_ready, b * GROUPS + g - 1)
                    first = 3 * HS - HS * j
                    for kt in range(TPB):
                        o = PT_OFFSET[kt]
                        ins = pe.matmul(psum[:, 6 + g % 2, P * kt:SEQ], v_pad[:, kt, g, first:first + P],
                                        probs_t[:, h % 2, o:o + SEQ - P * kt], start=j == 0 and kt == 0,
                                        stop=j == PER_GROUP - 1 and kt == TPB - 1, skip_group_check=True)
                    ins.then_inc(mixed, 1)

                for s in range(HEADS + 3):
                    if s < HEADS:
                        scores(s)
                    if s < 2:
                        values(2 + s)
                    if 0 <= s - 2 < HEADS:
                        turn(s - 2)
                    if 0 <= s - 3 < HEADS:
                        mix(s - 3)
                if more:
                    turn_x(b + 1)
                pe.wait_ge(y_lo_ready, b * GROUPS + GROUPS)
                for t in range(TPB):
                    product(psum[:, 4 + t, :], lambda k: y_hi[:, k, P * t:P * t + P],
                            lambda k: y_lo[:, k, P * t:P * t + P], w(w_hi, WO, D), w(w_lo, WO, D), range(GROUPS))\
                        .then_inc(out_ready, 1)

            pe.wait_ge(x_first_loaded, 32)
            turn_x(0)
            pe.wait_ge(weights_lo, KD)
            batches(pe, batch)



FF = 4 * D
KF = FF // P
PIECES = 4
Q_MAX = 128.0
BIT_EPS = 1e-6


def tiles_in_steps(engine, step):
    step(0, 0, True, False)
    step(1, 1, False, False)
    with engine.Fori(0, (TILES - 4) // 2) as j:
        for u in range(2):
            step(j * 2 + (2 + u), u, False, False)
    step(TILES - 2, 0, False, False)
    step(TILES - 1, 1, False, False)
    step(TILES, TILES % 2, False, True)


def ternary_mlp(nc, x_res, ident, weights, piece_sum):
    with ExitStack() as ctx:
        def sb(name, shape, dt=F32):
            return ctx.enter_context(nc.sbuf_tensor(name, shape, dt))

        sem = ctx.enter_context(semaphores(nc))

        psum = ctx.enter_context(nc.psum_tensor("b_psum", [P, 8, 512], F32))
        FC, PROJ = 0, 1
        TURN_X_BANK, OUT_BANK = 6, 7

        raw = sb("b_raw", [P, PIECES, FF])
        negative = sb("b_negative", [P, FF])
        tern = [sb("b_tern_fc", [P, PIECES, FF], F32R), sb("b_tern_proj", [P, PIECES, FF], F32R)]
        row_sum = sb("b_row_sum", [P, 2])
        ones = sb("b_ones", [P, P])
        gamma = sb("b_gamma", [P, 2])
        above = sb("b_above", [P, 2])
        below = sb("b_below", [P, 2])
        minus_half = sb("b_minus_half", [P, 1])
        x_stats = sb("b_x_stats", [P, 2, 6])
        x_mv = sb("b_x_mv", [P, 2, 2])
        x_ve = sb("b_x_ve", [P, 2])
        x_rstd = sb("b_x_rstd", [P, 2])
        x_shift = sb("b_x_shift", [P, 2])
        x_max = sb("b_x_max", [P, 2])
        x_inv = sb("b_x_inv", [P, 2])
        x_scale = sb("b_x_scale", [P, 2, 2])
        xn = sb("b_xn", [P, 2, D])
        xq_hi = sb("b_xq_hi", [P, 2, KD, P], F32R)
        xq_lo = sb("b_xq_lo", [P, 2, KD, P], F32R)
        h = sb("b_h", [P, 2, FF])
        h_stats = sb("b_h_stats", [P, 2, 4, 6])
        h_mv = sb("b_h_mv", [P, 2, 2])
        h_ve = sb("b_h_ve", [P, 2])
        h_rstd = sb("b_h_rstd", [P, 2])
        h_shift = sb("b_h_shift", [P, 2])
        h_max = sb("b_h_max", [P, 2])
        h_inv = sb("b_h_inv", [P, 2])
        h_scale = sb("b_h_scale", [P, 2, 2])
        ht_hi = sb("b_ht_hi", [P, KF, P], F32R)
        ht_lo = sb("b_ht_lo", [P, KF, P], F32R)

        loaded = [sem(f"b_loaded{k}") for k in range(PIECES)]
        const_ready = sem("b_const_ready")
        row_summed = sem("b_row_summed")
        total_ready = sem("b_total_ready")
        gamma_ready = sem("b_gamma_ready")
        neg_ready = sem("b_neg_ready")
        tern_ready = [sem("b_tern_fc_ready"), sem("b_tern_proj_ready")]
        x_stat = sem("b_x_stat")
        x_var = sem("b_x_var")
        x_ve_ready = sem("b_x_ve_ready")
        x_rstd_ready = sem("b_x_rstd_ready")
        x_shift_ready = sem("b_x_shift_ready")
        x_norm = sem("b_x_norm")
        x_peak = sem("b_x_peak")
        x_inv_ready = sem("b_x_inv_ready")
        x_scale_ready = sem("b_x_scale_ready")
        x_clip = sem("b_x_clip")
        xq_ready = sem("b_xq_ready")
        x_turned = sem("b_x_turned")
        xq_hi_ready = sem("b_xq_hi_ready")
        xq_lo_ready = sem("b_xq_lo_ready")
        fc_ready = sem("b_fc_ready")
        gelu_ready = sem("b_gelu_ready")
        h_stat = sem("b_h_stat")
        h_var = sem("b_h_var")
        h_ve_ready = sem("b_h_ve_ready")
        h_rstd_ready = sem("b_h_rstd_ready")
        h_shift_ready = sem("b_h_shift_ready")
        h_norm = sem("b_h_norm")
        h_peak = sem("b_h_peak")
        h_inv_ready = sem("b_h_inv_ready")
        h_scale_ready = sem("b_h_scale_ready")
        h_clip = sem("b_h_clip")
        hq_ready = sem("b_hq_ready")
        h_turned = sem("b_h_turned")
        ht_hi_ready = sem("b_ht_hi_ready")
        ht_lo_ready = sem("b_ht_lo_ready")
        proj_ready = sem("b_proj_ready")
        added = sem("b_added")

        block = ctx.enter_context(nc.Block())

        @block.sync
        def _(sp):
            for k in range(PIECES):
                sp.dma_start(raw[:, k, :], weights[k]).then_inc(loaded[k], 16)
            for k in range(PIECES):
                sp.wait_ge(tern_ready[FC], k + 1)
                sp.dma_start(raw[:, k, :], weights[PIECES + k]).then_inc(loaded[k], 16)

        @block.gpsimd
        def _(pool):
            pool.memset(ones[:], 1.0).then_inc(const_ready, 1)
            pool.memset(minus_half[:], -0.5).then_inc(const_ready, 1)
            pool.wait_ge(const_ready, 2)

            def x_deviation(t, par):
                wait_apart(pool, x_var, t + 1)
                pool.tensor_scalar(x_ve[:, par:par + 1], x_mv[:, par, 1:2], 1.0 + BIT_EPS, BIT_EPS * LN_EPS,
                                   ALU.mult, ALU.add).then_inc(x_ve_ready, 1)
                pool.wait_ge(x_ve_ready, t + 1)
                pool.tensor_tensor(x_rstd[:, par:par + 1], x_ve[:, par:par + 1], minus_half[:], ALU.pow)\
                    .then_inc(x_rstd_ready, 1)
                wait_apart(pool, x_rstd_ready, t + 1)
                pool.tensor_scalar(x_shift[:, par:par + 1], x_mv[:, par, 0:1], -1.0, x_rstd[:, par:par + 1],
                                   ALU.mult, ALU.mult).then_inc(x_shift_ready, 1)

            def x_quantise(t, par):
                wait_apart(pool, x_inv_ready, t + 1)
                pool.tensor_scalar(x_scale[:, par, 0:1], x_inv[:, par:par + 1], Q_MAX, None, ALU.mult)\
                    .then_inc(x_scale_ready, 1)
                pool.tensor_scalar(x_scale[:, par, 1:2], x_max[:, par:par + 1], 1.0 / Q_MAX, None, ALU.mult)\
                    .then_inc(x_scale_ready, 1)
                wait_apart(pool, x_scale_ready, 2 * t + 2)
                pool.tensor_scalar(xn[:, par, :], xn[:, par, :], x_scale[:, par, 0:1], Q_MAX, ALU.mult, ALU.min)\
                    .then_inc(x_clip, 1)
                wait_apart(pool, x_clip, t + 1)
                pool.tensor_scalar(xn[:, par, :], xn[:, par, :], -Q_MAX, x_scale[:, par, 1:2], ALU.max, ALU.mult)\
                    .then_inc(xq_ready, 1)

            def h_deviation(t, par):
                wait_apart(pool, h_var, t + 1)
                pool.tensor_scalar(h_ve[:, par:par + 1], h_mv[:, par, 1:2], BIT_EPS, None, ALU.add)\
                    .then_inc(h_ve_ready, 1)
                pool.wait_ge(h_ve_ready, t + 1)
                pool.tensor_tensor(h_rstd[:, par:par + 1], h_ve[:, par:par + 1], minus_half[:], ALU.pow)\
                    .then_inc(h_rstd_ready, 1)
                wait_apart(pool, h_rstd_ready, t + 1)
                pool.tensor_scalar(h_shift[:, par:par + 1], h_mv[:, par, 0:1], -1.0, h_rstd[:, par:par + 1],
                                   ALU.mult, ALU.mult).then_inc(h_shift_ready, 1)

            x_deviation(0, 0)
            x_quantise(0, 0)

            def step(t, par, first, last):
                nxt = None if last or (isinstance(t, int) and t == TILES - 1) else t + 1
                if nxt is not None:
                    x_deviation(nxt, 1 - par)
                    x_quantise(nxt, 1 - par)
                if not last:
                    h_deviation(t, par)

            tiles_in_steps(pool, step)

        @block.scalar
        def _(act):
            def normalise_x(t, par):
                act.wait_ge(x_shift_ready, t + 1)
                act.activation(xn[:, par, :], row(x_res, t), ACT.Identity, bias=x_shift[:, par:par + 1],
                               scale=x_rstd[:, par:par + 1]).then_inc(x_norm, 1)

            def keep_x(t, par):
                act.wait_ge(x_turned, t + 1)
                act.activation(xq_hi[:, par, :, :], psum[:, TURN_X_BANK, :].rearrange("p (k n) -> p k n", k=KD),
                               ACT.Copy).then_inc(xq_hi_ready, 1)

            def gelu(t, par):
                for s in range(4):
                    act.wait_ge(fc_ready, 4 * t + s + 1)
                    act.activation(h[:, par, 512 * s:512 * s + 512], psum[:, s, :], ACT.Gelu,
                                   scale=gamma[:, FC:FC + 1]).then_inc(gelu_ready, 1)

            def normalise_h(t, par):
                act.wait_ge(h_shift_ready, t + 1)
                act.activation(h[:, par, :], h[:, par, :], ACT.Identity, bias=h_shift[:, par:par + 1],
                               scale=h_rstd[:, par:par + 1]).then_inc(h_norm, 1)

            def keep_h(t):
                for s in range(4):
                    act.wait_ge(h_turned, 4 * t + s + 1)
                    act.activation(ht_hi[:, 4 * s:4 * s + 4, :],
                                   psum[:, 4 + s % 2, :].rearrange("p (k n) -> p k n", k=4), ACT.Copy)\
                       .then_inc(ht_hi_ready, 1)

            normalise_x(0, 0)
            keep_x(0, 0)

            def step(t, par, first, last):
                nxt = None if last or (isinstance(t, int) and t == TILES - 1) else t + 1
                if nxt is not None:
                    normalise_x(nxt, 1 - par)
                if not last:
                    gelu(t, par)
                if not first:
                    keep_h(t - 1)
                if first:
                    keep_x(nxt, 1 - par)
                if not last:
                    normalise_h(t, par)
                if nxt is not None and not first:
                    keep_x(nxt, 1 - par)

            act.wait_ge(gamma_ready, 3)
            tiles_in_steps(act, step)

        @block.vector
        def _(dve):
            def thresholds(w):
                dve.tensor_reduce(row_sum[:, w:w + 1], piece_sum[:, PIECES * w:PIECES * w + PIECES], AX.X, ALU.add)\
                   .then_inc(row_summed, 1)
                dve.wait_ge(total_ready, w + 1)
                mean = 1.0 / (D * FF)
                total = psum[:, TURN_X_BANK, 0:1]
                dve.tensor_scalar(gamma[:, w:w + 1], total, mean, None, ALU.mult).then_inc(gamma_ready, 1)
                dve.tensor_scalar(above[:, w:w + 1], total, 0.5 * mean, 0.5 * BIT_EPS, ALU.mult, ALU.add)\
                   .then_inc(gamma_ready, 1)
                dve.tensor_scalar(below[:, w:w + 1], total, -0.5 * mean, -0.5 * BIT_EPS, ALU.mult, ALU.add)\
                   .then_inc(gamma_ready, 1)
                dve.wait_ge(gamma_ready, 3 * (w + 1))

            def ternary(w, pieces):
                for k in pieces:
                    dve.wait_ge(loaded[k], 16 * (w + 1))
                    if k or w:
                        dve.wait_ge(tern_ready[0], k if w == 0 else PIECES)
                    if w and k:
                        dve.wait_ge(tern_ready[1], k)
                    dve.tensor_scalar(negative[:], raw[:, k, :], below[:, w:w + 1], None, ALU.is_lt)\
                       .then_inc(neg_ready, 1)
                    dve.wait_ge(neg_ready, PIECES * w + k + 1)
                    dve.scalar_tensor_tensor(out=tern[w][:, k, :], in0=raw[:, k, :], scalar=above[:, w:w + 1],
                                             in1=negative[:], op0=ALU.is_gt, op1=ALU.subtract)\
                       .then_inc(tern_ready[w], 1)

            def x_variance(t, par):
                dve.bn_stats(x_stats[:, par, :], row(x_res, t)).then_inc(x_stat, 1)
                wait_apart(dve, x_stat, t + 1)
                dve.bn_aggr(x_mv[:, par, :], x_stats[:, par, :]).then_inc(x_var, 1)

            def x_peaks(t, par):
                dve.wait_ge(x_norm, t + 1)
                dve.tensor_reduce(x_max[:, par:par + 1], xn[:, par, :], AX.X, ALU.max, apply_absolute_value=True)\
                   .then_inc(x_peak, 1)
                dve.wait_ge(x_peak, t + 1)
                dve.reciprocal(x_inv[:, par:par + 1], x_max[:, par:par + 1]).then_inc(x_inv_ready, 1)

            def keep_x_low(t, par):
                dve.wait_ge(xq_hi_ready, t + 1)
                dve.tensor_tensor(xq_lo[:, par, :, :], psum[:, TURN_X_BANK, :].rearrange("p (k n) -> p k n", k=KD),
                                  xq_hi[:, par, :, :].bitcast(F32), ALU.subtract).then_inc(xq_lo_ready, 1)

            def h_variance(t, par):
                for s in range(4):
                    dve.wait_ge(gelu_ready, 4 * t + s + 1)
                    dve.bn_stats(h_stats[:, par, s, :], h[:, par, 512 * s:512 * s + 512]).then_inc(h_stat, 1)
                wait_apart(dve, h_stat, 4 * t + 4)
                dve.bn_aggr(h_mv[:, par, :], h_stats[:, par, :, :].rearrange("p s n -> p (s n)")).then_inc(h_var, 1)

            def h_peaks(t, par):
                dve.wait_ge(h_norm, t + 1)
                dve.tensor_reduce(h_max[:, par:par + 1], h[:, par, :], AX.X, ALU.max, apply_absolute_value=True)\
                   .then_inc(h_peak, 1)

            def h_quantise(t, par):
                dve.wait_ge(h_peak, t + 1)
                dve.reciprocal(h_inv[:, par:par + 1], h_max[:, par:par + 1]).then_inc(h_inv_ready, 1)
                dve.wait_ge(h_inv_ready, t + 1)
                dve.tensor_scalar(h_scale[:, par, 0:1], h_inv[:, par:par + 1], Q_MAX, None, ALU.mult)\
                   .then_inc(h_scale_ready, 1)
                dve.tensor_scalar(h_scale[:, par, 1:2], h_max[:, par:par + 1], 1.0 / Q_MAX, None, ALU.mult)\
                   .then_inc(h_scale_ready, 1)
                dve.wait_ge(h_scale_ready, 2 * t + 2)
                dve.tensor_scalar(h[:, par, :], h[:, par, :], h_scale[:, par, 0:1], Q_MAX, ALU.mult, ALU.min)\
                   .then_inc(h_clip, 1)
                dve.wait_ge(h_clip, t + 1)
                dve.tensor_scalar(h[:, par, :], h[:, par, :], -Q_MAX, h_scale[:, par, 1:2], ALU.max, ALU.mult)\
                   .then_inc(hq_ready, 1)

            def keep_h_low(t):
                for s in range(4):
                    dve.wait_ge(ht_hi_ready, 4 * t + s + 1)
                    dve.tensor_tensor(ht_lo[:, 4 * s:4 * s + 4, :],
                                      psum[:, 4 + s % 2, :].rearrange("p (k n) -> p k n", k=4),
                                      ht_hi[:, 4 * s:4 * s + 4, :].bitcast(F32), ALU.subtract)\
                       .then_inc(ht_lo_ready, 1)

            def add(t):
                dve.wait_ge(proj_ready, t + 1)
                dve.scalar_tensor_tensor(out=row(x_res, t), in0=psum[:, OUT_BANK, :], scalar=gamma[:, PROJ:PROJ + 1],
                                         in1=row(x_res, t), op0=ALU.mult, op1=ALU.add).then_inc(added, 1)

            x_variance(0, 0)
            x_peaks(0, 0)
            thresholds(FC)
            thresholds(PROJ)
            ternary(FC, range(PIECES))
            keep_x_low(0, 0)

            def step(t, par, first, last):
                nxt = None if last or (isinstance(t, int) and t == TILES - 1) else t + 1
                other = 1 - par
                if nxt is not None:
                    x_variance(nxt, other)
                if not first:
                    h_peaks(t - 1, other)
                if nxt is not None:
                    x_peaks(nxt, other)
                if first:
                    ternary(PROJ, (0, 1))
                    keep_x_low(nxt, other)
                else:
                    h_quantise(t - 1, other)
                    if not (isinstance(t, int) and t == 1):
                        add(t - 2)
                if not last:
                    h_variance(t, par)
                if not first:
                    keep_h_low(t - 1)
                if first:
                    ternary(PROJ, (2, 3))
                elif nxt is not None:
                    keep_x_low(nxt, other)

            tiles_in_steps(dve, step)
            add(TILES - 1)
            dve.wait_ge(added, TILES)

        @block.tensor
        def _(pe):
            def total(w):
                pe.wait_ge(const_ready, 2)
                pe.wait_ge(row_summed, w + 1)
                pe.matmul(psum[:, TURN_X_BANK, 0:1], ones[:], row_sum[:, w:w + 1], start=True, stop=True)\
                  .then_inc(total_ready, 1)

            def turn_x(t, par):
                pe.wait_ge(xq_ready, t + 1)
                for k in range(KD):
                    ins = pe.transpose(psum[:, TURN_X_BANK, P * k:P * k + P], xn[:, par, P * k:P * k + P], ident[:])
                ins.then_inc(x_turned, 1)

            def fc(t, par, first):
                pe.wait_ge(xq_lo_ready, t + 1)
                for s in range(4):
                    if not first:
                        pe.wait_ge(gelu_ready, 4 * t + s - 3)
                    for k in range(KD):
                        for part in (xq_hi, xq_lo):
                            ins = pe.matmul(psum[:, s, :], part[:, par, k, :], tern[FC][:, k, 512 * s:512 * s + 512],
                                            start=k == 0 and part is xq_hi, stop=k == KD - 1 and part is xq_lo)
                    ins.then_inc(fc_ready, 1)

            def turn_h(t, par):
                pe.wait_ge(hq_ready, t + 1)
                for s in range(4):
                    if s >= 2:
                        pe.wait_ge(ht_lo_ready, 4 * t + s - 1)
                    for k in range(4):
                        c = P * (4 * s + k)
                        ins = pe.transpose(psum[:, 4 + s % 2, P * k:P * k + P], h[:, par, c:c + P], ident[:])
                    ins.then_inc(h_turned, 1)

            def proj(t, chunks):
                w = tern[PROJ][:, :, :].rearrange("p a (k n) -> p (a k) n", n=D)
                for k in chunks:
                    if k % 4 == 0:
                        pe.wait_ge(ht_lo_ready, 4 * t + k // 4 + 1)
                    for part in (ht_hi, ht_lo):
                        ins = pe.matmul(psum[:, OUT_BANK, :], part[:, k, :], w[:, k, :],
                                        start=k == 0 and part is ht_hi, stop=k == KF - 1 and part is ht_lo)
                if chunks[-1] == KF - 1:
                    ins.then_inc(proj_ready, 1)

            total(FC)
            pe.wait_ge(gamma_ready, 3)
            total(PROJ)
            pe.wait_ge(gamma_ready, 6)
            turn_x(0, 0)
            pe.wait_ge(tern_ready[FC], PIECES)

            def step(t, par, first, last):
                nxt = None if last or (isinstance(t, int) and t == TILES - 1) else t + 1
                if not last:
                    fc(t, par, first)
                if not first:
                    turn_h(t - 1, 1 - par)
                    if isinstance(t, int) and t == 1:
                        pe.wait_ge(tern_ready[PROJ], PIECES)
                    else:
                        pe.wait_ge(added, t - 1)
                    proj(t - 1, range(0, KF // 2))
                if nxt is not None:
                    turn_x(nxt, 1 - par)
                if not first:
                    proj(t - 1, range(KF // 2, KF))

            tiles_in_steps(pe, step)



L_HEADS = 16
Q_LORA, KV_LORA, NOPE, ROPE, D_V = 384, 128, 128, 64, 128
KQ = Q_LORA // P
TOKENS = BATCH * SEQ
RMS_EPS = 1e-6
SLABS = KQ + 2
H_WQ, H_WK, H_WR, H_WV, H_WO, H_COLS = 0, 384, 512, 896, 1024, 1536


class Step:

    SPAN = 8

    def __init__(self, j, off):
        self.j, self.off = j, off

    def back(self, lag):
        return Step(self.j, self.off - lag)

    def count(self, each=1, more=0):
        n = self.off * each + more
        return n if isinstance(self.j, int) else self.j * (self.SPAN * each) + n

    @property
    def b(self):
        return self.off % BATCH

    @property
    def head(self):
        return Step2(self.j, self.off // BATCH)


class Step2:

    def __init__(self, j, off):
        self.j, self.off = j, off

    def count(self, each=1, more=0):
        n = self.off * each + more
        return n if isinstance(self.j, int) else self.j * (2 * each) + n


def tiles_in_quads(engine, step):
    step(0, 0, True, False)
    step(1, 1, False, False)
    with engine.Fori(0, 3) as j:
        for u in range(4):
            step(j * 4 + (2 + u), (2 + u) % 4, False, False)
    for t in range(14, TILES + 1):
        step(t, t % 4, False, t == TILES)


def latent_projections(nc, x_res, ident, lat_hi, lat_lo, v_hi, v_lo, wqa, wkr, norm_w, key_cos, key_sin,
                       first_raw, first_head):
    with ExitStack() as ctx:
        def sb(name, shape, dt=F32):
            return ctx.enter_context(nc.sbuf_tensor(name, shape, dt))

        sem = ctx.enter_context(semaphores(nc))

        psum = ctx.enter_context(nc.psum_tensor("c_psum", [P, 8, 512], F32))
        X_BANK, Q_BANK, KV_BANK, TURN_BANK = 0, 1, 3, 5
        NQ, NKV = Q_LORA, KV_LORA + ROPE
        w_raw = sb("c_w_raw", [P, KD, NQ + NKV])
        w_hi = sb("c_w_hi", [P, KD, NQ + NKV], F32R)
        w_lo = sb("c_w_lo", [P, KD, NQ + NKV], F32R)
        gain = sb("c_gain", [P, Q_LORA + KV_LORA])
        cosine = sb("c_cosine", [P, TPB, ROPE])
        sine = sb("c_sine", [P, TPB, ROPE])
        minus_half = sb("c_minus_half", [P, 2])
        stats = sb("c_stats", [P, 2, 6])
        mv = sb("c_mv", [P, 2, 2])
        ve = sb("c_ve", [P, 2])
        rstd = sb("c_rstd", [P, 2])
        shift = sb("c_shift", [P, 2])
        xn = sb("c_xn", [P, 2, D])
        xt_hi = sb("c_xt_hi", [P, 2, KD, P], F32R)
        xt_lo = sb("c_xt_lo", [P, 2, KD, P], F32R)
        squares = sb("c_squares", [P, 2, Q_LORA])
        mean_sq = sb("c_mean_sq", [P, 2, 2])
        mean_sq_eps = sb("c_mean_sq_eps", [P, 2, 2])
        rms_inv = sb("c_rms_inv", [P, 2, 2])
        latent = sb("c_latent", [P, 2, SLABS * P])
        rot = sb("c_rot", [P, 2, 2, ROPE])

        loaded = sem("c_loaded")
        next_loaded = sem("c_next_loaded")
        w_hi_ready = sem("c_w_hi_ready")
        w_lo_ready = sem("c_w_lo_ready")
        const_ready = sem("c_const_ready")
        stat_ready = sem("c_stat_ready")
        var_ready = sem("c_var_ready")
        ve_ready = sem("c_ve_ready")
        rstd_ready = sem("c_rstd_ready")
        shift_ready = sem("c_shift_ready")
        xn_ready = sem("c_xn_ready")
        xn_turned = sem("c_xn_turned")
        xt_hi_ready = sem("c_xt_hi_ready")
        xt_lo_ready = sem("c_xt_lo_ready")
        projected = sem("c_projected")
        squared = sem("c_squared")
        ms_ready = sem("c_ms_ready")
        rms_ready = sem("c_rms_ready")
        rot_ready = sem("c_rot_ready")
        latent_ready = sem("c_latent_ready")
        latent_turned = sem("c_latent_turned")
        lat_hi_ready = sem("c_lat_hi_ready")
        lat_lo_ready = sem("c_lat_lo_ready")
        v_hi_ready = sem("c_v_hi_ready")
        v_lo_ready = sem("c_v_lo_ready")
        LATENT_OPS = 4

        block = ctx.enter_context(nc.Block())

        def turned_view():
            return psum[:, :, :].rearrange("p a n -> p (a n)")[:, 512 * TURN_BANK:512 * TURN_BANK + SLABS * P]\
                .rearrange("p (k n) -> p k n", k=SLABS)

        def cols(t):
            return bass.ds(t * P, P)

        def tile(part, t):
            return part[:, bass.ds(t, 1), :].rearrange("p a n -> p (a n)")

        def has_next(t, last, ahead=1):
            return not last and not (isinstance(t, int) and t + ahead >= TILES)

        @block.sync
        def _(sp):
            sp.dma_start(w_raw[:, :, 0:NQ], wqa.rearrange("(k p) n -> p k n", p=P)).then_inc(loaded, 16)
            sp.dma_start(w_raw[:, :, NQ:NQ + NKV], wkr.rearrange("(k p) n -> p k n", p=P)).then_inc(loaded, 16)
            sp.dma_start(gain[:], norm_w).then_inc(loaded, 16)
            sp.dma_start(cosine[:], key_cos).then_inc(loaded, 16)
            sp.dma_start(sine[:], key_sin).then_inc(loaded, 16)
            sp.dma_start(first_raw[:], first_head).then_inc(next_loaded, 16)
            sp.wait_ge(next_loaded, 16)

        @block.gpsimd
        def _(pool):
            pool.memset(minus_half[:], -0.5).then_inc(const_ready, 1)
            pool.wait_ge(const_ready, 1)

            def deviation(t, par):
                wait_apart(pool, var_ready, t + 1)
                pool.tensor_scalar(ve[:, par:par + 1], mv[:, par, 1:2], LN_EPS, None, ALU.add).then_inc(ve_ready, 1)
                pool.wait_ge(ve_ready, t + 1)
                pool.tensor_tensor(rstd[:, par:par + 1], ve[:, par:par + 1], minus_half[:, 0:1], ALU.pow)\
                    .then_inc(rstd_ready, 1)
                wait_apart(pool, rstd_ready, t + 1)
                pool.tensor_scalar(shift[:, par:par + 1], mv[:, par, 0:1], -1.0, rstd[:, par:par + 1],
                                   ALU.mult, ALU.mult).then_inc(shift_ready, 1)

            def rms(t, par):
                wait_apart(pool, squared, 2 * t + 2)
                pool.tensor_scalar(mean_sq_eps[:, par, :], mean_sq[:, par, :], RMS_EPS, None, ALU.add)\
                    .then_inc(ms_ready, 1)
                pool.wait_ge(ms_ready, t + 1)
                pool.tensor_tensor(rms_inv[:, par, :], mean_sq_eps[:, par, :], minus_half[:], ALU.pow)\
                    .then_inc(rms_ready, 1)

            deviation(0, 0)
            deviation(1, 1)

            def step(t, quad, first, last):
                par = quad % 2
                if has_next(t, last, 2):
                    deviation(t + 2, par)
                if not last:
                    rms(t, par)

            tiles_in_quads(pool, step)

        @block.scalar
        def _(act):
            def normalise(t, par):
                act.wait_ge(shift_ready, t + 1)
                act.activation(xn[:, par, :], row(x_res, t), ACT.Identity, bias=shift[:, par:par + 1],
                               scale=rstd[:, par:par + 1]).then_inc(xn_ready, 1)

            def keep_x(t, par):
                act.wait_ge(xn_turned, t + 1)
                act.activation(xt_hi[:, par, :, :], psum[:, X_BANK, :].rearrange("p (k n) -> p k n", k=KD), ACT.Copy)\
                   .then_inc(xt_hi_ready, 1)

            def mean_squares(t, par, first):
                act.wait_ge(projected, t + 1)
                for which, (bank, n) in enumerate(((Q_BANK, Q_LORA), (KV_BANK, KV_LORA))):
                    if not first:
                        act.wait_ge(squared, 2 * t + which - 1)
                    act.activation(squares[:, which, 0:n], psum[:, bank + par, 0:n], ACT.Square, scale=float(n) ** -0.5,
                                   accum_out=mean_sq[:, par, which:which + 1]).then_inc(squared, 1)

            def keep_latent(t, par):
                act.wait_ge(latent_ready, LATENT_OPS * (t + 1))
                act.activation(tile(v_hi, t), latent[:, par, Q_LORA:Q_LORA + KV_LORA], ACT.Copy).then_inc(v_hi_ready, 1)
                act.wait_ge(latent_turned, t + 1)
                act.activation(lat_hi[:, :, cols(t)], turned_view(), ACT.Copy).then_inc(lat_hi_ready, 1)

            normalise(0, 0)
            normalise(1, 1)
            act.wait_ge(loaded, 16 * 5)
            for k in range(KD):
                act.activation(w_hi[:, k, :], w_raw[:, k, :], ACT.Copy).then_inc(w_hi_ready, 1)
            keep_x(0, 0)

            def step(t, quad, first, last):
                par = quad % 2
                if has_next(t, last):
                    keep_x(t + 1, 1 - par)
                if not last:
                    mean_squares(t, par, first)
                if not first:
                    keep_latent(t - 1, 1 - par)
                if has_next(t, last, 2):
                    normalise(t + 2, par)

            tiles_in_quads(act, step)
            act.wait_ge(lat_hi_ready, TILES)

        @block.vector
        def _(dve):
            def statistics(t, par):
                dve.bn_stats(stats[:, par, :], row(x_res, t)).then_inc(stat_ready, 1)
                wait_apart(dve, stat_ready, t + 1)
                dve.bn_aggr(mv[:, par, :], stats[:, par, :]).then_inc(var_ready, 1)

            def keep_x_low(t, par):
                dve.wait_ge(xt_hi_ready, t + 1)
                dve.tensor_tensor(xt_lo[:, par, :, :], psum[:, X_BANK, :].rearrange("p (k n) -> p k n", k=KD),
                                  xt_hi[:, par, :, :].bitcast(F32), ALU.subtract).then_inc(xt_lo_ready, 1)

            def rotate(t, par, quad):
                half = ROPE // 2
                keys = psum[:, KV_BANK + par, KV_LORA:KV_LORA + ROPE]
                dve.wait_ge(projected, t + 1)
                dve.wait_ge(squared, 2 * t + 2)
                if not isinstance(t, int) or t >= 2:
                    dve.wait_ge(v_lo_ready, t - 1)
                dve.tensor_tensor(rot[:, par, 0, :], keys, cosine[:, quad, :], ALU.mult).then_inc(rot_ready, 1)
                dve.tensor_tensor(rot[:, par, 1, 0:half], keys[:, half:ROPE], sine[:, quad, 0:half], ALU.mult)\
                   .then_inc(rot_ready, 1)
                dve.tensor_tensor(rot[:, par, 1, half:ROPE], keys[:, 0:half], sine[:, quad, half:ROPE], ALU.mult)\
                   .then_inc(rot_ready, 1)

            def make_latent(t, par):
                dve.wait_ge(rms_ready, t + 1)
                dve.scalar_tensor_tensor(out=latent[:, par, 0:Q_LORA], in0=psum[:, Q_BANK + par, 0:Q_LORA],
                                         scalar=rms_inv[:, par, 0:1], in1=gain[:, 0:Q_LORA], op0=ALU.mult,
                                         op1=ALU.mult).then_inc(latent_ready, 1)
                dve.scalar_tensor_tensor(out=latent[:, par, Q_LORA:Q_LORA + KV_LORA],
                                         in0=psum[:, KV_BANK + par, 0:KV_LORA], scalar=rms_inv[:, par, 1:2],
                                         in1=gain[:, Q_LORA:Q_LORA + KV_LORA], op0=ALU.mult, op1=ALU.mult)\
                   .then_inc(latent_ready, 1)
                dve.wait_ge(rot_ready, 3 * t + 3)
                for c in range(2):
                    o = Q_LORA + KV_LORA + ROPE * c
                    dve.tensor_tensor(latent[:, par, o:o + ROPE], rot[:, par, 0, :], rot[:, par, 1, :], ALU.add)\
                       .then_inc(latent_ready, 1)

            def keep_latent_low(t, par):
                dve.wait_ge(v_hi_ready, t + 1)
                dve.tensor_tensor(tile(v_lo, t), latent[:, par, Q_LORA:Q_LORA + KV_LORA],
                                  tile(v_hi, t).bitcast(F32), ALU.subtract).then_inc(v_lo_ready, 1)
                dve.wait_ge(lat_hi_ready, t + 1)
                dve.tensor_tensor(lat_lo[:, :, cols(t)], turned_view(), lat_hi[:, :, cols(t)].bitcast(F32),
                                  ALU.subtract).then_inc(lat_lo_ready, 1)

            statistics(0, 0)
            statistics(1, 1)
            for k in range(KD):
                dve.wait_ge(w_hi_ready, k + 1)
                dve.tensor_tensor(w_lo[:, k, :], w_raw[:, k, :], w_hi[:, k, :].bitcast(F32), ALU.subtract)\
                   .then_inc(w_lo_ready, 1)
            keep_x_low(0, 0)

            def step(t, quad, first, last):
                par = quad % 2
                if has_next(t, last):
                    keep_x_low(t + 1, 1 - par)
                if has_next(t, last, 2):
                    statistics(t + 2, par)
                if not last:
                    rotate(t, par, quad)
                    make_latent(t, par)
                if not first:
                    keep_latent_low(t - 1, 1 - par)

            tiles_in_quads(dve, step)
            dve.wait_ge(lat_lo_ready, TILES)

        @block.tensor
        def _(pe):
            def turn_x(t, par):
                pe.wait_ge(xn_ready, t + 1)
                for k in range(KD):
                    ins = pe.transpose(psum[:, X_BANK, P * k:P * k + P], xn[:, par, P * k:P * k + P], ident[:])
                ins.then_inc(xn_turned, 1)

            def project(t, par, bank, lo, n):
                pe.wait_ge(xt_lo_ready, t + 1)
                for k in range(KD):
                    for i, (x, w) in enumerate(((xt_hi, w_hi), (xt_hi, w_lo), (xt_lo, w_hi))):
                        ins = pe.matmul(psum[:, bank + par, 0:n], x[:, par, k, :], w[:, k, lo:lo + n],
                                        start=k == 0 and i == 0, stop=k == KD - 1 and i == 2)
                return ins

            def turn_latent(t, par):
                pe.wait_ge(latent_ready, LATENT_OPS * (t + 1))
                out = psum[:, :, :].rearrange("p a n -> p (a n)")
                for k in range(SLABS):
                    o = 512 * TURN_BANK + P * k
                    ins = pe.transpose(out[:, o:o + P], latent[:, par, P * k:P * k + P], ident[:])
                ins.then_inc(latent_turned, 1)

            turn_x(0, 0)
            pe.wait_ge(w_lo_ready, KD)

            def step(t, quad, first, last):
                par = quad % 2
                if not last:
                    project(t, par, Q_BANK, 0, NQ)
                if has_next(t, last):
                    turn_x(t + 1, 1 - par)
                if not last:
                    project(t, par, KV_BANK, NQ, NKV).then_inc(projected, 1)
                if not first:
                    if not (isinstance(t, int) and t == 1):
                        pe.wait_ge(lat_lo_ready, t - 1)
                    turn_latent(t - 1, 1 - par)

            tiles_in_quads(pe, step)


L_OUT_BANKS = (6, 7, 0, 1)
L_Q_BANK, L_Z_BANK, L_O_BANK = 2, 6, 7
L_WP_BANK, L_WVO_BANK = 3, 4
LAST_LAG = 3


def latent_attention(nc, x_res, ident, lat_hi, lat_lo, v_hi, v_lo, w_raw, head_w, causal, rotation):
    with ExitStack() as ctx:
        def sb(name, shape, dt=F32):
            return ctx.enter_context(nc.sbuf_tensor(name, shape, dt))

        sem = ctx.enter_context(semaphores(nc))

        psum = ctx.enter_context(nc.psum_tensor("d_psum", [P, 8, 512], F32))
        pre_hi = sb("d_pre_hi", [P, 640], F32R)
        pre_lo = sb("d_pre_lo", [P, 640], F32R)
        wr_hi = sb("d_wr_hi", [P, 2, KQ * P], F32R)
        wr_lo = sb("d_wr_lo", [P, 2, KQ * P], F32R)
        wp_hi = sb("d_wp_hi", [P, 2, KQ * P], F32R)
        wp_lo = sb("d_wp_lo", [P, 2, KQ * P], F32R)
        wvo_hi = sb("d_wvo_hi", [P, 2, D], F32R)
        wvo_lo = sb("d_wvo_lo", [P, 2, D], F32R)
        mask = sb("d_mask", [P, SEQ])
        rotate = sb("d_rotate", [P, SEQ])
        q_hi = sb("d_q_hi", [P, 2, SEQ], F32R)
        q_lo = sb("d_q_lo", [P, 2, SEQ], F32R)
        zf = sb("d_zf", [P, SEQ])
        z_hi = sb("d_z_hi", [P, 2, SEQ], F32R)
        z_lo = sb("d_z_lo", [P, 2, SEQ], F32R)
        probs = sb("d_probs", [P, 2, SCORE_COLS])
        pt_hi = sb("d_pt_hi", [P, SCORE_COLS], F32R)
        pt_lo = sb("d_pt_lo", [P, SCORE_COLS], F32R)
        low = sb("d_low", [P, 2, TPB])
        rowsum = sb("d_rowsum", [P, 2, TPB])
        rinv = sb("d_rinv", [P, 2, TPB])
        o_hi = sb("d_o_hi", [P, SEQ], F32R)
        o_lo = sb("d_o_lo", [P, SEQ], F32R)

        tables_loaded = sem("d_tables_loaded")
        w_loaded = sem("d_w_loaded")
        keys_hi = sem("d_keys_hi")
        keys_lo = sem("d_keys_lo")
        rope_hi = sem("d_rope_hi")
        rope_lo = sem("d_rope_lo")
        values_hi = sem("d_values_hi")
        values_lo = sem("d_values_lo")
        wp_made = sem("d_wp_made")
        wp_hi_ready = sem("d_wp_hi_ready")
        wp_lo_ready = sem("d_wp_lo_ready")
        wvo_made = sem("d_wvo_made")
        wvo_hi_ready = sem("d_wvo_hi_ready")
        wvo_lo_ready = sem("d_wvo_lo_ready")
        q_made = sem("d_q_made")
        z_made = sem("d_z_made")
        q_hi_ready = sem("d_q_hi_ready")
        q_lo_ready = sem("d_q_lo_ready")
        zf_ready = sem("d_zf_ready")
        z_hi_ready = sem("d_z_hi_ready")
        z_lo_ready = sem("d_z_lo_ready")
        scores_ready = sem("d_scores_ready")
        masked_ready = sem("d_masked_ready")
        exp_ready = sem("d_exp_ready")
        rinv_ready = sem("d_rinv_ready")
        probs_ready = sem("d_probs_ready")
        turned = sem("d_turned")
        pt_hi_ready = sem("d_pt_hi_ready")
        pt_lo_ready = sem("d_pt_lo_ready")
        mixed = sem("d_mixed")
        o_hi_ready = sem("d_o_hi_ready")
        o_lo_ready = sem("d_o_lo_ready")
        out_ready = sem("d_out_ready")
        added = sem("d_added")

        STEPS = L_HEADS * BATCH
        PT_COPIES = ((3, 0, 512), (4, 512, 512), (5, 1024, 256))

        def run(engine, step):
            for off in range(Step.SPAN):
                step(Step(0, off))
            with engine.Fori(1, STEPS // Step.SPAN - 1) as j:
                for off in range(Step.SPAN):
                    step(Step(j, off))
            for off in range(STEPS - Step.SPAN, STEPS + LAST_LAG):
                step(Step(0, off))

        def begun(s):
            return not isinstance(s.j, int) or 0 <= s.off < STEPS

        def started(s, n=0):
            return not isinstance(s.j, int) or s.off >= n

        def prepares(s, b):
            return s.b == b and begun(s) and not (isinstance(s.j, int) and s.off >= STEPS - BATCH)

        block = ctx.enter_context(nc.Block())

        @block.sync
        def _(sp):
            sp.dma_start(mask[:], causal).then_inc(tables_loaded, 16)
            sp.dma_start(rotate[:], rotation).then_inc(tables_loaded, 16)
            with sp.Fori(1, L_HEADS) as h:
                sp.wait_ge(keys_lo, h)
                sp.wait_ge(rope_lo, h)
                sp.wait_ge(values_lo, h)
                sp.dma_start(w_raw[:], head_w[bass.ds(h, 1)].rearrange("a p n -> p (a n)")).then_inc(w_loaded, 16)
            sp.wait_ge(w_loaded, 16 * (L_HEADS - 1))

        @block.scalar
        def _(act):
            def split_keys(h, slot, first=False):
                if not first:
                    act.wait_ge(w_loaded, h.count(16))
                    act.wait_ge(wvo_made, h.count())
                act.activation(pre_hi[:, 0:512], w_raw[:, 0:512], ACT.Copy).then_inc(keys_hi, 1)
                act.activation(wr_hi[:, slot, :], w_raw[:, H_WR:H_WV], ACT.Copy).then_inc(rope_hi, 1)

            def keep_wp(h, slot):
                act.wait_ge(wp_made, h.count(1, 1))
                act.activation(wp_hi[:, slot, :], psum[:, L_WP_BANK, 0:KQ * P], ACT.Copy).then_inc(wp_hi_ready, 1)

            def split_values(h):
                act.wait_ge(wp_made, h.count(1, 1))
                act.activation(pre_hi[:, 0:640], w_raw[:, H_WV:H_COLS], ACT.Copy).then_inc(values_hi, 1)

            def keep_wvo(h, slot):
                act.wait_ge(wvo_made, h.count(1, 1))
                act.activation(wvo_hi[:, slot, :], psum[:, L_WVO_BANK, :], ACT.Copy).then_inc(wvo_hi_ready, 1)

            h0 = Step2(0, 0)
            split_keys(h0, 0, True)
            keep_wp(h0, 0)
            split_values(h0)
            keep_wvo(h0, 0)

            def step(s):
                o, e, n = s.back(3), s.back(2), s.back(1)
                nxt = s.head
                nxt = Step2(nxt.j, nxt.off + 1)
                slot = nxt.off % 2
                if prepares(s, 2):
                    keep_wp(nxt, slot)
                if prepares(s, 3):
                    keep_wvo(nxt, slot)
                if begun(o):
                    act.wait_ge(mixed, o.count(1, 1))
                    act.activation(o_hi[:], psum[:, L_O_BANK, :], ACT.Copy).then_inc(o_hi_ready, 1)
                if begun(n):
                    for i in range(TPB):
                        act.wait_ge(masked_ready, n.count(TPB, i + 1))
                        c, w = SCORE_OFFSET[i], P * (i + 1)
                        part = probs[:, n.off % 2, c:c + w]
                        act.activation(part, part, ACT.Exp, bias=low[:, n.off % 2, i:i + 1], scale=-1.0,
                                       accum_out=rowsum[:, n.off % 2, i:i + 1]).then_inc(exp_ready, 1)
                if begun(e):
                    act.wait_ge(turned, e.count(1, 1))
                    for bank, c, w in PT_COPIES:
                        act.activation(pt_hi[:, c:c + w], psum[:, bank, 0:w], ACT.Copy).then_inc(pt_hi_ready, 1)
                if begun(s):
                    act.wait_ge(q_made, s.count(1, 1))
                    act.activation(q_hi[:, s.off % 2, :], psum[:, L_Q_BANK, :], ACT.Copy).then_inc(q_hi_ready, 1)
                    act.wait_ge(zf_ready, s.count(1, 1))
                    act.activation(z_hi[:, s.off % 2, :], zf[:], ACT.Copy).then_inc(z_hi_ready, 1)
                if prepares(s, 0):
                    split_keys(nxt, slot)
                if prepares(s, 2):
                    split_values(nxt)

            run(act, step)

        @block.vector
        def _(dve):
            def split_keys(h, slot):
                dve.wait_ge(keys_hi, h.count(1, 1))
                dve.tensor_tensor(pre_lo[:, 0:512], w_raw[:, 0:512], pre_hi[:, 0:512].bitcast(F32), ALU.subtract)\
                   .then_inc(keys_lo, 1)
                dve.wait_ge(rope_hi, h.count(1, 1))
                dve.tensor_tensor(wr_lo[:, slot, :], w_raw[:, H_WR:H_WV], wr_hi[:, slot, :].bitcast(F32),
                                  ALU.subtract).then_inc(rope_lo, 1)

            def keep_wp(h, slot):
                dve.wait_ge(wp_hi_ready, h.count(1, 1))
                dve.tensor_tensor(wp_lo[:, slot, :], psum[:, L_WP_BANK, 0:KQ * P], wp_hi[:, slot, :].bitcast(F32),
                                  ALU.subtract).then_inc(wp_lo_ready, 1)

            def split_values(h):
                dve.wait_ge(values_hi, h.count(1, 1))
                dve.tensor_tensor(pre_lo[:, 0:640], w_raw[:, H_WV:H_COLS], pre_hi[:, 0:640].bitcast(F32),
                                  ALU.subtract).then_inc(values_lo, 1)

            def keep_wvo(h, slot):
                dve.wait_ge(wvo_hi_ready, h.count(1, 1))
                dve.tensor_tensor(wvo_lo[:, slot, :], psum[:, L_WVO_BANK, :], wvo_hi[:, slot, :].bitcast(F32),
                                  ALU.subtract).then_inc(wvo_lo_ready, 1)

            h0 = Step2(0, 0)
            dve.wait_ge(tables_loaded, 32)
            split_keys(h0, 0)
            keep_wp(h0, 0)
            split_values(h0)
            keep_wvo(h0, 0)

            def step(s):
                o, e, n = s.back(3), s.back(2), s.back(1)
                nxt = s.head
                nxt = Step2(nxt.j, nxt.off + 1)
                slot = nxt.off % 2
                if prepares(s, 2):
                    keep_wp(nxt, slot)
                if prepares(s, 3):
                    keep_wvo(nxt, slot)
                if begun(o):
                    dve.wait_ge(o_hi_ready, o.count(1, 1))
                    dve.tensor_tensor(o_lo[:], psum[:, L_O_BANK, :], o_hi[:].bitcast(F32),
                                      ALU.subtract).then_inc(o_lo_ready, 1)
                if begun(n):
                    if started(n, 2):
                        dve.wait_ge(turned, n.count(1, -1))
                    for i in range(TPB):
                        wait_apart(dve, scores_ready, n.count(TPB, (3, 2, 3, 4)[i]))
                        bank, at = SCORE_PLACE[i]
                        c, w = SCORE_OFFSET[i], P * (i + 1)
                        dve.tensor_tensor_reduce(probs[:, n.off % 2, c:c + w], psum[:, bank, at:at + w],
                                                 mask[:, SEQ - w:SEQ], -((NOPE + ROPE) ** -0.5), -MASKED,
                                                 ALU.add, ALU.min, low[:, n.off % 2, i:i + 1])\
                           .then_inc(masked_ready, 1)
                if begun(e):
                    for i, (bank, c, w) in enumerate(PT_COPIES):
                        dve.wait_ge(pt_hi_ready, e.count(3, i + 1))
                        dve.tensor_tensor(pt_lo[:, c:c + w], psum[:, bank, 0:w], pt_hi[:, c:c + w].bitcast(F32),
                                          ALU.subtract).then_inc(pt_lo_ready, 1)
                if begun(n):
                    dve.wait_ge(exp_ready, n.count(TPB, TPB))
                    dve.reciprocal(rinv[:, n.off % 2, :], rowsum[:, n.off % 2, :]).then_inc(rinv_ready, 1)
                    dve.wait_ge(rinv_ready, n.count(1, 1))
                    for i in range(TPB):
                        c, w = SCORE_OFFSET[i], P * (i + 1)
                        part = probs[:, n.off % 2, c:c + w]
                        dve.tensor_scalar(part, part, rinv[:, n.off % 2, i:i + 1], None, ALU.mult)\
                           .then_inc(probs_ready, 1)
                if begun(o):
                    for i, bank in enumerate(L_OUT_BANKS):
                        dve.wait_ge(out_ready, o.count(TPB, i + 1))
                        if started(o, BATCH):
                            dve.wait_ge(added, o.count(TPB, i + 1 - TPB * BATCH))
                        tile = x_res[:, o.b * TPB + i, :]
                        dve.tensor_tensor(tile, psum[:, bank, :], tile, ALU.add).then_inc(added, 1)
                if begun(s):
                    dve.wait_ge(z_made, s.count(1, 1))
                    if started(s, 1):
                        dve.wait_ge(z_hi_ready, s.count())
                        dve.wait_ge(z_lo_ready, s.count())
                    dve.tensor_tensor(zf[:], psum[:, L_Z_BANK, :], rotate[:], ALU.mult).then_inc(zf_ready, 1)
                    dve.wait_ge(q_hi_ready, s.count(1, 1))
                    dve.tensor_tensor(q_lo[:, s.off % 2, :], psum[:, L_Q_BANK, :], q_hi[:, s.off % 2, :].bitcast(F32),
                                      ALU.subtract).then_inc(q_lo_ready, 1)
                    dve.wait_ge(z_hi_ready, s.count(1, 1))
                    dve.tensor_tensor(z_lo[:, s.off % 2, :], zf[:], z_hi[:, s.off % 2, :].bitcast(F32),
                                      ALU.subtract).then_inc(z_lo_ready, 1)
                if prepares(s, 0):
                    split_keys(nxt, slot)
                if prepares(s, 2):
                    split_values(nxt)

            run(dve, step)
            dve.wait_ge(added, STEPS * TPB)

        @block.tensor
        def _(pe):
            def three(out, lhs_hi, lhs_lo, rhs_hi, rhs_lo, first, last):
                for i, (a, c) in enumerate(((lhs_hi, rhs_hi), (lhs_hi, rhs_lo), (lhs_lo, rhs_hi))):
                    ins = pe.matmul(out, a, c, start=first and i == 0, stop=last and i == 2)
                return ins

            def make_wp(h):
                pe.wait_ge(keys_lo, h.count(1, 1))
                for k in range(KQ):
                    ins = three(psum[:, L_WP_BANK, P * k:P * k + P], pre_hi[:, P * k:P * k + P],
                                pre_lo[:, P * k:P * k + P], pre_hi[:, H_WK:H_WK + P], pre_lo[:, H_WK:H_WK + P],
                                True, True)
                ins.then_inc(wp_made, 1)

            def make_wvo(h):
                pe.wait_ge(values_lo, h.count(1, 1))
                three(psum[:, L_WVO_BANK, :], pre_hi[:, 0:P], pre_lo[:, 0:P], pre_hi[:, P:P + D], pre_lo[:, P:P + D],
                      True, True).then_inc(wvo_made, 1)

            h0 = Step2(0, 0)
            make_wp(h0)
            make_wvo(h0)

            def scores(n):
                pe.wait_ge(q_lo_ready, n.count(1, 1))
                pe.wait_ge(z_lo_ready, n.count(1, 1))
                if started(n, 3):
                    pe.wait_ge(added, n.count(TPB, -2 * TPB))
                for i in range(TPB):
                    bank, at = SCORE_PLACE[i]
                    w = P * (i + 1)
                    rows = slice(P * i, P * i + P)
                    out = psum[:, bank, at:at + w]
                    ks = slice(n.b * SEQ, n.b * SEQ + w)
                    three(out, q_hi[:, n.off % 2, rows], q_lo[:, n.off % 2, rows], lat_hi[:, KQ, ks], lat_lo[:, KQ, ks],
                          True, False)
                    three(out, z_hi[:, n.off % 2, rows], z_lo[:, n.off % 2, rows], lat_hi[:, KQ + 1, ks],
                          lat_lo[:, KQ + 1, ks], False, True).then_inc(scores_ready, 1)

            def turn(e):
                pe.wait_ge(probs_ready, e.count(TPB, TPB))
                for kt in range(TPB):
                    bank, at = PT_PLACE[kt]
                    for i in range(kt, TPB):
                        c = SCORE_OFFSET[i] + P * kt
                        ins = pe.transpose(psum[:, bank, at + P * (i - kt):at + P * (i - kt + 1)],
                                           probs[:, e.off % 2, c:c + P], ident[:])
                ins.then_inc(turned, 1)

            def outputs(o):
                pe.wait_ge(o_lo_ready, o.count(1, 1))
                slot = o.head.off % 2
                for i, bank in enumerate(L_OUT_BANKS):
                    rows = slice(P * i, P * i + P)
                    three(psum[:, bank, :], o_hi[:, rows], o_lo[:, rows], wvo_hi[:, slot, :],
                          wvo_lo[:, slot, :], True, True).then_inc(out_ready, 1)

            def project(s):
                slot = s.head.off % 2
                toks = slice(s.b * SEQ, s.b * SEQ + SEQ)
                for bank, hi, lo, made in ((L_Q_BANK, wp_hi, wp_lo, q_made), (L_Z_BANK, wr_hi, wr_lo, z_made)):
                    if bank == L_Z_BANK and started(s, 3):
                        pe.wait_ge(added, s.count(TPB, 1 - 3 * TPB))
                    for k in range(KQ):
                        ins = three(psum[:, bank, :], hi[:, slot, P * k:P * k + P], lo[:, slot, P * k:P * k + P],
                                    lat_hi[:, k, toks], lat_lo[:, k, toks], k == 0, k == KQ - 1)
                    ins.then_inc(made, 1)

            def mix(e):
                pe.wait_ge(pt_lo_ready, e.count(3, 3))
                if started(e, 1):
                    pe.wait_ge(added, e.count(TPB, 2 - TPB))
                for kt in range(TPB):
                    c, w = PT_OFFSET[kt], SEQ - P * kt
                    out = psum[:, L_O_BANK, P * kt:SEQ]
                    t = e.b * TPB + kt
                    for i, (v, p) in enumerate(((v_hi, pt_hi), (v_hi, pt_lo), (v_lo, pt_hi))):
                        ins = pe.matmul(out, v[:, t, :], p[:, c:c + w], start=kt == 0 and i == 0,
                                        stop=kt == TPB - 1 and i == 2, skip_group_check=True)
                ins.then_inc(mixed, 1)

            def step(s):
                o, e, n = s.back(3), s.back(2), s.back(1)
                nxt = s.head
                nxt = Step2(nxt.j, nxt.off + 1)
                if begun(n):
                    scores(n)
                if begun(e):
                    if prepares(s, 2):
                        pe.wait_ge(wp_lo_ready, nxt.count(1, 1))
                    if prepares(s, 3):
                        pe.wait_ge(wvo_lo_ready, nxt.count(1, 1))
                    turn(e)
                if begun(n):
                    pe.wait_ge(masked_ready, n.count(TPB, TPB))
                if begun(o):
                    outputs(o)
                if begun(s):
                    if s.b == 0:
                        pe.wait_ge(wp_lo_ready, s.head.count(1, 1))
                        pe.wait_ge(rope_lo, s.head.count(1, 1))
                    project(s)
                if begun(e):
                    mix(e)
                if prepares(s, 1):
                    make_wp(nxt)
                if prepares(s, 2):
                    make_wvo(nxt)

            run(pe, step)



ROUTED, TOP_K = 7, 3
EXPERTS = ROUTED + 1
HALF = TILES // 2
ROUTED_SLOTS = TOP_K * TOKENS // P + ROUTED - 1
LAST_HALF = HALF + ROUTED_SLOTS
SLOTS = LAST_HALF + HALF
TURNS = ROUTED + 2
RANKS = ROUTED * ROUTED
TABLE = "table"
K_BEFORE, K_EARLIER, K_FILLS, K_SLOT = 0, P, P + RANKS, P + RANKS + TILES
K_COLS = K_SLOT + SLOTS


def mixture_of_experts(nc, x_res, ident, weights, gate_w, gate_b, select_b, constants, slot_in, slot_out,
                       out):
    with ExitStack() as ctx:
        def sb(name, shape, dt=F32):
            return ctx.enter_context(nc.sbuf_tensor(name, shape, dt))

        sem = ctx.enter_context(semaphores(nc))

        psum = ctx.enter_context(nc.psum_tensor("e_psum", [P, 8, 512], F32))
        X_BANK, UP_BANK, GATE_BANK, H_BANK, OUT_BANK, COUNT_BANK, LOGIT_BANK, PLACE_BANK = range(8)
        LOGIT_T_BANKS = (4, 5)
        raw = sb("e_raw", [P, 3, KD, D])
        w_hi = sb("e_w_hi", [P, 2, 3, KD, D], F32R)
        w_lo = sb("e_w_lo", [P, 2, 3, KD, D], F32R)
        gt_hi, gt_lo = w_hi[:, 1, 0], w_lo[:, 1, 0]
        rows = sb("e_rows", [P, 2, TPB, D])
        xs = sb("e_xs", [P, D])
        xt_hi = sb("e_xt_hi", [P, KD, P], F32R)
        xt_lo = sb("e_xt_lo", [P, KD, P], F32R)
        gated = sb("e_gated", [P, D])
        product = sb("e_product", [P, D])
        logits_t = (gated[0:EXPERTS, :], product[0:EXPERTS, :])
        ht_hi = sb("e_ht_hi", [P, KD, P], F32R)
        ht_lo = sb("e_ht_lo", [P, KD, P], F32R)
        ys = sb("e_ys", [P, D])
        stats = sb("e_stats", [P, TPB, 6])
        mv = sb("e_mv", [P, TPB, 2])
        ve = sb("e_ve", [P, TPB])
        rstd = sb("e_rstd", [P, 2, TPB])
        shift = sb("e_shift", [P, 2, TPB])
        minus_half = sb("e_minus_half", [P, TPB])
        ones = sb("e_ones", [P, P])
        ones_r = sb("e_ones_r", [P, P], F32R)
        above_r = sb("e_above_r", [P, P], F32R)
        zero = sb("e_zero", [P, TILES])
        table = sb("e_table", [P, K_COLS])
        g_raw = sb("e_g_raw", [P, KD, EXPERTS])
        g_hi = sb("e_g_hi", [P, KD, EXPERTS], F32R)
        g_lo = sb("e_g_lo", [P, KD, EXPERTS], F32R)
        g_bias = sb("e_g_bias", [EXPERTS, 1])
        s_bias = sb("e_s_bias", [P, ROUTED])
        logits = sb("e_logits", [P, TILES, ROUTED])
        top = sb("e_top", [P, TILES])
        proba = sb("e_proba", [P, TILES, ROUTED])
        biased = sb("e_biased", [P, TILES, ROUTED])
        beats = sb("e_beats", [P, TILES, ROUTED, ROUTED])
        rank = sb("e_rank", [P, TILES, ROUTED])
        total = sb("e_total", [P, 2, TILES])
        chosen = sb("e_chosen", [P, TILES, EXPERTS], F32R)
        per_expert = sb("e_per_expert", [P, ROUTED])
        fills = sb("e_fills", [P, ROUTED, TILES])
        slots_of = sb("e_slots_of", [P, ROUTED])
        before_of = sb("e_before_of", [P, ROUTED, ROUTED])
        start = sb("e_start", [P, EXPERTS])
        place = sb("e_place", [P, TILES, ROUTED])
        nth = sb("e_nth", [P, TILES, ROUTED])
        pick = sb("e_pick", [P, TILES, ROUTED])
        picked = sb("e_picked", [P, TILES, ROUTED])
        share = sb("e_share", [P, TILES, TOP_K])
        target = sb("e_target", [P, TILES, TOP_K])
        target_row = sb("e_target_row", [P, TILES * TOP_K], mybir.dt.int32)
        result_row = sb("e_result_row", [P, TILES * TOP_K], mybir.dt.int32)
        share_now = sb("e_share_now", [P, 2 * TOP_K])
        started = sb("e_started", [1, SLOTS, EXPERTS])
        turn = sb("e_turn", [1, SLOTS])
        fresh = sb("e_fresh", [1, 2, SLOTS])
        turn_of = sb("e_turn_of", [1, SLOTS], mybir.dt.int32)
        next_of = sb("e_next_of", [1, SLOTS], mybir.dt.int32)

        small_loaded = sem("e_small_loaded")
        w_loaded = [sem(f"e_w_loaded{m}") for m in range(3)]
        const_ready = sem("e_const_ready")
        g_hi_ready = sem("e_g_hi_ready")
        g_lo_ready = sem("e_g_lo_ready")
        stat_ready = sem("e_stat_ready")
        var_ready = sem("e_var_ready")
        ve_ready = sem("e_ve_ready")
        rstd_ready = sem("e_rstd_ready")
        shift_ready = sem("e_shift_ready")
        xn_ready = sem("e_xn_ready")
        xn_turned = sem("e_xn_turned")
        xn_stored = sem("e_xn_stored")
        gt_hi_ready = sem("e_gt_hi_ready")
        gt_lo_ready = sem("e_gt_lo_ready")
        logits_made = sem("e_logits_made")
        centred_ready = sem("e_centred_ready")
        exp_ready = sem("e_exp_ready")
        logits_kept = sem("e_logits_kept")
        logits_turned = sem("e_logits_turned")
        gate_step = sem("e_gate_step")
        sums_ready = sem("e_sums_ready")
        chosen_ready = sem("e_chosen_ready")
        place_made = sem("e_place_made")
        counted = sem("e_counted")
        targets_ready = sem("e_targets_ready")
        turns_ready = sem("e_turns_ready")
        rows_loaded = sem("e_rows_loaded")
        row_ready = sem("e_row_ready")
        scattered = sem("e_scattered")
        xs_loaded = sem("e_xs_loaded")
        x_turned = sem("e_x_turned")
        xt_hi_ready = sem("e_xt_hi_ready")
        xt_lo_ready = sem("e_xt_lo_ready")
        w_hi_ready = sem("e_w_hi_ready")
        first_lo_ready = sem("e_first_lo_ready")
        w_lo_ready = sem("e_w_lo_ready")
        up_made = sem("e_up_made")
        gated_ready = sem("e_gated_ready")
        product_ready = sem("e_product_ready")
        h_turned = sem("e_h_turned")
        ht_hi_ready = sem("e_ht_hi_ready")
        ht_lo_ready = sem("e_ht_lo_ready")
        out_made = sem("e_out_made")
        ys_ready = sem("e_ys_ready")
        ys_stored = sem("e_ys_stored")
        gathered = [sem("e_gathered0"), sem("e_gathered1")]
        share_ready = sem("e_share_ready")
        combined = sem("e_combined")
        stored = sem("e_stored")
        added = sem("e_added")

        block = ctx.enter_context(nc.Block())

        def steps(engine, step):
            last = TURNS - 1
            step(0, 0, None, None)
            step(1, 0, 0, "first half")
            with engine.Fori(2, HALF) as s:
                step(s, 0, 0, "first half")
            step(HALF, 1, 0, "first half")
            step(HALF + 1, TABLE, 1, "routed")
            with engine.Fori(HALF + 2, LAST_HALF) as s:
                step(s, TABLE, TABLE, "routed")
            step(LAST_HALF, last, TABLE, "routed")
            with engine.Fori(LAST_HALF + 1, SLOTS - 1) as s:
                step(s, last, last, "second half")
            step(SLOTS - 1, last, last, "second half")
            step(SLOTS, None, last, "second half")

        def has_next(s):
            return not (isinstance(s, int) and s >= SLOTS - 1)

        def turn_at(engine, s, known):
            if known is not TABLE:
                return known
            return engine.value_load(turn_of[0:1, bass.ds(s, 1)], min_val=1, max_val=TURNS - 2)

        def when_fresh(engine, s, turn_of_s, split, matrices):
            if turn_of_s is TABLE:
                n = engine.value_load(next_of[0:1, bass.ds(s, 1)], min_val=0, max_val=TURNS - 1)
                with engine.If(n != 0):
                    split(n, matrices)
            elif isinstance(s, int) and s in (0, HALF):
                split(turn_of_s + 1, matrices)

        def split_ahead(engine, s, now, before, split):
            when_fresh(engine, s - 1, before, split, (2,))
            when_fresh(engine, s, now, split, (0, 1))

        def matrix(part, n, m):
            if isinstance(n, int):
                return part[:, n % 2, m]
            return part[:, bass.ds(n % 2, 1), m].rearrange("p a k n -> p (a k) n")

        def block_of(part, n, m, k):
            if isinstance(n, int):
                return part[:, n % 2, m, k]
            return part[:, bass.ds(n % 2, 1), m, k].rearrange("p a n -> p (a n)")

        def home(b):
            slot = TPB * b if b < BATCH // 2 else LAST_HALF - HALF + TPB * b
            return slot_in[P * slot:P * (slot + TPB)].rearrange("(t p) n -> p t n", p=P)

        def chunks(bank):
            return psum[:, bank, :].rearrange("p (k n) -> p k n", k=KD)

        @block.sync
        def _(sp):
            for dest, source in ((table, constants), (g_bias, gate_b), (s_bias, select_b)):
                sp.dma_start(dest[:], source).then_inc(small_loaded, 16)
            sp.dma_start(g_raw[:], gate_w.rearrange("(k p) n -> p k n", p=P)).then_inc(small_loaded, 16)
            for b in range(BATCH):
                sp.wait_ge(xn_ready, TPB * (b + 1))
                if b:
                    sp.wait_ge(xn_stored, 16 * b)
                sp.dma_start(home(b), rows[:, b % 2]).then_inc(xn_stored, 16)
            sp.wait_ge(xn_stored, 16 * BATCH)

            def load(s):
                if not (isinstance(s, int) and s == 0):
                    sp.wait_ge(x_turned, s)
                sp.dma_start(xs[:], slot_in[bass.ds(s * P, P), :]).then_inc(xs_loaded, 16)

            def store(s):
                sp.wait_ge(ys_ready, s - (HALF - 1))
                sp.dma_start(slot_out[bass.ds((s - HALF) * P, P), :], ys[:]).then_inc(ys_stored, 16)

            load(0)
            with sp.Fori(1, HALF) as s:
                load(s)
            sp.wait_ge(scattered, 16 * TILES * TOP_K)
            load(HALF)
            load(HALF + 1)
            with sp.Fori(HALF + 1, LAST_HALF + 1) as s:
                load(s + 1)
                store(s - 1)
            with sp.Fori(LAST_HALF + 2, SLOTS) as s:
                load(s)
            sp.wait_ge(ys_stored, 16 * ROUTED_SLOTS)
            tiles = out.rearrange("b (t p) n -> p (b t) n", p=P)
            for t in range(0, TILES, 2):
                sp.wait_ge(combined, TOP_K * (t + 2))
                sp.dma_start(tiles[:, t:t + 2, :], x_res[:, t:t + 2, :]).then_inc(stored, 16)
            sp.wait_ge(stored, 16 * (TILES // 2))

        @block.gpsimd
        def _(pool):
            for m in range(3):
                pool.dma_start(raw[:, m], weights[0, m].rearrange("(k p) n -> p k n", p=P)).then_inc(w_loaded[m], 16)
            pool.memset(minus_half[:], -0.5).then_inc(const_ready, 1)
            pool.memset(ones[:], 1.0).then_inc(const_ready, 1)
            pool.memset(zero[:], 0.0).then_inc(const_ready, 1)
            pool.wait_ge(const_ready, 3)
            for b in range(BATCH):
                if b:
                    pool.wait_ge(rstd_ready, b)
                pool.wait_ge(var_ready, TPB * (b + 1))
                pool.tensor_scalar(ve[:], mv[:, :, 1], LN_EPS, None, ALU.add).then_inc(ve_ready, 1)
                pool.wait_ge(ve_ready, b + 1)
                if b >= 2:
                    pool.wait_ge(xn_ready, TPB * (b - 1))
                pool.tensor_tensor(rstd[:, b % 2, :], ve[:], minus_half[:], ALU.pow).then_inc(rstd_ready, 1)

            for m in range(3):
                pool.wait_ge(w_hi_ready, m + 1)
                pool.tensor_tensor(w_lo[:, 0, m], raw[:, m], w_hi[:, 0, m].bitcast(F32), ALU.subtract)\
                    .then_inc(first_lo_ready, 1)

            def load_weights(n):
                for m in range(3):
                    if isinstance(n, int):
                        pool.wait_ge(first_lo_ready, m + 1)
                    else:
                        pool.wait_ge(w_lo_ready, n * 3 + (m - 2))
                    source = weights[bass.ds(n, 1), m].rearrange("a (k p) n -> p (a k) n", p=P)
                    pool.dma_start(raw[:, m], source).then_inc(w_loaded[m], 16)

            load_weights(1)
            pool.wait_ge(xn_stored, 16 * BATCH)
            pool.wait_ge(targets_ready, 2)

            def load_rows(b):
                if b >= 2:
                    pool.wait_ge(scattered, 16 * TPB * TOP_K * (b - 1))
                pool.dma_start(rows[:, b % 2], home(b)).then_inc(rows_loaded, 16)

            def row_of(table_, t, c):
                at = t * TOP_K + c
                return bass.IndirectOffsetOnAxis(ap=table_[:, at:at + 1], axis=0)

            load_rows(0)
            for b in range(BATCH):
                pool.wait_ge(rows_loaded, 16 * (b + 1))
                if b + 1 < BATCH:
                    load_rows(b + 1)
                for i in range(TPB):
                    for c in range(TOP_K):
                        pool.indirect_dma_start(slot_in, row_of(target_row, TPB * b + i, c), rows[:, b % 2, i, :], None)\
                            .then_inc(scattered, 16)
            with pool.Fori(2, TURNS) as n:
                load_weights(n)

            pool.wait_ge(scattered, 16 * TILES * TOP_K)
            pool.wait_ge(ys_stored, 16 * ROUTED_SLOTS)
            for t in range(TILES):
                if t >= 2:
                    pool.wait_ge(combined, TOP_K * (t - 1))
                for c in range(TOP_K):
                    pool.indirect_dma_start(rows[:, t % 2, c, :], None, slot_out, row_of(result_row, t, c))\
                        .then_inc(gathered[t % 2], 16)

        @block.scalar
        def _(act):
            def keep_logits(b):
                act.wait_ge(logits_made, b + 1)
                if b >= 2:
                    act.wait_ge(logits_turned, b - 1)
                act.activation(logits_t[b % 2], psum[0:EXPERTS, LOGIT_T_BANKS[b % 2], :], ACT.Identity,
                               bias=g_bias[:]).then_inc(logits_kept, 1)

            for b in range(BATCH):
                act.wait_ge(shift_ready, b + 1)
                if b >= 2:
                    act.wait_ge(xn_stored, 16 * (b - 1))
                for i in range(TPB):
                    act.activation(rows[:, b % 2, i, :], x_res[:, TPB * b + i, :], ACT.Identity,
                                   bias=shift[:, b % 2, i:i + 1], scale=rstd[:, b % 2, i:i + 1]).then_inc(xn_ready, 1)
                if b:
                    keep_logits(b - 1)
                else:
                    act.wait_ge(small_loaded, 64)
                    act.activation(g_hi[:], g_raw[:], ACT.Copy).then_inc(g_hi_ready, 1)
                    act.activation(above_r[:], table[:, K_BEFORE:K_BEFORE + P], ACT.Copy).then_inc(sums_ready, 1)
                    act.wait_ge(const_ready, 3)
                    act.activation(ones_r[:], ones[:], ACT.Copy).then_inc(sums_ready, 1)
                for i in range(TPB):
                    act.wait_ge(xn_turned, TPB * b + i + 1)
                    if b:
                        act.wait_ge(logits_made, b)
                    act.activation(gt_hi[:, :, P * i:P * i + P], chunks(i), ACT.Copy).then_inc(gt_hi_ready, 1)
                if b < 3:
                    act.wait_ge(w_loaded[b], 16)
                    act.activation(w_hi[:, 0, b], raw[:, b], ACT.Copy).then_inc(w_hi_ready, 1)
            keep_logits(BATCH - 1)
            act.wait_ge(centred_ready, 1)
            act.activation(proba[:], logits[:], ACT.Exp).then_inc(exp_ready, 1)

            def keep_x(s):
                act.wait_ge(x_turned, s + 1)
                act.activation(xt_hi[:], chunks(X_BANK), ACT.Copy).then_inc(xt_hi_ready, 1)

            def split(n, matrices):
                for m in matrices:
                    act.wait_ge(w_loaded[m], n * 16 + 16)
                    act.activation(matrix(w_hi, n, m), raw[:, m], ACT.Copy).then_inc(w_hi_ready, 1)

            def step(s, now, before, kind):
                if now is not None:
                    act.wait_ge(up_made, s * 2 + 1)
                    act.activation(gated[:], psum[:, UP_BANK, :], ACT.Silu).then_inc(gated_ready, 1)
                    if has_next(s):
                        keep_x(s + 1)
                if kind == "routed":
                    act.wait_ge(out_made, s)
                    if not (isinstance(s, int) and s == HALF + 1):
                        act.wait_ge(ys_stored, s * 16 - 16 * (HALF + 1))
                    act.activation(ys[:], psum[:, OUT_BANK, :], ACT.Copy).then_inc(ys_ready, 1)
                if now is not None:
                    act.wait_ge(h_turned, s + 1)
                    act.activation(ht_hi[:], chunks(H_BANK), ACT.Copy).then_inc(ht_hi_ready, 1)
                    split_ahead(act, s, now, before, split)

            keep_x(0)
            steps(act, step)

        @block.vector
        def _(dve):
            own = Tally(gate_step)

            def done(ins):
                own.inc(ins)
                own.wait(dve)

            def over_experts(column):
                return column.unsqueeze(2).broadcast_to([P, TILES, ROUTED])

            def on_every_tile(line):
                return line.unsqueeze(1).broadcast_to([P, TILES, ROUTED])

            def statistics(b):
                for i in range(TPB):
                    dve.bn_stats(stats[:, i, :], x_res[:, TPB * b + i, :]).then_inc(stat_ready, 1)
                for i in range(TPB):
                    dve.wait_ge(stat_ready, TPB * b + i + 1)
                    dve.bn_aggr(mv[:, i, :], stats[:, i, :]).then_inc(var_ready, 1)

            statistics(0)
            for b in range(BATCH):
                dve.wait_ge(rstd_ready, b + 1)
                if b >= 2:
                    dve.wait_ge(xn_ready, TPB * (b - 1))
                dve.scalar_tensor_tensor(out=shift[:, b % 2, :], in0=mv[:, :, 0], scalar=-1.0, in1=rstd[:, b % 2, :],
                                         op0=ALU.mult, op1=ALU.mult).then_inc(shift_ready, 1)
                if b + 1 < BATCH:
                    dve.wait_ge(shift_ready, b + 1)
                    statistics(b + 1)
                if b == 0:
                    dve.wait_ge(g_hi_ready, 1)
                    dve.tensor_tensor(g_lo[:], g_raw[:], g_hi[:].bitcast(F32), ALU.subtract).then_inc(g_lo_ready, 1)
                for i in range(TPB):
                    dve.wait_ge(gt_hi_ready, TPB * b + i + 1)
                    cols = slice(P * i, P * i + P)
                    dve.tensor_tensor(gt_lo[:, :, cols], chunks(i), gt_hi[:, :, cols].bitcast(F32), ALU.subtract)\
                       .then_inc(gt_lo_ready, 1)

            dve.wait_ge(logits_turned, BATCH)
            made = psum[:, LOGIT_BANK, 0:TILES * EXPERTS].rearrange("p (t e) -> p t e", e=EXPERTS)[:, :, 0:ROUTED]
            done(dve.tensor_reduce(top[:], made, AX.X, ALU.max))
            dve.tensor_tensor(logits[:], made, over_experts(top[:]), ALU.subtract).then_inc(centred_ready, 1)
            dve.wait_ge(exp_ready, 1)
            done(dve.tensor_reduce(total[:, 0, :], proba[:], AX.X, ALU.add))
            done(dve.reciprocal(total[:, 1, :], total[:, 0, :]))
            done(dve.tensor_tensor(proba[:], proba[:], over_experts(total[:, 1, :]), ALU.mult))
            done(dve.tensor_tensor(biased[:], proba[:], on_every_tile(s_bias[:]), ALU.add))
            for j in range(ROUTED):
                for lo, hi, op in ((0, j, ALU.is_gt), (j, ROUTED, ALU.is_ge)):
                    if hi > lo:
                        other = biased[:, :, j:j + 1].broadcast_to([P, TILES, hi - lo])
                        own.inc(dve.tensor_tensor(beats[:, :, lo:hi, j], other, biased[:, :, lo:hi], op))
            own.wait(dve)
            done(dve.tensor_reduce(rank[:], beats[:], AX.X, ALU.add))
            dve.wait_ge(const_ready, 3)
            dve.tensor_copy(chosen[:, :, ROUTED], zero[:]).then_inc(chosen_ready, 1)
            dve.tensor_scalar(chosen[:, :, 0:ROUTED], rank[:], TOP_K + 0.5, None, ALU.is_lt).then_inc(chosen_ready, 1)
            dve.wait_ge(chosen_ready, 2)
            picks = chosen[:, :, 0:ROUTED].bitcast(F32)
            dve.tensor_reduce(per_expert[:], picks.rearrange("p t e -> p e t"), AX.X, ALU.add)\
               .then_inc(chosen_ready, 1)
            done(dve.tensor_tensor(proba[:], proba[:], picks, ALU.mult))
            done(dve.tensor_reduce(total[:, 0, :], proba[:], AX.X, ALU.add))
            done(dve.reciprocal(total[:, 1, :], total[:, 0, :]))
            done(dve.tensor_tensor(proba[:], proba[:], over_experts(total[:, 1, :]), ALU.mult))
            own.inc(dve.memset(nth[:, :, 0:1], 0.0))
            for e in range(1, ROUTED):
                own.wait(dve)
                own.inc(dve.tensor_tensor(nth[:, :, e:e + 1], nth[:, :, e - 1:e], picks[:, :, e - 1:e], ALU.add))


            dve.wait_ge(counted, 1)
            full = table[:, K_FILLS:K_FILLS + TILES].unsqueeze(1).broadcast_to([P, ROUTED, TILES])
            count = psum[:, COUNT_BANK, 0:ROUTED].unsqueeze(2).broadcast_to([P, ROUTED, TILES])
            done(dve.tensor_tensor(fills[:], count, full, ALU.is_gt))
            done(dve.tensor_reduce(slots_of[:], fills[:], AX.X, ALU.add))
            done(dve.tensor_scalar(slots_of[:], slots_of[:], 1.0, None, ALU.max))
            earlier = table[:, K_EARLIER:K_EARLIER + RANKS].rearrange("p (e f) -> p e f", f=ROUTED)
            done(dve.tensor_tensor(before_of[:], slots_of[:].unsqueeze(1).broadcast_to([P, ROUTED, ROUTED]), earlier,
                                   ALU.mult))
            done(dve.tensor_reduce(start[:, 0:ROUTED], before_of[:], AX.X, ALU.add))
            done(dve.tensor_scalar(start[:, 0:ROUTED], start[:, 0:ROUTED], float(HALF), None, ALU.add))
            done(dve.memset(start[:, ROUTED:EXPERTS], float(LAST_HALF)))
            ahead = psum[:, PLACE_BANK, 0:TILES * EXPERTS].rearrange("p (t e) -> p t e", e=EXPERTS)[:, :, 0:ROUTED]
            dve.wait_ge(place_made, 1)
            done(dve.scalar_tensor_tensor(out=place[:], in0=on_every_tile(start[:, 0:ROUTED]), scalar=float(P),
                                          in1=ahead, op0=ALU.mult, op1=ALU.add))
            for c in range(TOP_K):
                done(dve.scalar_tensor_tensor(out=pick[:], in0=nth[:], scalar=float(c), in1=picks,
                                              op0=ALU.is_equal, op1=ALU.mult))
                for source, dest in ((place, target), (proba, share)):
                    done(dve.tensor_tensor(picked[:], pick[:], source[:], ALU.mult))
                    done(dve.tensor_reduce(dest[:, :, c], picked[:], AX.X, ALU.add))
            dve.tensor_copy(target_row[:], target[:].rearrange("p t c -> p (t c)")).then_inc(targets_ready, 1)
            done(dve.tensor_scalar(target[:], target[:], float(-HALF * P), None, ALU.add))
            dve.tensor_copy(result_row[:], target[:].rearrange("p t c -> p (t c)")).then_inc(targets_ready, 1)
            slot = table[0:1, K_SLOT:K_SLOT + SLOTS].unsqueeze(2).broadcast_to([1, SLOTS, EXPERTS])
            done(dve.tensor_tensor(started[:], slot, start[0:1, :].unsqueeze(1).broadcast_to([1, SLOTS, EXPERTS]),
                                   ALU.is_ge))
            done(dve.tensor_reduce(turn[:], started[:], AX.X, ALU.add))
            done(dve.tensor_tensor(fresh[:, 0, 1:SLOTS], turn[:, 1:SLOTS], turn[:, 0:SLOTS - 1], ALU.subtract))
            done(dve.memset(fresh[:, 0, 0:1], 0.0))
            done(dve.scalar_tensor_tensor(out=fresh[:, 1, :], in0=turn[:], scalar=1.0, in1=fresh[:, 0, :],
                                          op0=ALU.add, op1=ALU.mult))
            dve.tensor_copy(turn_of[:], turn[:]).then_inc(turns_ready, 1)
            dve.tensor_copy(next_of[:], fresh[:, 1, :]).then_inc(turns_ready, 1)

            dve.wait_ge(first_lo_ready, 3)
            dve.nop(nofuse=True).then_inc(w_lo_ready, 3)

            def keep_x_low(s):
                dve.wait_ge(xt_hi_ready, s + 1)
                dve.tensor_tensor(xt_lo[:], chunks(X_BANK), xt_hi[:].bitcast(F32), ALU.subtract)\
                   .then_inc(xt_lo_ready, 1)

            def split(n, matrices):
                for m in matrices:
                    dve.wait_ge(w_hi_ready, n * 3 + (m + 1))
                    dve.tensor_tensor(matrix(w_lo, n, m), raw[:, m], matrix(w_hi, n, m).bitcast(F32), ALU.subtract)\
                       .then_inc(w_lo_ready, 1)

            def combine(s):
                i = s - (LAST_HALF + 1)
                dve.tensor_copy(share_now[:], share[:, bass.ds(i * 2, 2), :].rearrange("p t c -> p (t c)"))\
                   .then_inc(share_ready, 1)
                dve.wait_ge(share_ready, i + 1)
                for j in range(2):
                    dve.wait_ge(gathered[j], (i + 1) * (16 * TOP_K))
                    tile = x_res[:, bass.ds(i * 2 + j, 1), :].rearrange("p a n -> p (a n)")
                    for c in range(TOP_K):
                        dve.scalar_tensor_tensor(out=tile, in0=rows[:, j, c, :],
                                                 scalar=share_now[:, TOP_K * j + c:TOP_K * j + c + 1], in1=tile,
                                                 op0=ALU.mult, op1=ALU.add).then_inc(combined, 1)
                        dve.wait_ge(combined, i * (2 * TOP_K) + (TOP_K * j + c + 1))

            def step(s, now, before, kind):
                if now is not None:
                    dve.wait_ge(gated_ready, s + 1)
                    dve.wait_ge(up_made, s * 2 + 2)
                    dve.tensor_tensor(product[:], gated[:], psum[:, GATE_BANK, :], ALU.mult).then_inc(product_ready, 1)
                    if has_next(s):
                        keep_x_low(s + 1)
                if kind in ("first half", "second half"):
                    dve.wait_ge(out_made, s)
                    t = s - 1 if kind == "first half" else s - (LAST_HALF + 1 - HALF)
                    dve.tensor_tensor(row(x_res, t), psum[:, OUT_BANK, :], row(x_res, t), ALU.add).then_inc(added, 1)
                if now is not None:
                    dve.wait_ge(ht_hi_ready, s + 1)
                    dve.tensor_tensor(ht_lo[:], chunks(H_BANK), ht_hi[:].bitcast(F32), ALU.subtract)\
                       .then_inc(ht_lo_ready, 1)
                    split_ahead(dve, s, now, before, split)
                if kind == "second half":
                    dve.wait_ge(added, s - (LAST_HALF - HALF))
                    combine(s)

            keep_x_low(0)
            steps(dve, step)

        @block.tensor
        def _(pe):
            def three(out, lhs, rhs, first, last):
                for i, (a, c) in enumerate(((lhs[0], rhs[0]), (lhs[0], rhs[1]), (lhs[1], rhs[0]))):
                    ins = pe.matmul(out, a, c, start=first and i == 0, stop=last and i == 2)
                return ins

            def turn_logits(b):
                pe.wait_ge(logits_kept, b + 1)
                for i in range(TPB):
                    at = EXPERTS * (TPB * b + i)
                    ins = pe.transpose(psum[:, LOGIT_BANK, at:at + EXPERTS], logits_t[b % 2][:, P * i:P * i + P],
                                       ident[0:EXPERTS, 0:EXPERTS])
                ins.then_inc(logits_turned, 1)

            for b in range(BATCH):
                for i in range(TPB):
                    pe.wait_ge(xn_ready, TPB * b + i + 1)
                    if b:
                        pe.wait_ge(gt_lo_ready, TPB * (b - 1) + i + 1)
                    for k in range(KD):
                        ins = pe.transpose(psum[:, i, P * k:P * k + P], rows[:, b % 2, i, P * k:P * k + P], ident[:])
                    ins.then_inc(xn_turned, 1)
                if b:
                    turn_logits(b - 1)
                else:
                    pe.wait_ge(g_lo_ready, 1)
                pe.wait_ge(gt_lo_ready, TPB * (b + 1))
                for k in range(KD):
                    ins = three(psum[0:EXPERTS, LOGIT_T_BANKS[b % 2], :], (g_hi[:, k], g_lo[:, k]),
                                (gt_hi[:, k], gt_lo[:, k]), k == 0, k == KD - 1)
                ins.then_inc(logits_made, 1)
            turn_logits(BATCH - 1)

            pe.wait_ge(sums_ready, 2)
            pe.wait_ge(chosen_ready, 2)
            flags = chosen[:].rearrange("p t e -> p (t e)")
            n = TILES * EXPERTS
            pe.matmul(psum[:, PLACE_BANK, 0:n], above_r[:], flags, start=True, stop=False, skip_group_check=True)
            for t in range(1, TILES):
                ins = pe.matmul(psum[:, PLACE_BANK, EXPERTS * t:n], ones_r[:], flags[:, 0:n - EXPERTS * t],
                                start=False, stop=t == TILES - 1, skip_group_check=True)
            ins.then_inc(place_made, 1)
            pe.wait_ge(chosen_ready, 3)
            pe.matmul(psum[:, COUNT_BANK, 0:ROUTED], ones[:], per_expert[:], start=True, stop=True)\
              .then_inc(counted, 1)

            def turn_x(s):
                pe.wait_ge(xs_loaded, s * 16 + 16)
                for k in range(KD):
                    ins = pe.transpose(psum[:, X_BANK, P * k:P * k + P], xs[:, P * k:P * k + P], ident[:])
                ins.then_inc(x_turned, 1)

            def step(s, now, before, kind):
                if now is not None:
                    n = turn_at(pe, s, now)
                    pe.wait_ge(xt_lo_ready, s + 1)
                    pe.wait_ge(w_lo_ready, n * 3 + 2)
                    for m, bank in ((0, UP_BANK), (1, GATE_BANK)):
                        for k in range(KD):
                            ins = three(psum[:, bank, :], (xt_hi[:, k], xt_lo[:, k]),
                                        (block_of(w_hi, n, m, k), block_of(w_lo, n, m, k)), k == 0, k == KD - 1)
                        ins.then_inc(up_made, 1)
                    if has_next(s):
                        turn_x(s + 1)
                if before is not None:
                    n = turn_at(pe, s - 1, before)
                    pe.wait_ge(ht_lo_ready, s)
                    pe.wait_ge(w_lo_ready, n * 3 + 3)
                    for k in range(KD):
                        ins = three(psum[:, OUT_BANK, :], (ht_hi[:, k], ht_lo[:, k]),
                                    (block_of(w_hi, n, 2, k), block_of(w_lo, n, 2, k)), k == 0, k == KD - 1)
                    ins.then_inc(out_made, 1)
                if now is not None:
                    pe.wait_ge(product_ready, s + 1)
                    for k in range(KD):
                        ins = pe.transpose(psum[:, H_BANK, P * k:P * k + P], product[:, P * k:P * k + P], ident[:])
                    ins.then_inc(h_turned, 1)

            pe.wait_ge(gt_lo_ready, TILES)
            turn_x(0)
            pe.wait_ge(turns_ready, 2)
            steps(pe, step)



def program(nc, x, a_wq, a_wk, a_wv, a_wo, a_mask, b_weights, c_wqa, c_wkr, c_gain, c_cos, c_sin, c_heads,
            c_causal, c_rotation, d_weights, d_gate_w, d_gate_b, d_select_b, d_constants, identity, out):
    with ExitStack() as ctx:
        x_res = ctx.enter_context(nc.sbuf_tensor("x_res", [P, TILES, D], F32))
        ident = ctx.enter_context(nc.sbuf_tensor("ident", [P, P], F32))
        zeroed = ctx.enter_context(nc.semaphore("zeroed"))
        slots_cleared = ctx.enter_context(nc.semaphore("slots_cleared"))
        slot_in = nc.dram_tensor("slot_in", [SLOTS * P, D], F32).ap()
        slot_out = nc.dram_tensor("slot_out", [ROUTED_SLOTS * P, D], F32).ap()
        early = ctx.enter_context(ExitStack())
        piece_sum = early.enter_context(nc.sbuf_tensor("piece_sum", [P, 2 * PIECES], F32))
        zeros = early.enter_context(nc.sbuf_tensor("zeros", [P, D // 2], F32))
        with nc.Block() as block:

            @block.gpsimd
            def _(pool):
                pool.memset(zeros[:], 0.0).then_inc(zeroed, 1)

            @block.sync
            def _(sp):
                sp.wait_ge(zeroed, 1)

        each = ROUTED_SLOTS // BATCH

        def clear_slots(sp, b):
            n = each if not isinstance(b, int) else ROUTED_SLOTS - BATCH * each
            rows = slot_in[bass.ds(b * (each * P) + HALF * P, n * P), :].rearrange("(p r) (a m) -> p (r a) m", p=P, a=2)
            sp.dma_start(rows, zeros[:].unsqueeze(1).broadcast_to([P, 2 * n, D // 2])).then_inc(slots_cleared, 16)

        window_attention(nc, x_res, ident, x, identity, a_wq, a_wk, a_wv, a_wo, a_mask, b_weights, piece_sum,
                         clear_slots)
        ternary_mlp(nc, x_res, ident, b_weights, piece_sum)
        with nc.Block() as block:

            @block.sync
            def _(sp):
                sp.wait_ge(slots_cleared, 16 * (BATCH + 1))

        early.close()
        with ExitStack() as latents:
            lat_hi = latents.enter_context(nc.sbuf_tensor("lat_hi", [P, SLABS, TOKENS], F32R))
            lat_lo = latents.enter_context(nc.sbuf_tensor("lat_lo", [P, SLABS, TOKENS], F32R))
            v_hi = latents.enter_context(nc.sbuf_tensor("v_hi", [P, TILES, P], F32R))
            v_lo = latents.enter_context(nc.sbuf_tensor("v_lo", [P, TILES, P], F32R))
            first_raw = latents.enter_context(nc.sbuf_tensor("head_raw", [P, H_COLS], F32))
            latent_projections(nc, x_res, ident, lat_hi, lat_lo, v_hi, v_lo, c_wqa, c_wkr, c_gain, c_cos, c_sin,
                               first_raw, c_heads[0])
            latent_attention(nc, x_res, ident, lat_hi, lat_lo, v_hi, v_lo, first_raw, c_heads, c_causal, c_rotation)
        mixture_of_experts(nc, x_res, ident, d_weights, d_gate_w, d_gate_b, d_select_b, d_constants, slot_in, slot_out,
                           out)



def window_mask():
    i, j = np.arange(SEQ)[:, None], np.arange(SEQ)[None, :]
    seen = ((j <= i) & (j >= i - 255)) | (j < 4)
    seen &= (i >= 4) | (j <= i)
    m = np.where(seen, 0.0, MASKED).astype(np.float32)
    return np.concatenate([m[P * t:P * t + P, :P * (t + 1)] for t in range(TPB)], axis=1)


def rotary():
    freq = (np.float32(1.0) / np.float32(10000.0) ** (np.arange(0, ROPE, 2, dtype=np.float32) / np.float32(ROPE)))
    angle = np.outer(np.arange(SEQ, dtype=np.float32), freq.astype(np.float32)).astype(np.float32)
    c, s = np.cos(angle), np.sin(angle)
    return np.concatenate([c, c], axis=1), np.concatenate([-s, s], axis=1)


def ternary_pieces(w_fc, w_proj):
    fc = w_fc.T.reshape(PIECES, P, FF)
    proj = w_proj.T.reshape(PIECES, KF // PIECES, P, D).transpose(0, 2, 1, 3).reshape(PIECES, P, FF)
    return np.concatenate([fc, proj])


def slot_constants():
    c = np.zeros((P, K_COLS), np.float32)
    c[:, K_BEFORE:K_BEFORE + P] = np.arange(P)[:, None] < np.arange(P)[None, :]
    e = np.arange(ROUTED)
    c[:, K_EARLIER:K_EARLIER + RANKS] = (e[None, :] < e[:, None]).reshape(-1)
    c[:, K_FILLS:K_FILLS + TILES] = P * np.arange(TILES)
    c[:, K_SLOT:K_SLOT + SLOTS] = np.arange(SLOTS)
    return c


def head_weights(wq_b, wkv_b, wo):
    wq = wq_b.reshape(Q_LORA, L_HEADS, NOPE + ROPE)
    wkv = wkv_b.reshape(KV_LORA, L_HEADS, NOPE + D_V)
    half = NOPE + ROPE // 2
    wr = np.concatenate([wq[:, :, NOPE:], wq[:, :, half:], wq[:, :, NOPE:half]], axis=2)
    wr = wr.reshape(KQ, P, L_HEADS, P).transpose(2, 1, 0, 3).reshape(L_HEADS, P, KQ * P)
    return np.concatenate([wq[:, :, :NOPE].transpose(1, 2, 0), wkv[:, :, :NOPE].transpose(1, 2, 0), wr,
                           wkv[:, :, NOPE:].transpose(1, 2, 0), wo.reshape(L_HEADS, D_V, D)], axis=2)


def kernel(**inputs):
    import numpy as _np
    import concourse.bacc as _bacc
    from concourse.bass_utils import run_bass_kernel_spmd as _run

    a = {name: _np.asarray(value) for name, value in inputs.items()}
    cos, sin = rotary()
    wq = a["L0_attn_Wq"].T.reshape(D, GROUPS, PER_GROUP, HS).transpose(0, 2, 1, 3).reshape(D, D)
    tri = _np.where(_np.arange(P)[None, :] <= _np.arange(P)[:, None], 0.0, MASKED)
    experts = _np.stack([_np.concatenate([a["L1_ffn_" + s][None], a["L1_ffn_" + r], a["L1_ffn_" + s][None]])
                         for r, s in (("W1", "Ws1"), ("Wg", "Wsg"), ("W2", "Ws2"))], axis=1)
    arrays = {
        "x": a["L0_attn_x"],
        "a_wq": wq, "a_wk": a["L0_attn_Wk"].T, "a_wv": a["L0_attn_Wv"].T, "a_wo": a["L0_attn_Wo"].T,
        "a_mask": window_mask(),
        "b_weights": ternary_pieces(a["L0_ffn_w_fc"], a["L0_ffn_w_proj"]),
        "c_wqa": a["L1_attn_Wq_a"],
        "c_wkr": _np.concatenate([a["L1_attn_Wkv_a"], a["L1_attn_Wk_rope"]], axis=1),
        "c_gain": _np.broadcast_to(_np.concatenate([a["L1_attn_q_norm_w"], a["L1_attn_kv_norm_w"]]),
                                   (P, Q_LORA + KV_LORA)),
        "c_cos": cos.reshape(TPB, P, ROPE).transpose(1, 0, 2), "c_sin": sin.reshape(TPB, P, ROPE).transpose(1, 0, 2),
        "c_heads": head_weights(a["L1_attn_Wq_b"], a["L1_attn_Wkv_b"], a["L1_attn_Wo"]),
        "c_causal": _np.concatenate([_np.zeros((P, SEQ - P)), tri], axis=1).astype(_np.float32),
        "c_rotation": _np.concatenate([cos.T, sin.T], axis=0),
        "d_weights": experts,
        "d_gate_w": _np.concatenate([a["L1_ffn_gate_w"], _np.zeros((D, 1), _np.float32)], axis=1),
        "d_gate_b": _np.concatenate([a["L1_ffn_gate_b"], _np.zeros(1, _np.float32)])[:, None],
        "d_select_b": _np.broadcast_to(a["L1_ffn_biases"], (P, ROUTED)),
        "d_constants": slot_constants(),
        "identity": _np.eye(P, dtype=_np.float32),
    }
    arrays = {name + "_dram": _np.ascontiguousarray(value) for name, value in arrays.items()}
    nc = _bacc.Bacc("TRN2", target_bir_lowering=False, num_devices=1)
    args = [nc.dram_tensor(name, value.shape, mybir.dt.from_np(value.dtype), kind="ExternalInput").ap()
            for name, value in arrays.items()]
    args.append(nc.dram_tensor("out_dram", [BATCH, SEQ, D], F32, kind="ExternalOutput").ap())
    program(nc, *args)
    return _run(nc, [arrays], core_ids=[0]).results[0]["out_dram"]
```
